# Optimizing a Trainium2 kernel written in Bass

```python
import numpy as np
import jax
import jax.numpy as jnp

def _softmax(x, axis=-1):
    return jax.nn.softmax(x, axis=axis)

def _gelu(x):
    return jax.nn.gelu(x, approximate=True)

def _silu(x):
    return jax.nn.silu(x)

def _sigmoid(x):
    return jax.nn.sigmoid(x)

def _layernorm(x, axis=-1, eps=1e-05):
    m = jnp.mean(x, axis=axis, keepdims=True)
    v = jnp.var(x, axis=axis, keepdims=True)
    return (x - m) / jnp.sqrt(v + eps)

def _scatter_add(tgt, idx, src, axis=0):
    return tgt.at[idx].add(src)

def _segment_sum(src, seg, n):
    return jax.ops.segment_sum(src, seg, n)
kernel_name = 'mk_seq_preln_d2_jaxref_r4_8fb818'

def setup_inputs(seed: int=0):
    np.random.seed(seed)
    _w = jnp.asarray

    def _L0_attn_setup():
        import jax, jax.numpy as jnp
        import numpy as np
        B, L, D = (4, 512, 256)
        H, DK, DV = (4, 64, 64)
        CHUNK = 32
        MIN_FLOOR, MAX_FLOOR = (0.01, 0.1)
        EPS = 1e-05

        def _l2norm(x):
            return x * jax.lax.rsqrt(jnp.sum(x * x, -1, keepdims=True) + 1e-06)

        def _causal_dwconv(x, w):
            b, l, c = x.shape
            k = w.shape[-1]
            xt = jnp.transpose(x, (0, 2, 1))
            y = jax.lax.conv_general_dilated(xt, w[:, None, :], (1,), [(k - 1, 0)], dimension_numbers=('NCH', 'OIH', 'NCH'), feature_group_count=c)
            return jnp.transpose(y, (0, 2, 1))

        def _delta_rule_chunkwise(q, k, v, beta, chunk=CHUNK):
            b, h, l, dk = q.shape
            dv = v.shape[-1]
            q = _l2norm(q)
            k = _l2norm(k)
            v = v * beta[..., None]
            kb = k * beta[..., None]
            n = l // chunk
            resh = lambda t: t.reshape(b, h, n, chunk, t.shape[-1])
            q, k, v, kb = (resh(q), resh(k), resh(v), resh(kb))
            tri = jnp.triu(jnp.ones((chunk, chunk), bool))
            strict = jnp.triu(jnp.ones((chunk, chunk), bool), 1)
            att = jnp.where(tri, 0.0, -(kb @ jnp.swapaxes(k, -1, -2)))
            for i in range(1, chunk):
                upd = jnp.einsum('bhnj,bhnjk->bhnk', att[..., i, :], att)
                att = att.at[..., i, :i].add(upd[..., :i])
            att = att + jnp.eye(chunk, dtype=att.dtype)
            u = att @ v
            w = att @ kb

            def step(S, xs):
                q_i, k_i, u_i, w_i = xs
                local = jnp.where(strict, 0.0, q_i @ jnp.swapaxes(k_i, -1, -2))
                u_adj = u_i - w_i @ S
                o_i = q_i @ S + local @ u_adj
                return (S + jnp.swapaxes(k_i, -1, -2) @ u_adj, o_i)
            xs = tuple((jnp.moveaxis(t, 2, 0) for t in (q, k, u, w)))
            S0 = jnp.zeros((b, h, dk, dv), q.dtype)
            S, o = jax.lax.scan(step, S0, xs)
            return (jnp.moveaxis(o, 0, 2).reshape(b, h, l, dv), S)

        def _rmsnorm(x, w):
            return x * jax.lax.rsqrt(jnp.mean(x * x, -1, keepdims=True) + EPS) * w
        key = jax.random.key(seed)
        ks = jax.random.split(key, 16)
        s = 0.02
        return {'hidden_states': jax.random.normal(ks[0], (B, L, D), jnp.float32), 'W_q': jax.random.normal(ks[1], (D, H * DK), jnp.float32) * s, 'W_k': jax.random.normal(ks[2], (D, H * DK), jnp.float32) * s, 'W_v': jax.random.normal(ks[3], (D, H * DV), jnp.float32) * s, 'W_b': jax.random.normal(ks[4], (D, H), jnp.float32) * s, 'conv_w_q': jax.random.normal(ks[5], (H * DK, 4), jnp.float32) * 0.3, 'conv_w_k': jax.random.normal(ks[6], (H * DK, 4), jnp.float32) * 0.3, 'conv_w_v': jax.random.normal(ks[7], (H * DV, 4), jnp.float32) * 0.3, 'fir_short_w': jax.random.normal(ks[8], (H, DV, 3), jnp.float32) * 0.1, 'fir_long_w': jax.random.normal(ks[9], (H, DV, 31), jnp.float32) * 0.1, 'W_fuse1': jax.random.normal(ks[10], (D + 3 * H * DV, 2 * D), jnp.float32) * s, 'b_fuse1': jnp.zeros((2 * D,), jnp.float32), 'W_fuse2': jax.random.normal(ks[11], (2 * D, H * 4), jnp.float32) * s, 'b_fuse2': jnp.zeros((H * 4,), jnp.float32).at[3::4].set(4.0), 'others_log_tau': jnp.zeros((H,), jnp.float32), 'norm_w': jnp.ones((DV,), jnp.float32), 'W_o': jax.random.normal(ks[12], (H * DV, D), jnp.float32) * s}
    _L0_attn_in = _L0_attn_setup()

    def _L0_ffn_setup():
        import jax, jax.numpy as jnp
        import numpy as np
        NUM_EXPERTS = 8
        EXPERT_CAPACITY = 2.0
        DIM = 256
        HIDDEN_DIM = 1024
        key = jax.random.key(seed)
        k_x, k_g, k_w1, k_w2 = jax.random.split(key, 4)
        n, t, d, f, e = (8, 256, DIM, HIDDEN_DIM, NUM_EXPERTS)
        x = jax.random.normal(k_x, (n, t, d), dtype=jnp.float32)
        gate_w = jax.random.normal(k_g, (e, d), dtype=jnp.float32) * 0.02
        w1 = jax.random.normal(k_w1, (e, d, f), dtype=jnp.float32) * 0.02
        w2 = jax.random.normal(k_w2, (e, f, d), dtype=jnp.float32) * 0.02
        return {'x': x, 'gate_w': gate_w, 'w1': w1, 'w2': w2}
    _L0_ffn_in = _L0_ffn_setup()

    def _L1_attn_setup():
        import jax, jax.numpy as jnp
        import numpy as np
        DIM = 256
        HEADS = 16
        DHEAD = DIM // HEADS
        EPS_NORM = 1e-06
        EPS_DEN = 1e-06

        def rmsnorm(x, w):
            xf = x.astype(jnp.float32)
            return (w * xf * jax.lax.rsqrt(jnp.mean(xf * xf, axis=-1, keepdims=True) + EPS_NORM)).astype(x.dtype)
        key = jax.random.key(seed)
        ks = jax.random.split(key, 6)
        b, n = (4, 1024)
        x = jax.random.normal(ks[0], (b, n, DIM), dtype=jnp.float32)
        W_qkv = jax.random.normal(ks[1], (DIM, 3 * DIM), dtype=jnp.float32) * DIM ** (-0.5)
        qn_w = jnp.ones((DIM,), dtype=jnp.float32)
        kn_w = jnp.ones((DIM,), dtype=jnp.float32)
        W_out = jax.random.normal(ks[2], (DIM, DIM), dtype=jnp.float32) * DIM ** (-0.5)
        b_out = jnp.zeros((DIM,), dtype=jnp.float32)
        return {'x': x, 'W_qkv': W_qkv, 'qn_w': qn_w, 'kn_w': kn_w, 'W_out': W_out, 'b_out': b_out}
    _L1_attn_in = _L1_attn_setup()

    def _L1_ffn_setup():
        import jax, jax.numpy as jnp
        import numpy as np
        DIM = 256
        HIDDEN = 768
        SCALE = 1.0 / 127.0

        def _dequant(w_int, dtype):
            return w_int.astype(dtype) * jnp.asarray(SCALE, dtype)
        key = jax.random.key(seed)
        k_x, k_g, k_u, k_d = jax.random.split(key, 4)
        x = jax.random.normal(k_x, (4, 512, DIM), dtype=jnp.float32)
        w_gate = jax.random.randint(k_g, (HIDDEN, DIM), -127, 128, dtype=jnp.int32)
        w_up = jax.random.randint(k_u, (HIDDEN, DIM), -127, 128, dtype=jnp.int32)
        w_down = jax.random.randint(k_d, (DIM, HIDDEN), -127, 128, dtype=jnp.int32)
        return {'x': x, 'w_gate': w_gate, 'w_up': w_up, 'w_down': w_down}
    _L1_ffn_in = _L1_ffn_setup()
    _d = {'L0_attn_hidden_states': _L0_attn_in['hidden_states'], 'L0_attn_W_q': _L0_attn_in['W_q'], 'L0_attn_W_k': _L0_attn_in['W_k'], 'L0_attn_W_v': _L0_attn_in['W_v'], 'L0_attn_W_b': _L0_attn_in['W_b'], 'L0_attn_conv_w_q': _L0_attn_in['conv_w_q'], 'L0_attn_conv_w_k': _L0_attn_in['conv_w_k'], 'L0_attn_conv_w_v': _L0_attn_in['conv_w_v'], 'L0_attn_fir_short_w': _L0_attn_in['fir_short_w'], 'L0_attn_fir_long_w': _L0_attn_in['fir_long_w'], 'L0_attn_W_fuse1': _L0_attn_in['W_fuse1'], 'L0_attn_b_fuse1': _L0_attn_in['b_fuse1'], 'L0_attn_W_fuse2': _L0_attn_in['W_fuse2'], 'L0_attn_b_fuse2': _L0_attn_in['b_fuse2'], 'L0_attn_others_log_tau': _L0_attn_in['others_log_tau'], 'L0_attn_norm_w': _L0_attn_in['norm_w'], 'L0_attn_W_o': _L0_attn_in['W_o'], 'L0_ffn_gate_w': _L0_ffn_in['gate_w'], 'L0_ffn_w1': _L0_ffn_in['w1'], 'L0_ffn_w2': _L0_ffn_in['w2'], 'L1_attn_W_qkv': _L1_attn_in['W_qkv'], 'L1_attn_qn_w': _L1_attn_in['qn_w'], 'L1_attn_kn_w': _L1_attn_in['kn_w'], 'L1_attn_W_out': _L1_attn_in['W_out'], 'L1_attn_b_out': _L1_attn_in['b_out'], 'L1_ffn_w_gate': _L1_ffn_in['w_gate'], 'L1_ffn_w_up': _L1_ffn_in['w_up'], 'L1_ffn_w_down': _L1_ffn_in['w_down']}
    _x0 = _d['L0_attn_hidden_states']
    _d['L0_attn_hidden_states'] = jax.random.normal(jax.random.fold_in(jax.random.key(seed), 1), (8, 512, 256), dtype=_x0.dtype)
    del _x0
    return _d

def reference(L0_attn_hidden_states, L0_attn_W_q, L0_attn_W_k, L0_attn_W_v, L0_attn_W_b, L0_attn_conv_w_q, L0_attn_conv_w_k, L0_attn_conv_w_v, L0_attn_fir_short_w, L0_attn_fir_long_w, L0_attn_W_fuse1, L0_attn_b_fuse1, L0_attn_W_fuse2, L0_attn_b_fuse2, L0_attn_others_log_tau, L0_attn_norm_w, L0_attn_W_o, L0_ffn_gate_w, L0_ffn_w1, L0_ffn_w2, L1_attn_W_qkv, L1_attn_qn_w, L1_attn_kn_w, L1_attn_W_out, L1_attn_b_out, L1_ffn_w_gate, L1_ffn_w_up, L1_ffn_w_down):

    def _L0_attn_ref(hidden_states, W_q, W_k, W_v, W_b, conv_w_q, conv_w_k, conv_w_v, fir_short_w, fir_long_w, W_fuse1, b_fuse1, W_fuse2, b_fuse2, others_log_tau, norm_w, W_o):
        import jax, jax.numpy as jnp
        import numpy as np
        B, L, D = (4, 512, 256)
        H, DK, DV = (4, 64, 64)
        CHUNK = 32
        MIN_FLOOR, MAX_FLOOR = (0.01, 0.1)
        EPS = 1e-05

        def _l2norm(x):
            return x * jax.lax.rsqrt(jnp.sum(x * x, -1, keepdims=True) + 1e-06)

        def _causal_dwconv(x, w):
            b, l, c = x.shape
            k = w.shape[-1]
            xt = jnp.transpose(x, (0, 2, 1))
            y = jax.lax.conv_general_dilated(xt, w[:, None, :], (1,), [(k - 1, 0)], dimension_numbers=('NCH', 'OIH', 'NCH'), feature_group_count=c)
            return jnp.transpose(y, (0, 2, 1))

        def _delta_rule_chunkwise(q, k, v, beta, chunk=CHUNK):
            b, h, l, dk = q.shape
            dv = v.shape[-1]
            q = _l2norm(q)
            k = _l2norm(k)
            v = v * beta[..., None]
            kb = k * beta[..., None]
            n = l // chunk
            resh = lambda t: t.reshape(b, h, n, chunk, t.shape[-1])
            q, k, v, kb = (resh(q), resh(k), resh(v), resh(kb))
            tri = jnp.triu(jnp.ones((chunk, chunk), bool))
            strict = jnp.triu(jnp.ones((chunk, chunk), bool), 1)
            att = jnp.where(tri, 0.0, -(kb @ jnp.swapaxes(k, -1, -2)))
            for i in range(1, chunk):
                upd = jnp.einsum('bhnj,bhnjk->bhnk', att[..., i, :], att)
                att = att.at[..., i, :i].add(upd[..., :i])
            att = att + jnp.eye(chunk, dtype=att.dtype)
            u = att @ v
            w = att @ kb

            def step(S, xs):
                q_i, k_i, u_i, w_i = xs
                local = jnp.where(strict, 0.0, q_i @ jnp.swapaxes(k_i, -1, -2))
                u_adj = u_i - w_i @ S
                o_i = q_i @ S + local @ u_adj
                return (S + jnp.swapaxes(k_i, -1, -2) @ u_adj, o_i)
            xs = tuple((jnp.moveaxis(t, 2, 0) for t in (q, k, u, w)))
            S0 = jnp.zeros((b, h, dk, dv), q.dtype)
            S, o = jax.lax.scan(step, S0, xs)
            return (jnp.moveaxis(o, 0, 2).reshape(b, h, l, dv), S)

        def _rmsnorm(x, w):
            return x * jax.lax.rsqrt(jnp.mean(x * x, -1, keepdims=True) + EPS) * w
        b, l, d = hidden_states.shape
        q = jax.nn.silu(_causal_dwconv(hidden_states @ W_q, conv_w_q))
        k = jax.nn.silu(_causal_dwconv(hidden_states @ W_k, conv_w_k))
        v = jax.nn.silu(_causal_dwconv(hidden_states @ W_v, conv_w_v))
        q = q.reshape(b, l, H, DK)
        k = k.reshape(b, l, H, DK)
        v = v.reshape(b, l, H, DV)
        beta = jax.nn.sigmoid(hidden_states @ W_b)
        delta_out, _ = _delta_rule_chunkwise(jnp.transpose(q, (0, 2, 1, 3)), jnp.transpose(k, (0, 2, 1, 3)), jnp.transpose(v, (0, 2, 1, 3)), jnp.transpose(beta, (0, 2, 1)))
        delta_out = jnp.transpose(delta_out, (0, 2, 1, 3))
        vc = v.reshape(b, l, H * DV)
        fir_s = _causal_dwconv(vc, fir_short_w.reshape(H * DV, -1)).reshape(b, l, H, DV)
        fir_l = _causal_dwconv(vc, fir_long_w.reshape(H * DV, -1)).reshape(b, l, H, DV)
        gate_in = jnp.concatenate([hidden_states, fir_s.reshape(b, l, -1), fir_l.reshape(b, l, -1), delta_out.reshape(b, l, -1)], -1)
        hid = jax.nn.gelu(gate_in @ W_fuse1 + b_fuse1, approximate=False)
        logits = (hid @ W_fuse2 + b_fuse2).reshape(b, l, H, 4)
        p_raw = jax.nn.sigmoid(logits[..., 3])
        floor = MIN_FLOOR + (MAX_FLOOR - MIN_FLOOR) * (1.0 - p_raw)
        p_val = (1.0 - floor) * p_raw
        tau = jnp.exp(others_log_tau)
        others = jax.nn.softmax(logits[..., :3] / tau[None, None, :, None], -1)
        p_ctx = (1.0 - p_val)[..., None] * others
        o = p_ctx[..., 0:1] * fir_s + p_ctx[..., 1:2] * fir_l + p_ctx[..., 2:3] * delta_out + p_val[..., None] * v
        o = _rmsnorm(o, norm_w)
        return o.reshape(b, l, H * DV) @ W_o

    def _L0_ffn_ref(x, gate_w, w1, w2):
        import jax, jax.numpy as jnp
        import numpy as np
        NUM_EXPERTS = 8
        EXPERT_CAPACITY = 2.0
        DIM = 256
        HIDDEN_DIM = 1024
        n, t, d = x.shape
        e = gate_w.shape[0]
        k = int(EXPERT_CAPACITY * t / e)
        scores = jnp.einsum('ntd,ed->nte', x, gate_w)
        probs = jax.nn.softmax(scores, axis=-1)
        g, m = jax.lax.top_k(probs.transpose(0, 2, 1), k)
        batch_idx = jnp.arange(n)[:, None, None]
        xin = x[batch_idx, m]
        h = jnp.einsum('nekd,edf->nekf', xin, w1)
        h = jax.nn.gelu(h, approximate=False)
        h = jnp.einsum('nekf,efd->nekd', h, w2)
        out_tok = g[..., None] * h
        out = jnp.zeros((n, t, d), dtype=x.dtype).at[batch_idx, m].add(out_tok)
        return out

    def _L1_attn_ref(x, W_qkv, qn_w, kn_w, W_out, b_out):
        import jax, jax.numpy as jnp
        import numpy as np
        DIM = 256
        HEADS = 16
        DHEAD = DIM // HEADS
        EPS_NORM = 1e-06
        EPS_DEN = 1e-06

        def rmsnorm(x, w):
            xf = x.astype(jnp.float32)
            return (w * xf * jax.lax.rsqrt(jnp.mean(xf * xf, axis=-1, keepdims=True) + EPS_NORM)).astype(x.dtype)
        b, n, _ = x.shape
        qkv = x @ W_qkv
        q, k, v = jnp.split(qkv, 3, axis=-1)
        q = rmsnorm(q, qn_w)
        k = rmsnorm(k, kn_w)

        def split_heads(t):
            return t.reshape(b, n, HEADS, DHEAD).transpose(0, 2, 1, 3)
        q, k, v = map(split_heads, (q, k, v))
        q = jax.nn.relu(q).astype(jnp.float32)
        k = jax.nn.relu(k).astype(jnp.float32)
        v = v.astype(jnp.float32)
        kv = jnp.einsum('bhnd,bhne->bhde', k, v)
        out = jnp.einsum('bhnd,bhde->bhne', q, kv)
        k_sum = k.sum(axis=2)
        normalizer = jnp.einsum('bhnd,bhd->bhn', q, k_sum) + EPS_DEN
        out = out / normalizer[..., None]
        out = out.transpose(0, 2, 1, 3).reshape(b, n, DIM)
        return out @ W_out + b_out

    def _L1_ffn_ref(x, w_gate, w_up, w_down):
        import jax, jax.numpy as jnp
        import numpy as np
        DIM = 256
        HIDDEN = 768
        SCALE = 1.0 / 127.0

        def _dequant(w_int, dtype):
            return w_int.astype(dtype) * jnp.asarray(SCALE, dtype)
        wg = _dequant(w_gate, x.dtype)
        wu = _dequant(w_up, x.dtype)
        wd = _dequant(w_down, x.dtype)
        gate = jnp.einsum('bsd,hd->bsh', x, wg)
        up = jnp.einsum('bsd,hd->bsh', x, wu)
        h = jax.nn.silu(gate) * up
        return jnp.einsum('bsh,dh->bsd', h, wd)
    x = L0_attn_hidden_states
    x = x + _L0_attn_ref(_layernorm(x, axis=-1), L0_attn_W_q, L0_attn_W_k, L0_attn_W_v, L0_attn_W_b, L0_attn_conv_w_q, L0_attn_conv_w_k, L0_attn_conv_w_v, L0_attn_fir_short_w, L0_attn_fir_long_w, L0_attn_W_fuse1, L0_attn_b_fuse1, L0_attn_W_fuse2, L0_attn_b_fuse2, L0_attn_others_log_tau, L0_attn_norm_w, L0_attn_W_o)
    x = x + _L0_ffn_ref(_layernorm(x, axis=-1), L0_ffn_gate_w, L0_ffn_w1, L0_ffn_w2)
    x = x + _L1_attn_ref(_layernorm(x, axis=-1), L1_attn_W_qkv, L1_attn_qn_w, L1_attn_kn_w, L1_attn_W_out, L1_attn_b_out)
    x = x + _L1_ffn_ref(_layernorm(x, axis=-1), L1_ffn_w_gate, L1_ffn_w_up, L1_ffn_w_down)
    return x

_drawn_inputs = setup_inputs


def setup_inputs(seed=0):
    import zlib

    import numpy as np

    out = dict(_drawn_inputs(seed))
    spreads = {'L0_attn_b_fuse1': (0.0, 0.8),
     'L0_attn_others_log_tau': (0.0, 2.0),
     'L0_attn_norm_w': (1.0, 0.2),
     'L1_attn_qn_w': (1.0, 0.6),
     'L1_attn_kn_w': (1.0, 0.6),
     'L1_attn_b_out': (0.0, 0.1)}
    factors = {'L0_attn_W_q': 8.0,
     'L0_attn_W_k': 8.0,
     'L0_attn_W_b': 8.0,
     'L0_attn_conv_w_q': 8.0,
     'L0_attn_conv_w_k': 8.0,
     'L0_attn_fir_short_w': 8.0,
     'L0_attn_fir_long_w': 8.0,
     'L0_attn_W_fuse1': 8.0,
     'L0_attn_W_fuse2': 8.0}
    for name, (base, spread) in spreads.items():
        noise = np.random.default_rng([zlib.crc32(name.encode()), seed]).standard_normal(out[name].shape)
        drawn = base * np.exp(spread * noise) if base else spread * noise
        out[name] = jnp.asarray(drawn.astype(out[name].dtype))
    for name, factor in factors.items():
        out[name] = (out[name] * factor).astype(out[name].dtype)
    return out
```

```python
import concourse.bass as bass
from concourse import mybir
from contextlib import ExitStack

F32 = mybir.dt.float32
I32 = mybir.dt.int32
U32 = mybir.dt.uint32
ALU = mybir.AluOpType
ACT = mybir.ActivationFunctionType
AX = mybir.AxisListType

P = 128
B, L, D = 8, 512, 256
NT = L // P
DB = D // P
H, DK = 4, 64
E, CAP = 8, 2 * L // 8
F0 = 1024
H1, DH1 = 16, 16
F1 = 768
LEVELS = 7
TAPS_S, TAPS_L = 3, 31

C_EYE = 0
C_LEVEL = C_EYE + P
C_UP1 = C_LEVEL + LEVELS * P
C_CAUSAL = C_UP1 + P
C_HEADS = C_CAUSAL + P
C_TOK = C_HEADS + P + 8
C_TOKID = C_TOK + L
C_ONE = C_TOKID + NT
C_MHALF = C_ONE + P
C_END = C_MHALF + 32


def constant_table():
    import numpy as np
    i = np.arange(P)
    t = np.zeros((P, C_END), np.float32)
    t[:, C_EYE:C_EYE + P] = np.eye(P)
    for n in range(LEVELS):
        s = 1 << n
        low = (i[:, None] // (2 * s) == i[None] // (2 * s)) & (i[:, None] // s % 2 == 1) & (i[None] // s % 2 == 0)
        t[:, C_LEVEL + n * P:C_LEVEL + (n + 1) * P] = -1.0 * low
        if n == 0:
            t[:, C_UP1:C_UP1 + P] = -1.0 * low.T
    t[:, C_CAUSAL:C_CAUSAL + P] = i[:, None] <= i[None]
    t[:, C_HEADS:C_HEADS + P] = i[:, None] // DH1 == i[None] // DH1
    t[:, C_HEADS + P:C_HEADS + P + 8] = i[:, None] // DH1 == np.arange(8)[None]
    t[:, C_TOK:C_TOK + L] = np.arange(L)[None]
    t[:, C_TOKID:C_TOKID + NT] = i[:, None] + P * np.arange(NT)[None]
    t[:, C_ONE:C_ONE + P] = 1.0
    t[:, C_MHALF:C_MHALF + 32] = -0.5
    return t


def spread(ap, axis, n):
    shape = list(ap.shape)
    shape.insert(axis, n)
    return ap.unsqueeze(axis).broadcast_to(shape)


class Maker:

    def __init__(self, nc, ctx, prefix=""):
        self.nc, self.ctx, self.prefix = nc, ctx, prefix

    def sb(self, name, shape, dt=F32):
        return self.ctx.enter_context(self.nc.sbuf_tensor(self.prefix + name, shape, dt))

    def sem(self, name):
        return self.ctx.enter_context(self.nc.semaphore(self.prefix + name))


MERGE = 7


def merge_stats(nc, dve, stats, mean, var, done, i):
    ev, od = stats[:, :, 1], stats[:, :, 4]
    nc.vector.tensor_tensor(mean[:], ev, od, ALU.add).then_inc(done, 1)
    nc.vector.tensor_tensor(var[:, 1, :], ev, od, ALU.subtract).then_inc(done, 1)
    nc.vector.tensor_tensor(var[:, 2, :], stats[:, :, 2], stats[:, :, 5], ALU.add).then_inc(done, 1)
    dve.wait_ge(done, i * MERGE + 3)
    nc.vector.tensor_scalar(mean[:], mean[:], 0.5, None, ALU.mult).then_inc(done, 1)
    nc.vector.tensor_scalar(var[:, 2, :], var[:, 2, :], 1.0 / D, 1e-5, ALU.mult, ALU.add).then_inc(done, 1)
    nc.vector.tensor_tensor(var[:, 1, :], var[:, 1, :], var[:, 1, :], ALU.mult).then_inc(done, 1)
    dve.wait_ge(done, i * MERGE + 6)
    nc.vector.scalar_tensor_tensor(var[:, 0, :], var[:, 1, :], 0.25, var[:, 2, :], ALU.mult, ALU.add).then_inc(done, 1)


def attention0(nc, A, const, resid, ps):
    with ExitStack() as ctx:
        mk = Maker(nc, ctx, "a0_")
        sb, sem = mk.sb, mk.sem
        eye = const[:, C_EYE:C_EYE + P]
        eye4 = spread(eye, 1, H)
        level = [spread(const[:, C_LEVEL + n * P:C_LEVEL + (n + 1) * P], 1, H) for n in range(LEVELS)]
        up1 = spread(const[:, C_UP1:C_UP1 + P], 1, H)
        causal = spread(const[:, C_CAUSAL:C_CAUSAL + P], 1, H)
        one_row = const[0:1, C_ONE:C_ONE + P]
        mhalf = const[:, C_MHALF:C_MHALF + 32]

        w_qkv = sb("w_qkv", [P, DB, 3 * D])
        w_beta = sb("w_beta", [P, DB, H])
        conv_w = sb("conv_w", [P, 6, 4])
        fir_sw = sb("fir_sw", [P, DB, TAPS_S])
        fir_lw = sb("fir_lw", [P, DB, TAPS_L])
        w_f1 = sb("w_f1", [P, 8, 2 * D])
        b_f1 = sb("b_f1", [P, 4])
        w_f2 = sb("w_f2", [P, 4, 16])
        b_f2 = sb("b_f2", [1, 16])
        rtau = sb("rtau", [P, H])
        normw = sb("normw", [P, 1])
        w_o = sb("w_o", [P, DB, D])

        stats = sb("stats", [P, NT, 6])
        mean = sb("mean", [P, NT])
        var = sb("var", [P, 3, NT])
        rstd = sb("rstd", [P, NT])
        xn = sb("xn", [P, NT, D])
        xT = sb("xT", [P, DB, L])
        qkv = sb("qkv", [P, 6, L])
        ez = sb("ez", [P, NT * H])
        beta = sb("beta", [P, NT * H])
        sq = sb("sq", [P, 2, 512])
        ss = sb("ss", [P, NT * 8])
        rs = sb("rs", [P, NT * 8])
        kqn = sb("kqn", [P, NT, 512])
        dv = sb("dv", [P, NT, 2, D])
        vb = sb("vb", [P, NT, D])
        kb = sb("kb", [P, NT, D])
        kbqT = [[sb(f"kbqT{t}{hb}", [P, 3, P]) for hb in range(DB)] for t in range(NT)]
        AT = [sb(f"AT{t}", [P, H, P]) for t in range(NT)]
        loc = [sb(f"loc{t}", [P, H, P]) for t in range(NT)]
        TT = [sb(f"TT{t}", [P, H, P]) for t in range(NT)]
        T = [sb(f"T{g}", [P, H, P]) for g in range(2)]
        X = [sb(f"X{g}", [P, H, P]) for g in range(2)]
        nwT = [sb(f"nwT{t}", [P, DB, P]) for t in range(NT)]
        uadj = sb("uadj", [P, NT, D])
        S = sb("S", [P, DB, DK])
        dT = sb("dT", [P, DB, L])
        firT = sb("firT", [P, 2, DB, L])
        hidT = sb("hidT", [P, 4, L])
        lg = sb("lg", [P, NT * H, 4])
        mx = sb("mx", [P, NT * H])
        ex = sb("ex", [P, NT * H, 4])
        sm = sb("sm", [P, NT * H])
        pv = sb("pv", [P, NT * H])
        wt = sb("wt", [P, NT * H, 4])
        mixa = sb("mixa", [P, 2, 2, D])
        mixb = sb("mixb", [P, 2, 2, D])
        o = sb("o", [P, NT, D])
        oo = sb("oo", [P, D])
        so = sb("so", [P, NT * H])
        ro = sb("ro", [P, NT * H])
        oT = [sb(f"oT{t}", [P, DB, P]) for t in range(NT)]

        loaded, prepared, prep = sem("loaded"), sem("prepared"), sem("prep")
        tau_exp = sem("tau_exp")
        mean_ready, rstd_ready, xn_ready = sem("mean_ready"), sem("rstd_ready"), sem("xn_ready")
        xT_ps, xT_ready = sem("xT_ps"), sem("xT_ready")
        proj_ps, tap3_done, conv_done, silu_done = sem("proj_ps"), sem("tap3_done"), sem("conv_done"), sem("silu_done")
        z_ps, ez_ready, beta_ready = sem("z_ps"), sem("ez_ready"), sem("beta_ready")
        kq_ps, sq_ready, ss_ready, rs_ready, kqn_ready = (sem(n) for n in ("kq_ps", "sq_ready", "ss_ready", "rs_ready", "kqn_ready"))
        v_ps, v_ready, vb_ready, kb_ready = sem("v_ps"), sem("v_ready"), sem("vb_ready"), sem("kb_ready")
        kT_ps, kT_ready, al_ps, AT_ready, loc_ready = (sem(n) for n in ("kT_ps", "kT_ready", "al_ps", "AT_ready", "loc_ready"))
        tt1_ready, t1_ps, t1_ready = sem("tt1_ready"), sem("t1_ps"), sem("t1_ready")
        x_ps, x_ready, y_ready, t_ps, t_ready, tt_ps, tt_ready = (
            sem(n) for n in ("x_ps", "x_ready", "y_ready", "t_ps", "t_ready", "tt_ps", "tt_ready"))
        wT_ps, wT_ready = sem("wT_ps"), sem("wT_ready")
        u_ps, u_ready, o_ps, o_ready, s_ps, s_ready, d_ps, d_ready = (
            sem(n) for n in ("u_ps", "u_ready", "o_ps", "o_ready", "s_ps", "s_ready", "d_ps", "d_ready"))
        fir_step = sem("fir_step")
        hid_ps, hid_ready, lg_ps = sem("hid_ps"), sem("hid_ready"), sem("lg_ps")
        ml_ready, ex_ready, wt_ready = sem("ml_ready"), sem("ex_ready"), sem("wt_ready")
        f_ps, mixa_ready, mixb_ready, mix_ready = sem("f_ps"), sem("mixa_ready"), sem("mixb_ready"), sem("mix_ready")
        so_ready, ro_ready, on_ready = sem("so_ready"), sem("ro_ready"), sem("on_ready")
        oT_ps, oT_ready, y_ps, resid_done = sem("oT_ps"), sem("oT_ready"), sem("y_ps"), sem("resid_done")
        dve_step, pool_step, act_step = sem("dve_step"), sem("pool_step"), sem("act_step")

        def bank(n, lo=0, hi=512):
            return ps[:, n, lo:hi]

        def by_parity(n):
            return ps[:, n:n + 2, 0:2 * DK].rearrange("p a (k c) -> p k a c", k=2)

        def pair(ap):
            return ap.rearrange("p (h c) -> p h c", h=H)

        NLOAD = 17
        block = ctx.enter_context(nc.Block())

        @block.sync
        def _(sp):
            with nc.allow_non_contiguous_dma(reason="small parameters"):
                for j, n in enumerate(("W_q", "W_k", "W_v")):
                    sp.dma_start(w_qkv[:, :, j * D:(j + 1) * D],
                                 A["L0_attn_" + n].rearrange("(c p) n -> p c n", p=P)).then_inc(loaded, 16)
                sp.dma_start(w_beta[:], A["L0_attn_W_b"].rearrange("(c p) n -> p c n", p=P)).then_inc(loaded, 16)
                for j, n in enumerate("qkv"):
                    sp.dma_start(conv_w[:, 2 * j:2 * j + 2, :],
                                 A[f"L0_attn_conv_w_{n}"].rearrange("(c p) k -> p c k", p=P)).then_inc(loaded, 16)
                sp.dma_start(fir_sw[:], A["L0_attn_fir_short_w"].rearrange("h d k -> (h d) k")
                             .rearrange("(c p) k -> p c k", p=P)).then_inc(loaded, 16)
                sp.dma_start(fir_lw[:], A["L0_attn_fir_long_w"].rearrange("h d k -> (h d) k")
                             .rearrange("(c p) k -> p c k", p=P)).then_inc(loaded, 16)
                sp.dma_start(w_f1[:], A["L0_attn_W_fuse1"].rearrange("(c p) n -> p c n", p=P)).then_inc(loaded, 16)
                sp.dma_start(b_f1[:], A["L0_attn_b_fuse1"].rearrange("(c p) -> p c", p=P)).then_inc(loaded, 16)
                sp.dma_start(w_f2[:], A["L0_attn_W_fuse2"].rearrange("(c p) n -> p c n", p=P)).then_inc(loaded, 16)
                sp.dma_start(b_f2[:], A["L0_attn_b_fuse2"].unsqueeze(0)).then_inc(loaded, 16)
                sp.dma_start(rtau[:], A["L0_attn_others_log_tau"].unsqueeze(0).broadcast_to([P, H])).then_inc(loaded, 16)
                for half in range(2):
                    sp.dma_start(normw[64 * half:64 * half + 64, :],
                                 A["L0_attn_norm_w"].unsqueeze(1)).then_inc(loaded, 16)
                sp.dma_start(w_o[:], A["L0_attn_W_o"].rearrange("(c p) n -> p c n", p=P)).then_inc(loaded, 16)

        NFIR = 2 * (TAPS_S + TAPS_L)

        def fir_order(k):
            if k < 4 * TAPS_S:
                return k // 2 % 2, k % 2, k // 4, 4
            k -= 4 * TAPS_S
            return 1, k % 2, TAPS_S + k // 2, 2

        @block.vector
        def _(dve):
            dve.wait_ge(loaded, 16 * NLOAD)
            nc.vector.tensor_scalar(w_o[:].rearrange("p c n -> p (c n)"), w_o[:].rearrange("p c n -> p (c n)"),
                                    normw[:, 0:1], None, ALU.mult).then_inc(prepared, 1)
            dve.wait_ge(tau_exp, 1)
            nc.vector.reciprocal(rtau[:], rtau[:]).then_inc(prep, 1)
            dve.wait_ge(prep, 1)

            with dve.Fori(0, B) as b:
                for t in range(NT):
                    nc.vector.bn_stats(stats[:, t, :], resid[:, bass.ds(b * NT + t, 1), :].rearrange("p a d -> p (a d)")).then_inc(dve_step, 1)
                dve.wait_ge(dve_step, b * 4 + 4)
                merge_stats(nc, dve, stats, mean, var, mean_ready, b)
                dve.wait_ge(mean_ready, b * MERGE + MERGE)
                dve.wait_ge(rstd_ready, b + 1)
                for t in range(NT):
                    nc.vector.tensor_scalar(xn[:, t, :], resid[:, bass.ds(b * NT + t, 1), :].rearrange("p a d -> p (a d)"), mean[:, t:t + 1],
                                            rstd[:, t:t + 1], ALU.subtract, ALU.mult).then_inc(xn_ready, 1)
                for m in range(6):
                    dve.wait_ge(tap3_done, b * 6 + m + 1)
                    for s in range(1, 4):
                        if s > 1:
                            dve.wait_ge(conv_done, b * 18 + 3 * m + s - 1)
                        nc.vector.scalar_tensor_tensor(
                            qkv[:, m, s:], bank(m % 2, 0, L - s), conv_w[:, m, 3 - s:4 - s],
                            qkv[:, m, s:], ALU.mult, ALU.add).then_inc(conv_done, 1)
                dve.wait_ge(ez_ready, b + 1)
                nc.vector.tensor_scalar(beta[:], ez[:], 1.0, None, ALU.add).then_inc(beta_ready, 1)
                dve.wait_ge(beta_ready, 2 * b + 1)
                nc.vector.reciprocal(beta[:], beta[:]).then_inc(beta_ready, 1)
                for t in range(NT):
                    dve.wait_ge(sq_ready, b * 4 + t + 1)
                    nc.vector.reduce_sum(ss[:, 8 * t:8 * t + 8], sq[:, t % 2, :].rearrange("p (h c) -> p h c", c=DK),
                                         axis=AX.X).then_inc(ss_ready, 1)
                dve.wait_ge(ss_ready, b * 5 + 4)
                nc.vector.tensor_scalar(ss[:], ss[:], 1e-6, None, ALU.add).then_inc(ss_ready, 1)
                dve.wait_ge(rs_ready, b + 1)
                for t in range(NT):
                    nc.vector.tensor_tensor(kqn[:, t, :].rearrange("p (h c) -> p h c", c=DK),
                                            bank(t).rearrange("p (h c) -> p h c", c=DK),
                                            spread(rs[:, 8 * t:8 * t + 8], 2, DK), ALU.mult).then_inc(kqn_ready, 1)
                for t in range(NT):
                    dve.wait_ge(AT_ready, b * 4 + t + 1)
                    src = ps[:, 2 * (t % 2):2 * (t % 2) + 2, :].rearrange("p a (k c) -> p k a c", k=2)
                    for k in range(2):
                        ins = nc.vector.tensor_tensor(loc[t][:, 2 * k:2 * k + 2, :], src[:, k, :, P:2 * P],
                                                      causal[:, 0:2, :], ALU.mult)
                    ins.then_inc(loc_ready, 1)

                def fir(lo, hi):
                    for k in range(lo, hi):
                        kind, c, s, back = fir_order(k)
                        w = (fir_sw, fir_lw)[kind]
                        n = (TAPS_S, TAPS_L)[kind]
                        v = qkv[:, 4 + c, 0:L - s]
                        if k == 0:
                            dve.wait_ge(silu_done, b * 6 + 6)
                        if s == 0:
                            nc.vector.tensor_scalar(firT[:, kind, c, :], v, w[:, c, n - 1:n], None, ALU.mult).then_inc(fir_step, 1)
                        else:
                            dve.wait_ge(fir_step, b * NFIR + k - back + 1)
                            nc.vector.scalar_tensor_tensor(firT[:, kind, c, s:], v, w[:, c, n - 1 - s:n - s],
                                                           firT[:, kind, c, s:], ALU.mult, ALU.add).then_inc(fir_step, 1)

                slot = 0
                for p2 in range(2):
                    for lv in range(1, LEVELS):
                        for g in range(2):
                            n = p2 * 12 + (lv - 1) * 2 + g + 1
                            dve.wait_ge(x_ps, b * 24 + n)
                            nc.vector.tensor_tensor(X[g][:], pair(bank(g)), level[lv], ALU.mult).then_inc(x_ready, 1)
                        fir(slot * NFIR // 12, (slot + 1) * NFIR // 12)
                        slot += 1
                for t in range(NT):
                    dve.wait_ge(u_ps, b * 4 + t + 1)
                    nc.vector.tensor_copy(uadj[:, t, :].rearrange("p (k a c) -> p k a c", k=2, a=2), by_parity(0)).then_inc(u_ready, 1)
                    if t < NT - 1:
                        dve.wait_ge(s_ps, b * 3 + t + 1)
                        s_flat = S[:].rearrange("p a c -> p (a c)")
                        if t == 0:
                            nc.vector.tensor_copy(s_flat, bank(4, 0, P)).then_inc(s_ready, 1)
                        else:
                            dve.wait_ge(s_ready, b * 3 + t)
                            nc.vector.tensor_tensor(s_flat, bank(4, 0, P), s_flat, ALU.add).then_inc(s_ready, 1)
                base = [0]

                def step(ins):
                    base[0] += 1
                    ins.then_inc(ml_ready, 1)
                    dve.wait_ge(ml_ready, b * 11 + base[0])

                dve.wait_ge(lg_ps, b + 1)
                step(nc.vector.tensor_copy(lg[:].rearrange("p a c -> p (a c)"), bank(4, 0, NT * H * 4)))
                rt = spread(spread(rtau[:], 1, NT), 3, 3)
                l3 = lg[:, :, 0:3]
                step(nc.vector.tensor_tensor(l3.rearrange("p (t h) c -> p t h c", t=NT), l3.rearrange("p (t h) c -> p t h c", t=NT), rt, ALU.mult))
                step(nc.vector.reduce_max(mx[:], l3, axis=AX.X))
                step(nc.vector.tensor_tensor(l3, l3, spread(mx[:], 2, 3), ALU.subtract))
                dve.wait_ge(ex_ready, 2 * b + 2)
                step(nc.vector.reduce_sum(sm[:], ex[:, :, 0:3], axis=AX.X))
                step(nc.vector.reciprocal(sm[:], sm[:]))
                step(nc.vector.tensor_scalar(pv[:], ex[:, :, 3], 1.0, None, ALU.add))
                step(nc.vector.reciprocal(pv[:], pv[:]))
                step(nc.vector.tensor_scalar(mx[:], pv[:], 0.1 - 0.01, 1.0 - 0.1, ALU.mult, ALU.add))
                step(nc.vector.tensor_tensor(pv[:], pv[:], mx[:], ALU.mult))
                nc.vector.tensor_copy(wt[:, :, 3], pv[:]).then_inc(wt_ready, 1)
                step(nc.vector.tensor_scalar(mx[:], pv[:], -1.0, 1.0, ALU.mult, ALU.add))
                assert base[0] == 11
                nc.vector.tensor_tensor(sm[:], sm[:], mx[:], ALU.mult).then_inc(wt_ready, 1)
                dve.wait_ge(wt_ready, b * 3 + 2)
                nc.vector.tensor_tensor(wt[:, :, 0:3], ex[:, :, 0:3], spread(sm[:], 2, 3), ALU.mult).then_inc(wt_ready, 1)
                dve.wait_ge(wt_ready, b * 3 + 3)
                for t in range(NT):
                    dve.wait_ge(f_ps, b * 4 + t + 1)
                    w2 = wt[:, H * t:H * t + H, 0:2].rearrange("p h k -> p k h")
                    nc.vector.tensor_tensor(mixa[:, t % 2, :, :].rearrange("p k (h c) -> p k h c", h=H),
                                            bank(t % 2).rearrange("p (k h c) -> p k h c", k=2, h=H),
                                            spread(w2, 3, DK), ALU.mult).then_inc(mixa_ready, 1)
                    dve.wait_ge(mixa_ready, b * 4 + t + 1)
                    dve.wait_ge(mixb_ready, b * 4 + t + 1)
                    nc.vector.tensor_tensor(mixa[:, t % 2, :, :], mixa[:, t % 2, :, :], mixb[:, t % 2, :, :],
                                            ALU.add).then_inc(mix_ready, 1)
                    dve.wait_ge(mix_ready, b * 12 + 3 * t + 1)
                    nc.vector.tensor_tensor(o[:, t, :], mixa[:, t % 2, 0, :], mixa[:, t % 2, 1, :], ALU.add).then_inc(mix_ready, 1)
                    dve.wait_ge(mix_ready, b * 12 + 3 * t + 2)
                    nc.vector.tensor_tensor(oo[:], o[:, t, :], o[:, t, :], ALU.mult).then_inc(mix_ready, 1)
                    dve.wait_ge(mix_ready, b * 12 + 3 * t + 3)
                    nc.vector.reduce_sum(so[:, H * t:H * t + H], oo[:].rearrange("p (h c) -> p h c", h=H), axis=AX.X).then_inc(so_ready, 1)
                dve.wait_ge(so_ready, b * 5 + 4)
                nc.vector.tensor_scalar(so[:], so[:], 1.0 / DK, 1e-5, ALU.mult, ALU.add).then_inc(so_ready, 1)
                dve.wait_ge(ro_ready, b + 1)
                for t in range(NT):
                    nc.vector.tensor_tensor(o[:, t, :].rearrange("p (h c) -> p h c", h=H),
                                            o[:, t, :].rearrange("p (h c) -> p h c", h=H),
                                            spread(ro[:, H * t:H * t + H], 2, DK), ALU.mult).then_inc(on_ready, 1)
                for t in range(NT):
                    dve.wait_ge(y_ps, b * 4 + t + 1)
                    r = resid[:, bass.ds(b * NT + t, 1), :].rearrange("p a d -> p (a d)")
                    nc.vector.tensor_tensor(r, bank(6 + t % 2, 0, D), r, ALU.add).then_inc(resid_done, 1)

        @block.gpsimd
        def _(pool):
            with pool.Fori(0, B) as b:
                pool.wait_ge(mean_ready, b * MERGE + MERGE)
                pool.tensor_tensor(rstd[:], var[:, 0, :], mhalf[:, 0:NT], ALU.pow).then_inc(rstd_ready, 1)
                pool.wait_ge(ss_ready, b * 5 + 5)
                pool.tensor_tensor(rs[:], ss[:], mhalf[:, 0:32], ALU.pow).then_inc(rs_ready, 1)
                pool.wait_ge(beta_ready, 2 * b + 2)
                pool.wait_ge(v_ready, 2 * b + 2)
                for t in range(NT):
                    pool.tensor_tensor(vb[:, t, :].rearrange("p (h c) -> p h c", h=H),
                                       dv[:, t, 1, :].rearrange("p (h c) -> p h c", h=H),
                                       spread(beta[:, H * t:H * t + H], 2, DK), ALU.mult).then_inc(vb_ready, 1)
                    pool.wait_ge(kqn_ready, b * 4 + t + 1)
                    pool.tensor_tensor(kb[:, t, :].rearrange("p (h c) -> p h c", h=H),
                                       kqn[:, t, 0:D].rearrange("p (h c) -> p h c", h=H),
                                       spread(beta[:, H * t:H * t + H], 2, DK), ALU.mult).then_inc(kb_ready, 1)
                for p2 in range(2):
                    for g in range(2):
                        t = 2 * p2 + g
                        pool.wait_ge(AT_ready, b * 4 + t + 1)
                        pool.tensor_tensor(TT[t][:], AT[t][:], up1, ALU.mult).then_inc(tt1_ready, 1)
                        pool.wait_ge(tt1_ready, b * 8 + 2 * t + 1)
                        pool.tensor_tensor(TT[t][:], TT[t][:], eye4, ALU.add).then_inc(tt1_ready, 1)
                    for lv in (1, LEVELS - 1):
                        for g in range(2):
                            pool.wait_ge(x_ready, b * 24 + p2 * 12 + (lv - 1) * 2 + g + 1)
                            pool.tensor_tensor(X[g][:], X[g][:], eye4, ALU.add).then_inc(y_ready, 1)
                pool.wait_ge(wt_ready, b * 3 + 3)
                for t in range(NT):
                    pool.wait_ge(o_ready, b * 4 + t + 1)
                    if t >= 2:
                        pool.wait_ge(mix_ready, b * 12 + 3 * (t - 2) + 1)
                    pool.tensor_tensor(mixb[:, t % 2, :, :].rearrange("p k (h c) -> p k h c", h=H),
                                       dv[:, t, :, :].rearrange("p k (h c) -> p k h c", h=H),
                                       spread(wt[:, H * t:H * t + H, 2:4].rearrange("p h k -> p k h"), 3, DK),
                                       ALU.mult).then_inc(mixb_ready, 1)
                pool.wait_ge(so_ready, b * 5 + 5)
                pool.tensor_tensor(ro[:], so[:], mhalf[:, 0:NT * H], ALU.pow).then_inc(ro_ready, 1)

        @block.scalar
        def _(act):
            act.wait_ge(loaded, 16 * NLOAD)
            nc.scalar.activation(rtau[:], rtau[:], ACT.Exp).then_inc(tau_exp, 1)
            with act.Fori(0, B) as b:
                for c in range(DB):
                    act.wait_ge(xT_ps, b * 2 + c + 1)
                    nc.scalar.activation(xT[:, c, :], bank(c), ACT.Copy).then_inc(xT_ready, 1)
                for m in range(6):
                    act.wait_ge(proj_ps, b * 6 + m + 1)
                    nc.scalar.activation(qkv[:, m, :], bank(m % 2), ACT.Copy, scale=conv_w[:, m, 3:4]).then_inc(tap3_done, 1)
                    if m >= 1:
                        act.wait_ge(conv_done, b * 18 + 3 * m)
                        nc.scalar.activation(qkv[:, m - 1, :], qkv[:, m - 1, :], ACT.Silu).then_inc(silu_done, 1)
                act.wait_ge(conv_done, b * 18 + 18)
                nc.scalar.activation(qkv[:, 5, :], qkv[:, 5, :], ACT.Silu).then_inc(silu_done, 1)
                act.wait_ge(z_ps, b + 1)
                nc.scalar.activation(ez[:], bank(7, 0, NT * H), ACT.Exp, scale=-1.0).then_inc(ez_ready, 1)
                for t in range(NT):
                    act.wait_ge(kq_ps, b * 4 + t + 1)
                    if t >= 2:
                        act.wait_ge(ss_ready, b * 5 + t - 1)
                    nc.scalar.activation(sq[:, t % 2, :], bank(t), ACT.Square).then_inc(sq_ready, 1)
                for j in range(2):
                    act.wait_ge(v_ps, b * 2 + j + 1)
                    nc.scalar.activation(dv[:, 2 * j:2 * j + 2, 1, :], bank(4 + j).rearrange("p (t c) -> p t c", t=2), ACT.Copy).then_inc(v_ready, 1)
                for t in range(NT):
                    for hb in range(DB):
                        act.wait_ge(kT_ps, b * 8 + 2 * t + hb + 1)
                        nc.scalar.activation(kbqT[t][hb][:].rearrange("p a c -> p (a c)"), bank(6 + hb, 0, 3 * P), ACT.Copy).then_inc(kT_ready, 1)
                    act.wait_ge(al_ps, b * 4 + t + 1)
                    src = ps[:, 2 * (t % 2):2 * (t % 2) + 2, :].rearrange("p a (k c) -> p k a c", k=2)
                    nc.scalar.activation(AT[t][:].rearrange("p (k a) c -> p k a c", a=2), src[:, :, :, 0:P], ACT.Copy).then_inc(AT_ready, 1)
                for p2 in range(2):
                    for g in range(2):
                        act.wait_ge(t1_ps, b * 4 + 2 * p2 + g + 1)
                        nc.scalar.activation(T[g][:], pair(bank(4 + g)), ACT.Copy).then_inc(t1_ready, 1)
                    for lv in range(1, LEVELS):
                        if lv < LEVELS - 1:
                            for g in range(2):
                                act.wait_ge(t_ps, b * 20 + p2 * 10 + (lv - 1) * 2 + g + 1)
                                nc.scalar.activation(T[g][:], pair(bank(2 + g)), ACT.Copy).then_inc(t_ready, 1)
                        for g in range(2):
                            act.wait_ge(tt_ps, b * 24 + p2 * 12 + (lv - 1) * 2 + g + 1)
                            nc.scalar.activation(TT[2 * p2 + g][:], pair(bank(4 + g)), ACT.Copy).then_inc(tt_ready, 1)
                for t in range(NT):
                    act.wait_ge(wT_ps, b * 4 + t + 1)
                    nc.scalar.activation(nwT[t][:].rearrange("p a c -> p (a c)"), bank(6 + t % 2, 0, 2 * P), ACT.Copy, scale=-1.0).then_inc(wT_ready, 1)
                for t in range(NT):
                    act.wait_ge(o_ps, b * 4 + t + 1)
                    nc.scalar.activation(dv[:, t, 0, :].rearrange("p (k a c) -> p k a c", k=2, a=2), by_parity(2), ACT.Copy).then_inc(o_ready, 1)
                    act.wait_ge(d_ps, b * 4 + t + 1)
                    nc.scalar.activation(dT[:, :, t * P:(t + 1) * P], bank(5, 0, 2 * P).rearrange("p (a c) -> p a c", a=DB), ACT.Copy).then_inc(d_ready, 1)
                for m in range(4):
                    act.wait_ge(hid_ps, b * 4 + m + 1)
                    nc.scalar.activation(hidT[:, m, :], bank(6 + m % 2), ACT.Gelu, bias=b_f1[:, m:m + 1]).then_inc(hid_ready, 1)
                act.wait_ge(ml_ready, b * 11 + 4)
                nc.scalar.activation(ex[:, :, 0:3], lg[:, :, 0:3], ACT.Exp).then_inc(ex_ready, 1)
                nc.scalar.activation(ex[:, :, 3], lg[:, :, 3], ACT.Exp, scale=-1.0).then_inc(ex_ready, 1)
                for t in range(NT):
                    act.wait_ge(oT_ps, b * 4 + t + 1)
                    nc.scalar.activation(oT[t][:].rearrange("p a c -> p (a c)"), bank(2 + t % 2, 0, 2 * P), ACT.Copy).then_inc(oT_ready, 1)

        @block.tensor
        def _(pe):
            mm = nc.tensor.matmul
            pe.wait_ge(loaded, 16 * NLOAD)
            pe.wait_ge(prepared, 1)
            with pe.Fori(0, B) as b:
                pe.wait_ge(mixa_ready, b * 4)
                pe.wait_ge(xn_ready, b * 4 + 4)
                for c in range(DB):
                    for t in range(NT):
                        ins = nc.tensor.transpose(bank(c, t * P, (t + 1) * P), xn[:, t, c * P:(c + 1) * P], eye)
                    ins.then_inc(xT_ps, 1)
                for m in range(6):
                    if m < 2:
                        pe.wait_ge(xT_ready, b * 2 + 2)
                    else:
                        pe.wait_ge(conv_done, b * 18 + 3 * (m - 1))
                    for c in range(DB):
                        ins = mm(bank(m % 2), w_qkv[:, c, m * P:(m + 1) * P], xT[:, c, :], start=c == 0, stop=c == DB - 1)
                    ins.then_inc(proj_ps, 1)
                pe.wait_ge(resid_done, b * 4)
                for t in range(NT):
                    for c in range(DB):
                        ins = mm(bank(7, t * H, (t + 1) * H), xT[:, c, t * P:(t + 1) * P], w_beta[:, c, :], start=c == 0, stop=c == DB - 1)
                ins.then_inc(z_ps, 1)
                pe.wait_ge(oT_ready, b * 4)
                pe.wait_ge(ml_ready, b * 11)
                pe.wait_ge(silu_done, b * 6 + 4)
                pe.wait_ge(conv_done, b * 18 + 18)
                for t in range(NT):
                    for c in range(4):
                        ins = nc.tensor.transpose(bank(t, c * P, (c + 1) * P), qkv[:, (c + 2) % 4, t * P:(t + 1) * P], eye)
                    ins.then_inc(kq_ps, 1)
                pe.wait_ge(silu_done, b * 6 + 6)
                for t in range(NT):
                    for c in range(2):
                        ins = nc.tensor.transpose(bank(4 + t // 2, (t % 2) * D + c * P, (t % 2) * D + (c + 1) * P),
                                                  qkv[:, 4 + c, t * P:(t + 1) * P], eye)
                    if t % 2:
                        ins.then_inc(v_ps, 1)
                pe.wait_ge(ez_ready, b + 1)
                pe.wait_ge(kqn_ready, b * 4 + 4)
                for t in range(NT):
                    pe.wait_ge(kb_ready, b * 4 + t + 1)
                    if t:
                        pe.wait_ge(kT_ready, b * 8 + 2 * t)
                    for hb in range(DB):
                        for n, src in enumerate((kqn[:, t, hb * P:(hb + 1) * P], kb[:, t, hb * P:(hb + 1) * P],
                                                 kqn[:, t, D + hb * P:D + (hb + 1) * P])):
                            ins = nc.tensor.transpose(bank(6 + hb, n * P, (n + 1) * P), src, eye)
                        ins.then_inc(kT_ps, 1)
                    pe.wait_ge(kT_ready, b * 8 + 2 * t + 2)
                    if t >= 2:
                        pe.wait_ge(AT_ready, b * 4 + t - 1)
                        pe.wait_ge(loc_ready, b * 4 + t - 1)
                    for h in range(H):
                        r = 64 * (h % 2)
                        k3 = kbqT[t][h // 2]
                        ins = mm(bank(2 * (t % 2) + h % 2, (h // 2) * 2 * P, (h // 2 + 1) * 2 * P),
                                 k3[r:r + 64, 0, :], k3[r:r + 64, 1:3, :], start=True, stop=True)
                    ins.then_inc(al_ps, 1)

                def x_of(p2, lv, g):
                    t = 2 * p2 + g
                    if lv == 1:
                        pe.wait_ge(t1_ready, b * 4 + t + 1)
                    else:
                        pe.wait_ge(t_ready, b * 20 + p2 * 10 + (lv - 2) * 2 + g + 1)
                    for h in range(H):
                        ins = mm(bank(g, h * P, (h + 1) * P), AT[t][:, h, :], T[g][:, h, :], start=True, stop=True)
                    ins.then_inc(x_ps, 1)

                for p2 in range(2):
                    for g in range(2):
                        t = 2 * p2 + g
                        pe.wait_ge(tt1_ready, b * 8 + 2 * t + 2)
                        pe.wait_ge(v_ready, b * 2 + 2)
                        if p2:
                            pe.wait_ge(tt_ready, b * 24 + 10 + g + 1)
                        for h in range(H):
                            ins = nc.tensor.transpose(bank(4 + g, h * P, (h + 1) * P), TT[t][:, h, :], eye)
                        ins.then_inc(t1_ps, 1)
                    if p2 == 0:
                        pe.wait_ge(AT_ready, b * 4 + 4)
                        pe.wait_ge(loc_ready, b * 4 + 4)
                    for g in range(2):
                        x_of(p2, 1, g)
                    for lv in range(1, LEVELS):
                        for g in range(2):
                            t = 2 * p2 + g
                            if lv in (1, LEVELS - 1):
                                pe.wait_ge(y_ready, b * 8 + p2 * 4 + (lv > 1) * 2 + g + 1)
                            else:
                                pe.wait_ge(x_ready, b * 24 + p2 * 12 + (lv - 1) * 2 + g + 1)
                            if lv > 1:
                                pe.wait_ge(tt_ready, b * 24 + p2 * 12 + (lv - 2) * 2 + g + 1)
                            if lv == LEVELS - 1:
                                for h in range(H):
                                    ins = mm(bank(4 + g, h * P, (h + 1) * P), X[g][:, h, :], TT[t][:, h, :], start=True, stop=True)
                                ins.then_inc(tt_ps, 1)
                            else:
                                for h in range(H):
                                    ins = mm(bank(2 + g, h * P, (h + 1) * P), TT[t][:, h, :], X[g][:, h, :],
                                             start=lv == 1 and h == 0, stop=lv == LEVELS - 2 and h == H - 1, skip_group_check=True)
                                ins.then_inc(t_ps, 1)
                        if lv < LEVELS - 1:
                            for g in range(2):
                                t = 2 * p2 + g
                                pe.wait_ge(t_ready, b * 20 + p2 * 10 + (lv - 1) * 2 + g + 1)
                                for h in range(H):
                                    ins = nc.tensor.transpose(bank(4 + g, h * P, (h + 1) * P), T[g][:, h, :], eye)
                                ins.then_inc(tt_ps, 1)
                                x_of(p2, lv + 1, g)
                for t in range(NT):
                    pe.wait_ge(tt_ready, b * 24 + (t // 2) * 12 + 10 + t % 2 + 1)
                    if t >= 2:
                        pe.wait_ge(wT_ready, b * 4 + t - 1)
                    for h in range(H):
                        r = 64 * (h % 2)
                        ins = mm(ps[r:r + 64, 6 + t % 2, (h // 2) * P:(h // 2 + 1) * P], kb[:, t, h * DK:(h + 1) * DK], TT[t][:, h, :],
                                 start=True, stop=True)
                    ins.then_inc(wT_ps, 1)
                pe.wait_ge(vb_ready, b * 4 + 4)
                for t in range(NT):
                    if t:
                        pe.wait_ge(s_ready, b * 3 + t)
                    pe.wait_ge(wT_ready, b * 4 + t + 1)
                    for h in range(H):
                        r = 64 * (h % 2)
                        ins = mm(bank(h % 2, (h // 2) * DK, (h // 2 + 1) * DK), TT[t][:, h, :], vb[:, t, h * DK:(h + 1) * DK], start=True, stop=t == 0)
                        if t:
                            ins = mm(bank(h % 2, (h // 2) * DK, (h // 2 + 1) * DK), nwT[t][r:r + 64, h // 2, :], S[r:r + 64, h // 2, :], start=False, stop=True)
                    ins.then_inc(u_ps, 1)
                    if t:
                        pe.wait_ge(o_ready, b * 4 + t)
                    pe.wait_ge(u_ready, b * 4 + t + 1)
                    for h in range(H):
                        r = 64 * (h % 2)
                        out = bank(2 + h % 2, (h // 2) * DK, (h // 2 + 1) * DK)
                        if t:
                            mm(out, kbqT[t][h // 2][r:r + 64, 2, :], S[r:r + 64, h // 2, :], start=True, stop=False)
                        ins = mm(out, loc[t][:, h, :], uadj[:, t, h * DK:(h + 1) * DK], start=t == 0, stop=True)
                    ins.then_inc(o_ps, 1)
                    if t < NT - 1:
                        for h in range(H):
                            r = 64 * (h % 2)
                            ins = mm(ps[r:r + 64, 4, (h // 2) * DK:(h // 2 + 1) * DK], kqn[:, t, h * DK:(h + 1) * DK],
                                     uadj[:, t, h * DK:(h + 1) * DK], start=True, stop=True)
                        ins.then_inc(s_ps, 1)
                    pe.wait_ge(o_ready, b * 4 + t + 1)
                    if t:
                        pe.wait_ge(d_ready, b * 4 + t)
                    for c in range(DB):
                        ins = nc.tensor.transpose(bank(5, c * P, (c + 1) * P), dv[:, t, 0, c * P:(c + 1) * P], eye)
                    ins.then_inc(d_ps, 1)
                pe.wait_ge(fir_step, b * NFIR + NFIR)
                pe.wait_ge(d_ready, b * 4 + 4)
                gate_in = [xT[:, 0, :], xT[:, 1, :], firT[:, 0, 0, :], firT[:, 0, 1, :], firT[:, 1, 0, :], firT[:, 1, 1, :],
                           dT[:, 0, :], dT[:, 1, :]]
                for m in range(4):
                    if m >= 2:
                        pe.wait_ge(hid_ready, b * 4 + m - 1)
                    for c in range(8):
                        ins = mm(bank(6 + m % 2), w_f1[:, c, m * P:(m + 1) * P], gate_in[c], start=c == 0, stop=c == 7)
                    ins.then_inc(hid_ps, 1)
                pe.wait_ge(hid_ready, b * 4 + 4)
                for t in range(NT):
                    out = bank(4, t * 16, (t + 1) * 16)
                    mm(out, one_row, b_f2[:], start=True, stop=False)
                    for c in range(4):
                        ins = mm(out, hidT[:, c, t * P:(t + 1) * P], w_f2[:, c, :], start=False, stop=c == 3)
                ins.then_inc(lg_ps, 1)
                for t in range(NT):
                    if t >= 2:
                        pe.wait_ge(mixa_ready, b * 4 + t - 1)
                    for kind in range(2):
                        for c in range(DB):
                            ins = nc.tensor.transpose(bank(t % 2, (2 * kind + c) * P, (2 * kind + c + 1) * P), firT[:, kind, c, t * P:(t + 1) * P], eye)
                    ins.then_inc(f_ps, 1)
                for t in range(NT):
                    pe.wait_ge(on_ready, b * 4 + t + 1)
                    if t >= 2:
                        pe.wait_ge(oT_ready, b * 4 + t - 1)
                    for c in range(DB):
                        ins = nc.tensor.transpose(bank(2 + t % 2, c * P, (c + 1) * P), o[:, t, c * P:(c + 1) * P], eye)
                    ins.then_inc(oT_ps, 1)
                for t in range(NT):
                    pe.wait_ge(oT_ready, b * 4 + t + 1)
                    if t >= 2:
                        pe.wait_ge(resid_done, b * 4 + t - 1)
                    for c in range(DB):
                        ins = mm(bank(6 + t % 2, 0, D), oT[t][:, c, :], w_o[:, c, :], start=c == 0, stop=c == 1)
                    ins.then_inc(y_ps, 1)


def expert_scores(nc, A, const, resid, ps, prob, mean_all, rstd_all):
    with ExitStack() as ctx:
        mk = Maker(nc, ctx, "sc_")
        sb, sem = mk.sb, mk.sem
        eye = const[:, C_EYE:C_EYE + P]
        mhalf = const[:, C_MHALF:C_MHALF + NT]
        w_rows = sb("w_rows", [E, D])
        w_gate = sb("w_gate", [P, DB, E])
        stats = sb("stats", [P, NT, 6])
        mean, var, rstd = sb("mean", [P, NT]), sb("var", [P, 3, NT]), sb("rstd", [P, NT])
        xn = sb("xn", [P, NT, D])
        xT = sb("xT", [P, DB, L])
        sc = sb("sc", [P, NT, E])
        top = sb("top", [P, NT])
        ex = sb("ex", [P, NT, E])
        den = sb("den", [P, NT])
        loaded, gate_ps, gate_ready = sem("loaded"), sem("gate_ps"), sem("gate_ready")
        stat_done, mean_ready, rstd_ready, xn_ready = sem("stat_done"), sem("mean_ready"), sem("rstd_ready"), sem("xn_ready")
        xT_ps, xT_ready, sc_ps, sc_ready, ex_ready, den_ready, prob_done = (
            sem(n) for n in ("xT_ps", "xT_ready", "sc_ps", "sc_ready", "ex_ready", "den_ready", "prob_done"))
        block = ctx.enter_context(nc.Block())

        @block.sync
        def _(sp):
            sp.dma_start(w_rows[:], A["L0_ffn_gate_w"]).then_inc(loaded, 16)

        @block.vector
        def _(dve):
            dve.wait_ge(gate_ps, 1)
            nc.vector.tensor_copy(w_gate[:].rearrange("p c e -> p (c e)"), ps[:, 3, 0:DB * E]).then_inc(gate_ready, 1)
            with dve.Fori(0, B) as b:
                for t in range(NT):
                    nc.vector.bn_stats(stats[:, t, :], resid[:, bass.ds(b * NT + t, 1), :].rearrange("p a d -> p (a d)")).then_inc(stat_done, 1)
                dve.wait_ge(stat_done, b * NT + NT)
                merge_stats(nc, dve, stats, mean, var, mean_ready, b)
                dve.wait_ge(mean_ready, b * MERGE + MERGE)
                dve.wait_ge(rstd_ready, b + 1)
                for t in range(NT):
                    nc.vector.tensor_scalar(xn[:, t, :], resid[:, bass.ds(b * NT + t, 1), :].rearrange("p a d -> p (a d)"),
                                            mean[:, t:t + 1], rstd[:, t:t + 1], ALU.subtract, ALU.mult).then_inc(xn_ready, 1)
                nc.vector.tensor_copy(mean_all[:, bass.ds(b * NT, NT)], mean[:]).then_inc(prob_done, 1)
                nc.vector.tensor_copy(rstd_all[:, bass.ds(b * NT, NT)], rstd[:]).then_inc(prob_done, 1)
                dve.wait_ge(sc_ps, b + 1)
                nc.vector.tensor_copy(sc[:].rearrange("p t e -> p (t e)"), ps[:, 2, 0:NT * E]).then_inc(sc_ready, 1)
                dve.wait_ge(sc_ready, b * 3 + 1)
                nc.vector.reduce_max(top[:], sc[:], axis=AX.X).then_inc(sc_ready, 1)
                dve.wait_ge(sc_ready, b * 3 + 2)
                nc.vector.tensor_tensor(sc[:], sc[:], spread(top[:], 2, E), ALU.subtract).then_inc(sc_ready, 1)
                dve.wait_ge(ex_ready, b + 1)
                nc.vector.reduce_sum(den[:], ex[:], axis=AX.X).then_inc(den_ready, 1)
                dve.wait_ge(den_ready, b * 2 + 1)
                nc.vector.reciprocal(den[:], den[:]).then_inc(den_ready, 1)
                dve.wait_ge(den_ready, b * 2 + 2)
                nc.vector.tensor_tensor(prob[:, :, bass.ds(b * E, E)], ex[:], spread(den[:], 2, E), ALU.mult).then_inc(prob_done, 1)

        @block.gpsimd
        def _(pool):
            with pool.Fori(0, B) as b:
                pool.wait_ge(mean_ready, b * MERGE + MERGE)
                pool.tensor_tensor(rstd[:], var[:, 0, :], mhalf, ALU.pow).then_inc(rstd_ready, 1)

        @block.scalar
        def _(act):
            with act.Fori(0, B) as b:
                for c in range(DB):
                    act.wait_ge(xT_ps, b * 2 + c + 1)
                    nc.scalar.activation(xT[:, c, :], ps[:, c, :], ACT.Copy).then_inc(xT_ready, 1)
                act.wait_ge(sc_ready, b * 3 + 3)
                nc.scalar.activation(ex[:], sc[:], ACT.Exp).then_inc(ex_ready, 1)

        @block.tensor
        def _(pe):
            pe.wait_ge(loaded, 16)
            for c in range(DB):
                ins = nc.tensor.transpose(ps[:, 3, c * E:(c + 1) * E], w_rows[:, c * P:(c + 1) * P], const[0:E, C_EYE:C_EYE + E])
            ins.then_inc(gate_ps, 1)
            pe.wait_ge(gate_ready, 1)
            with pe.Fori(0, B) as b:
                pe.wait_ge(xn_ready, b * NT + NT)
                pe.wait_ge(xT_ready, b * 2)
                for c in range(DB):
                    for t in range(NT):
                        ins = nc.tensor.transpose(ps[:, c, t * P:(t + 1) * P], xn[:, t, c * P:(c + 1) * P], eye)
                    ins.then_inc(xT_ps, 1)
                pe.wait_ge(xT_ready, b * 2 + 2)
                pe.wait_ge(sc_ready, b * 3)
                for t in range(NT):
                    for c in range(DB):
                        ins = nc.tensor.matmul(ps[:, 2, t * E:(t + 1) * E], xT[:, c, t * P:(t + 1) * P], w_gate[:, c, :],
                                               start=c == 0, stop=c == DB - 1)
                ins.then_inc(sc_ps, 1)


def choose_tokens(nc, const, ps, prob, idxT, gT, idx_dram):
    R = B * E
    with ExitStack() as ctx:
        mk = Maker(nc, ctx, "ch_")
        sb, sem = mk.sb, mk.sem
        work = sb("work", [R, L])
        vals = sb("vals", [R, CAP])
        idx = sb("idx", [R, CAP], U32)
        idxf = sb("idxf", [R, CAP])
        rows_ps, found, moved, idx_out, back_ps = (sem(n) for n in ("rows_ps", "found", "moved", "idx_out", "back_ps"))
        block = ctx.enter_context(nc.Block())

        @block.vector
        def _(dve):
            n = [0]

            def chain(ins):
                n[0] += 1
                ins.then_inc(found, 1)
                dve.wait_ge(found, n[0])

            dve.wait_ge(rows_ps, 1)
            chain(nc.vector.tensor_copy(work[:], ps[0:R, 0, :]))
            for r in range(CAP // 8):
                v = vals[:, 8 * r:8 * r + 8]
                chain(nc.vector.max(v, work[:]))
                chain(nc.vector.max_index(idx[:, 8 * r:8 * r + 8], v, work[:]))
                chain(nc.vector.match_replace(work[:], v, work[:], -1.0))
            nc.vector.tensor_copy(idxf[:], idx[:]).then_inc(moved, 1)
            dve.wait_ge(back_ps, 1)
            nc.vector.tensor_copy(idxT[:], ps[:, 1, 0:R]).then_inc(moved, 1)
            nc.vector.tensor_copy(gT[:], ps[:, 1, P:P + R]).then_inc(moved, 1)

        @block.sync
        def _(sp):
            sp.wait_ge(moved, 1)
            sp.dma_start(idx_dram, idxf[:]).then_inc(idx_out, 16)
            sp.wait_ge(idx_out, 16)

        @block.tensor
        def _(pe):
            for t in range(NT):
                ins = nc.tensor.transpose(ps[0:R, 0, t * P:(t + 1) * P], prob[:, t, :], const[:, C_EYE:C_EYE + P])
            ins.then_inc(rows_ps, 1)
            pe.wait_ge(moved, 1)
            nc.tensor.transpose(ps[:, 1, 0:R], idxf[:], const[0:R, C_EYE:C_EYE + R])
            nc.tensor.transpose(ps[:, 1, P:P + R], vals[:], const[0:R, C_EYE:C_EYE + R]).then_inc(back_ps, 1)


def gather_tokens(nc, const, resid, ps, mean_all, rstd_all, idx_dram, slots):
    with ExitStack() as ctx:
        mk = Maker(nc, ctx, "ga_")
        sb, sem = mk.sb, mk.sem
        idxb = [sb(f"idxb{j}", [P, E * CAP]) for j in range(2)]
        xn = [[sb(f"xn{j}{t}", [P, D]) for t in range(NT)] for j in range(2)]
        pick = [sb(f"pick{j}", [P, NT, E * CAP]) for j in range(2)]
        st = [[sb(f"m{j}", [P, NT]), sb(f"r{j}", [P, NT])] for j in range(2)]
        idx_in, stat_ready, in_ready, out_ps, out_ready = ([sem(f"{n}{j}") for j in range(2)] for n in ("idx_in", "stat_ready", "in_ready", "out_ps", "out_ready"))
        rows = idx_dram.rearrange("(n e) s -> n (e s)", e=E)
        block = ctx.enter_context(nc.Block())

        @block.sync
        def _(sp):
            with sp.Fori(0, B // 2) as i:
                for j in range(2):
                    sp.wait_ge(in_ready[j], i * 2 * NT)
                    sp.dma_start(idxb[j][:], rows[bass.ds(2 * i + j, 1), :].broadcast_to([P, E * CAP])).then_inc(idx_in[j], 16)

        @block.vector
        def _(dve):
            with dve.Fori(0, B // 2) as i:
                for j in range(2):
                    nc.vector.tensor_copy(st[j][0][:], mean_all[:, bass.ds((2 * i + j) * NT, NT)]).then_inc(stat_ready[j], 1)
                    nc.vector.tensor_copy(st[j][1][:], rstd_all[:, bass.ds((2 * i + j) * NT, NT)]).then_inc(stat_ready[j], 1)
                    dve.wait_ge(stat_ready[j], i * 2 + 2)
                    dve.wait_ge(out_ps[j], i * 4)
                    dve.wait_ge(idx_in[j], i * 16 + 16)
                    for t in range(NT):
                        nc.vector.tensor_scalar(xn[j][t][:], resid[:, bass.ds((2 * i + j) * NT + t, 1), :].rearrange("p a d -> p (a d)"),
                                                st[j][0][:, t:t + 1], st[j][1][:, t:t + 1], ALU.subtract, ALU.mult).then_inc(in_ready[j], 1)
                        nc.vector.tensor_scalar(pick[j][:, t, :], idxb[j][:], const[:, C_TOKID + t:C_TOKID + t + 1], None,
                                                ALU.is_equal).then_inc(in_ready[j], 1)

        @block.scalar
        def _(act):
            with act.Fori(0, B // 2) as i:
                for j in range(2):
                    for half in range(2):
                        for c in range(DB):
                            act.wait_ge(out_ps[j], i * 4 + 2 * half + c + 1)
                            dst = slots[:, 4 * half:4 * half + 4, bass.ds(c * B * CAP + (2 * i + j) * CAP, CAP)]
                            nc.scalar.activation(dst, ps[:, 4 * j + 2 * half + c, :].rearrange("p (e s) -> p e s", e=4),
                                                 ACT.Copy).then_inc(out_ready[j], 1)

        @block.tensor
        def _(pe):
            with pe.Fori(0, B // 2) as i:
                for j in range(2):
                    pe.wait_ge(out_ready[j], i * 4)
                    pe.wait_ge(in_ready[j], i * 2 * NT + 2 * NT)
                    for half in range(2):
                        for c in range(DB):
                            for t in range(NT):
                                ins = nc.tensor.matmul(ps[:, 4 * j + 2 * half + c, :], xn[j][t][:, c * P:(c + 1) * P],
                                                       pick[j][:, t, half * 512:(half + 1) * 512], start=t == 0, stop=t == NT - 1)
                            ins.then_inc(out_ps[j], 1)


def experts(nc, A, ps, slots):
    FB = F0 // P
    with ExitStack() as ctx:
        mk = Maker(nc, ctx, "ex_")
        sb, sem = mk.sb, mk.sem
        w1 = [sb(f"w1_{j}", [P, DB, F0]) for j in range(2)]
        w2 = [sb(f"w2_{j}", [P, FB, D]) for j in range(2)]
        hT = [sb(f"hT{half}", [P, FB, 512]) for half in range(2)]
        w_in, dn_ps = ([sem(f"{n}{j}") for j in range(2)] for n in ("w_in", "dn_ps"))
        up_ps, up_ready, dn_ready = sem("up_ps"), sem("up_ready"), sem("dn_ready")
        w1_dram = A["L0_ffn_w1"].rearrange("e (c p) f -> p e c f", p=P)
        w2_dram = A["L0_ffn_w2"].rearrange("e (c p) d -> p e c d", p=P)
        block = ctx.enter_context(nc.Block())

        @block.sync
        def _(sp):
            with sp.Fori(0, E // 2) as i:
                for j in range(2):
                    sp.wait_ge(dn_ps[j], i * B)
                    e = bass.ds(2 * i + j, 1)
                    sp.dma_start(w1[j][:], w1_dram[:, e, :, :].rearrange("p a c f -> p (a c) f")).then_inc(w_in[j], 16)
                    sp.dma_start(w2[j][:], w2_dram[:, e, :, :].rearrange("p a c f -> p (a c) f")).then_inc(w_in[j], 16)

        @block.tensor
        def _(pe):
            with pe.Fori(0, E // 2) as i:
                for j in range(2):
                    up, dn = i * 4 * FB + j * 2 * FB, i * 2 * B + j * B
                    pe.wait_ge(w_in[j], i * 32 + 32)
                    for half in range(2):
                        for f in range(FB):
                            n = half * FB + f
                            if n >= 4:
                                pe.wait_ge(up_ready, up + n - 3)
                            for c in range(DB):
                                ins = nc.tensor.matmul(ps[:, n % 4, :], w1[j][:, c, f * P:(f + 1) * P],
                                                       slots[:, bass.ds(2 * i + j, 1), c * B * CAP + half * 512:c * B * CAP + half * 512 + 512].rearrange("p a s -> p (a s)"),
                                                       start=c == 0, stop=c == DB - 1)
                            ins.then_inc(up_ps, 1)
                    for n in range(B):
                        half = n // 4
                        if n % 4 == 0:
                            pe.wait_ge(up_ready, up + (half + 1) * FB)
                        if n >= 4:
                            pe.wait_ge(dn_ready, dn + n - 3)
                        else:
                            pe.wait_ge(dn_ready, dn)
                        for f in range(FB):
                            ins = nc.tensor.matmul(ps[:, 4 + n % 4, 0:D], hT[half][:, f, (n % 4) * CAP:(n % 4 + 1) * CAP], w2[j][:, f, :],
                                                   start=f == 0, stop=f == FB - 1)
                        ins.then_inc(dn_ps[j], 1)

        @block.scalar
        def _(act):
            with act.Fori(0, E // 2) as i:
                for j in range(2):
                    up, dn = i * 4 * FB + j * 2 * FB, i * 2 * B + j * B
                    for half in range(2):
                        act.wait_ge(dn_ps[1 - j], (i + j) * B)
                        for f in range(FB):
                            n = half * FB + f
                            act.wait_ge(up_ps, up + n + 1)
                            nc.scalar.activation(hT[half][:, f, :], ps[:, n % 4, :], ACT.Gelu).then_inc(up_ready, 1)

        @block.vector
        def _(dve):
            with dve.Fori(0, E // 2) as i:
                for j in range(2):
                    up, dn = i * 4 * FB + j * 2 * FB, i * 2 * B + j * B
                    for n in range(B):
                        dve.wait_ge(dn_ps[j], i * B + n + 1)
                        nc.vector.tensor_copy(slots[:, bass.ds(2 * i + j, 1), n * D:(n + 1) * D].rearrange("p a d -> p (a d)"),
                                              ps[:, 4 + n % 4, 0:D]).then_inc(dn_ready, 1)


def layer1(nc, A, const, resid, ps, slots, idxT, gT, out):
    HB = F1 // P
    NB = P + 8
    with ExitStack() as ctx:
        mk = Maker(nc, ctx, "l1_")
        sb, sem = mk.sb, mk.sem
        eye = const[:, C_EYE:C_EYE + P]
        mhalf = const[:, C_MHALF:C_MHALF + NT]
        one_row = const[0:1, C_ONE:C_ONE + P]
        one_col = const[:, C_ONE:C_ONE + 1]
        heads = const[:, C_HEADS:C_HEADS + NB]
        wqkv = sb("wqkv", [P, DB, 3 * D])
        qnw = sb("qnw", [P, DB])
        knw = sb("knw", [P, D])
        wout = sb("wout", [P, DB, D])
        bout = sb("bout", [1, D])
        wg, wu = sb("wg", [P, DB, F1]), sb("wu", [P, DB, F1])
        wd = sb("wd", [P, HB, D])
        idxn, gn = sb("idxn", [P, E]), sb("gn", [P, E])
        put = sb("put", [P, E, L])
        xw = sb("xw", [P, NT, D])
        stats = sb("stats", [P, NT, 6])
        mean, var, rstd = sb("mean", [P, NT]), sb("var", [P, 3, NT]), sb("rstd", [P, NT])
        xn = sb("xn", [P, NT, D])
        xT = sb("xT", [P, DB, L])
        qT = sb("qT", [P, DB, L])
        sqq = xn[:].rearrange("p t d -> p (t d)").rearrange("p (c l) -> p c l", c=DB)
        sqk = sb("sqk", [P, D])
        ssk, ssq = sb("ssk", [P, NT]), sb("ssq", [P, NT])
        rk, rq = sb("rk", [P, NT]), sb("rq", [P, NT])
        k2 = sb("k2", [P, NT, D])
        vx = sb("vx", [P, NT, DB, NB])
        kvm = sb("kvm", [P, DB, NB])
        nrm = sb("nrm", [P, 2, DB, 8])
        o = sb("o", [P, 2, D])
        oT = [sb(f"oT{t}", [P, DB, P]) for t in range(2)]
        gs = sb("gs", [P, 2, 512])
        hT = sb("hT", [P, HB, L])
        yo = sb("yo", [P, 2, NT, D])
        raw = put[:].rearrange("p e l -> p (e l)")[:, 0:HB * D].bitcast(I32)
        rawf = hT[:].rearrange("p m l -> p (m l)")[:, 0:HB * D]

        loaded, raw_in, raw_ready, raw_ps, raw_done, ones_set = (
            sem(n) for n in ("loaded", "raw_in", "raw_ready", "raw_ps", "raw_done", "ones_set"))
        small, put_ready, add_ps, xw_ready = sem("small"), sem("put_ready"), sem("add_ps"), sem("xw_ready")
        stat_done, mean_ready, rstd_ready, xn_ready, xT_ps, xT_ready = (
            sem(n) for n in ("stat_done", "mean_ready", "rstd_ready", "xn_ready", "xT_ps", "xT_ready"))
        kv_ps, v_ready, ssk_ready, rk_ready, kk_ready, k2_ready = (
            sem(n) for n in ("kv_ps", "v_ready", "ssk_ready", "rk_ready", "kk_ready", "k2_ready"))
        q_ps, q_ready, ssq_ps, ssq_ready, rq_ready, kvm_ps, kvm_ready = (
            sem(n) for n in ("q_ps", "q_ready", "ssq_ps", "ssq_ready", "rq_ready", "kvm_ps", "kvm_ready"))
        att_ps, nrm_step, o_ready, oT_ps, oT_ready, wo_ps = (
            sem(n) for n in ("att_ps", "nrm_step", "o_ready", "oT_ps", "oT_ready", "wo_ps"))
        g_ps, g_ready, u_ps, h_ready, y_ps, y_ready = (
            sem(n) for n in ("g_ps", "g_ready", "u_ps", "h_ready", "y_ps", "y_ready"))
        stored = [sem(f"stored{j}") for j in range(2)]
        mm = nc.tensor.matmul
        block = ctx.enter_context(nc.Block())

        def bank(n, lo=0, hi=512):
            return ps[:, n, lo:hi]

        out_v = out.rearrange("b (t p) d -> p b t d", p=P)
        ints = [("L1_ffn_w_gate", HB, D), ("L1_ffn_w_up", HB, D), ("L1_ffn_w_down", DB, F1)]

        @block.sync
        def _(sp):
            with nc.allow_non_contiguous_dma(reason="small parameters"):
                sp.dma_start(wqkv[:], A["L1_attn_W_qkv"].rearrange("(c p) n -> p c n", p=P)).then_inc(loaded, 16)
                sp.dma_start(qnw[:], A["L1_attn_qn_w"].rearrange("(c p) -> p c", p=P)).then_inc(loaded, 16)
                sp.dma_start(knw[:], A["L1_attn_kn_w"].unsqueeze(0).broadcast_to([P, D])).then_inc(loaded, 16)
                sp.dma_start(wout[:], A["L1_attn_W_out"].rearrange("(c p) n -> p c n", p=P)).then_inc(loaded, 16)
                sp.dma_start(bout[:], A["L1_attn_b_out"].unsqueeze(0)).then_inc(loaded, 16)
            for n, (name, rb, cols) in enumerate(ints):
                if n:
                    sp.wait_ge(raw_ready, n)
                sp.dma_start(raw.rearrange("p (r c) -> p r c", r=rb), A[name].rearrange("(r p) c -> p r c", p=P)).then_inc(raw_in, 16)
            with sp.Fori(0, B // 2) as i:
                for j in range(2):
                    sp.wait_ge(y_ready, i * 2 * NT + (j + 1) * NT)
                    sp.dma_start(out_v[:, bass.ds(2 * i + j, 1), :, :].rearrange("p a t d -> p (a t) d"), yo[:, j, :, :]).then_inc(stored[j], 16)
            for j in range(2):
                sp.wait_ge(stored[j], 16 * (B // 2))

        def norm(dve, base, half):
            for t in range(NT):
                nc.vector.bn_stats(stats[:, t, :], xw[:, t, :]).then_inc(stat_done, 1)
            dve.wait_ge(stat_done, base * 2 * NT + (half + 1) * NT)
            merge_stats(nc, dve, stats, mean, var, mean_ready, base * 2 + half)
            dve.wait_ge(rstd_ready, base * 2 + half + 1)
            for t in range(NT):
                nc.vector.tensor_scalar(xn[:, t, :], xw[:, t, :], mean[:, t:t + 1], rstd[:, t:t + 1], ALU.subtract, ALU.mult).then_inc(xn_ready, 1)

        @block.vector
        def _(dve):
            nc.vector.memset(vx[:, :, :, P:NB].rearrange("p a b c -> p (a b) c"), 1.0).then_inc(ones_set, 1)
            for n, (name, rb, cols) in enumerate(ints):
                dve.wait_ge(raw_in, 16 * n + 16)
                if n:
                    dve.wait_ge(raw_ps, 4 * n)
                nc.vector.tensor_scalar(rawf, raw, 1.0 / 127.0, None, ALU.mult).then_inc(raw_ready, 1)
                for q in range(4):
                    dve.wait_ge(raw_ps, 4 * n + q + 1)
                    if n < 2:
                        dst = (wg, wu)[n][:, q // 2, (q % 2) * 384:(q % 2) * 384 + 384]
                    else:
                        dst = wd[:, 3 * (q // 2):3 * (q // 2) + 3, (q % 2) * P:(q % 2 + 1) * P]
                    src = bank(q, 0, 384)
                    nc.vector.tensor_copy(dst, src if n < 2 else src.rearrange("p (a c) -> p a c", a=3)).then_inc(raw_done, 1)
            dve.wait_ge(raw_done, 12)
            dve.wait_ge(loaded, 80)
            with dve.Fori(0, B // 2) as i:
                for j in range(2):
                    n = 2 * i + j
                    nc.vector.tensor_copy(idxn[:], idxT[:, bass.ds(n * E, E)]).then_inc(small, 1)
                    nc.vector.tensor_copy(gn[:], gT[:, bass.ds(n * E, E)]).then_inc(small, 1)
                    dve.wait_ge(small, n * 2 + 2)
                    dve.wait_ge(add_ps, n * NT)
                    for e in range(E):
                        nc.vector.tensor_scalar(put[:, e, :], const[:, C_TOK:C_TOK + L], idxn[:, e:e + 1], gn[:, e:e + 1],
                                                ALU.is_equal, ALU.mult).then_inc(put_ready, 1)
                    for t in range(NT):
                        dve.wait_ge(add_ps, n * NT + t + 1)
                        nc.vector.tensor_tensor(xw[:, t, :], bank(t % 2, 0, D),
                                                resid[:, bass.ds(n * NT + t, 1), :].rearrange("p a d -> p (a d)"), ALU.add).then_inc(xw_ready, 1)
                    dve.wait_ge(xw_ready, n * 2 * NT + NT)
                    norm(dve, n, 0)
                    dve.wait_ge(ssk_ready, n * (NT + 1) + NT)
                    nc.vector.tensor_scalar(ssk[:], ssk[:], 1.0 / D, 1e-6, ALU.mult, ALU.add).then_inc(ssk_ready, 1)
                    dve.wait_ge(ssq_ps, n + 1)
                    nc.vector.tensor_scalar(ssq[:], bank(2, 0, NT), 1.0 / D, 1e-6, ALU.mult, ALU.add).then_inc(ssq_ready, 1)
                    dve.wait_ge(rk_ready, n + 1)
                    dve.wait_ge(v_ready, n * NT + NT)
                    for t in range(NT):
                        nc.vector.scalar_tensor_tensor(k2[:, t, :], bank(4 + t, 0, D), rk[:, t:t + 1], knw[:], ALU.mult, ALU.mult).then_inc(kk_ready, 1)
                    dve.wait_ge(kvm_ps, n + 1)
                    for hb in range(DB):
                        nc.vector.tensor_tensor(kvm[:, hb, :], bank(3, hb * NB, (hb + 1) * NB), heads, ALU.mult).then_inc(kvm_ready, 1)
                    dve.wait_ge(rq_ready, n + 1)
                    for t in range(NT):
                        r = nrm[:, t % 2, :, :]
                        dve.wait_ge(att_ps, n * NT + t + 1)
                        att = bank(t % 2, 0, DB * NB).rearrange("p (k c) -> p k c", k=DB)
                        nc.vector.tensor_scalar(r, att[:, :, P:NB], rq[:, t:t + 1], 1e-6, ALU.mult, ALU.add).then_inc(nrm_step, 1)
                        dve.wait_ge(nrm_step, n * 3 * NT + 3 * t + 1)
                        nc.vector.reciprocal(r, r).then_inc(nrm_step, 1)
                        dve.wait_ge(nrm_step, n * 3 * NT + 3 * t + 2)
                        nc.vector.tensor_scalar(r, r, rq[:, t:t + 1], None, ALU.mult).then_inc(nrm_step, 1)
                        dve.wait_ge(nrm_step, n * 3 * NT + 3 * t + 3)
                        if t >= 2:
                            dve.wait_ge(oT_ps, n * NT + t - 1)
                        for hb in range(DB):
                            ins = nc.vector.tensor_tensor(o[:, t % 2, hb * P:(hb + 1) * P].rearrange("p (h c) -> p h c", h=8),
                                                          att[:, hb, 0:P].rearrange("p (h c) -> p h c", h=8),
                                                          spread(r[:, hb, :], 2, DH1), ALU.mult)
                        ins.then_inc(o_ready, 1)
                    for t in range(NT):
                        dve.wait_ge(wo_ps, n * NT + t + 1)
                        nc.vector.tensor_tensor(xw[:, t, :], bank(4 + t % 2, 0, D), xw[:, t, :], ALU.add).then_inc(xw_ready, 1)
                    dve.wait_ge(xw_ready, n * 2 * NT + 2 * NT)
                    norm(dve, n, 1)
                    for m in range(HB):
                        dve.wait_ge(u_ps, n * HB + m + 1)
                        dve.wait_ge(g_ready, n * HB + m + 1)
                        if m == 0:
                            dve.wait_ge(y_ps, n * NT)
                        nc.vector.tensor_tensor(hT[:, m, :], bank(2 + m % 2), gs[:, m % 2, :], ALU.mult).then_inc(h_ready, 1)
                    dve.wait_ge(stored[j], 16 * i)
                    for t in range(NT):
                        dve.wait_ge(y_ps, n * NT + t + 1)
                        nc.vector.tensor_tensor(yo[:, j, t, :], bank(4 + t, 0, D), xw[:, t, :], ALU.add).then_inc(y_ready, 1)

        @block.gpsimd
        def _(pool):
            with pool.Fori(0, B) as n:
                pool.wait_ge(mean_ready, (n * 2 + 1) * MERGE)
                pool.tensor_tensor(rstd[:], var[:, 0, :], mhalf, ALU.pow).then_inc(rstd_ready, 1)
                pool.wait_ge(ssk_ready, (n + 1) * (NT + 1))
                pool.tensor_tensor(rk[:], ssk[:], mhalf, ALU.pow).then_inc(rk_ready, 1)
                pool.wait_ge(ssq_ready, n + 1)
                pool.tensor_tensor(rq[:], ssq[:], mhalf, ALU.pow).then_inc(rq_ready, 1)
                pool.wait_ge(mean_ready, (n * 2 + 2) * MERGE)
                pool.tensor_tensor(rstd[:], var[:, 0, :], mhalf, ALU.pow).then_inc(rstd_ready, 1)

        @block.scalar
        def _(act):
            act.wait_ge(loaded, 80)
            act.wait_ge(ones_set, 1)
            with act.Fori(0, B) as n:
                for c in range(DB):
                    act.wait_ge(xT_ps, n * 4 + c + 1)
                    nc.scalar.activation(xT[:, c, :], bank(2 + c), ACT.Copy).then_inc(xT_ready, 1)
                for c in range(DB):
                    act.wait_ge(q_ps, n * 2 + c + 1)
                    nc.scalar.activation(sqq[:, c, :], bank(c), ACT.Square).then_inc(q_ready, 1)
                    nc.scalar.activation(qT[:, c, :], bank(c), ACT.Relu, scale=qnw[:, c:c + 1]).then_inc(q_ready, 1)
                for t in range(NT):
                    act.wait_ge(kv_ps, n * NT + t + 1)
                    act.wait_ge(ssk_ready, n * (NT + 1) + t)
                    nc.scalar.activation(sqk[:], bank(4 + t, 0, D), ACT.Square, accum_out=ssk[:, t:t + 1]).then_inc(ssk_ready, 1)
                    nc.scalar.activation(vx[:, t, :, 0:P], bank(4 + t, D, 2 * D).rearrange("p (k c) -> p k c", k=DB), ACT.Copy).then_inc(v_ready, 1)
                for t in range(NT):
                    act.wait_ge(kk_ready, n * NT + t + 1)
                    nc.scalar.activation(k2[:, t, :], k2[:, t, :], ACT.Relu).then_inc(k2_ready, 1)
                for t in range(NT):
                    act.wait_ge(oT_ps, n * NT + t + 1)
                    nc.scalar.activation(oT[t % 2][:].rearrange("p a c -> p (a c)"), bank(2 + t % 2, 0, D), ACT.Copy).then_inc(oT_ready, 1)
                for c in range(DB):
                    act.wait_ge(xT_ps, n * 4 + 2 + c + 1)
                    nc.scalar.activation(xT[:, c, :], bank(6 + c), ACT.Copy).then_inc(xT_ready, 1)
                for m in range(HB):
                    act.wait_ge(g_ps, n * HB + m + 1)
                    if m >= 2:
                        act.wait_ge(h_ready, n * HB + m - 1)
                    nc.scalar.activation(gs[:, m % 2, :], bank(m % 2), ACT.Silu).then_inc(g_ready, 1)

        def out_tile(pe, n, t):
            pe.wait_ge(o_ready, n * NT + t + 1)
            if t == 0:
                pe.wait_ge(kvm_ready, n * 2 + 2)
            if t >= 2:
                pe.wait_ge(oT_ready, n * NT + t - 1)
            for c in range(DB):
                ins = nc.tensor.transpose(bank(2 + t % 2, c * P, (c + 1) * P), o[:, t % 2, c * P:(c + 1) * P], eye)
            ins.then_inc(oT_ps, 1)
            pe.wait_ge(oT_ready, n * NT + t + 1)
            if t >= 2:
                pe.wait_ge(xw_ready, n * 2 * NT + NT + t - 1)
            mm(bank(4 + t % 2, 0, D), one_row, bout[:], start=True, stop=False)
            for c in range(DB):
                ins = mm(bank(4 + t % 2, 0, D), oT[t % 2][:, c, :], wout[:, c, :], start=False, stop=c == DB - 1)
            ins.then_inc(wo_ps, 1)

        @block.tensor
        def _(pe):
            for n, (name, rb, cols) in enumerate(ints):
                pe.wait_ge(raw_ready, n + 1)
                for q in range(4):
                    if n:
                        pe.wait_ge(raw_done, 4 * (n - 1) + q + 1)
                    for r in range(3):
                        if n < 2:
                            src = rawf[:, (3 * (q % 2) + r) * D + (q // 2) * P:(3 * (q % 2) + r) * D + (q // 2 + 1) * P]
                        else:
                            src = rawf[:, (q % 2) * F1 + (3 * (q // 2) + r) * P:(q % 2) * F1 + (3 * (q // 2) + r + 1) * P]
                        ins = nc.tensor.transpose(bank(q, r * P, (r + 1) * P), src, eye)
                    ins.then_inc(raw_ps, 1)
            pe.wait_ge(raw_done, 12)
            pe.wait_ge(loaded, 80)
            with pe.Fori(0, B) as n:
                pe.wait_ge(put_ready, n * E + E)
                pe.wait_ge(g_ready, n * HB)
                for t in range(NT):
                    if t >= 2:
                        pe.wait_ge(xw_ready, n * 2 * NT + t - 1)
                    for e in range(E):
                        ins = mm(bank(t % 2, 0, D), put[:, e, t * P:(t + 1) * P], slots[:, e, bass.ds(n * D, D)], start=e == 0, stop=e == E - 1)
                    ins.then_inc(add_ps, 1)
                pe.wait_ge(h_ready, n * HB)
                pe.wait_ge(xn_ready, n * 2 * NT + NT)
                for c in range(DB):
                    for t in range(NT):
                        ins = nc.tensor.transpose(bank(2 + c, t * P, (t + 1) * P), xn[:, t, c * P:(c + 1) * P], eye)
                    ins.then_inc(xT_ps, 1)
                pe.wait_ge(xw_ready, n * 2 * NT + NT)
                pe.wait_ge(xT_ready, n * 4 + 2)
                for m in range(DB):
                    for c in range(DB):
                        ins = mm(bank(m), wqkv[:, c, m * P:(m + 1) * P], xT[:, c, :], start=c == 0, stop=c == DB - 1)
                    ins.then_inc(q_ps, 1)
                pe.wait_ge(y_ready, n * NT)
                for t in range(NT):
                    for c in range(DB):
                        ins = mm(bank(4 + t), xT[:, c, t * P:(t + 1) * P], wqkv[:, c, D:3 * D], start=c == 0, stop=c == DB - 1)
                    ins.then_inc(kv_ps, 1)
                pe.wait_ge(q_ready, n * 4 + 4)
                for t in range(NT):
                    for c in range(DB):
                        ins = mm(bank(2, t, t + 1), sqq[:, c, t * P:(t + 1) * P], one_col, start=c == 0, stop=c == DB - 1)
                ins.then_inc(ssq_ps, 1)
                for hb in range(DB):
                    for t in range(NT):
                        pe.wait_ge(k2_ready, n * NT + t + 1)
                        ins = mm(bank(3, hb * NB, (hb + 1) * NB), k2[:, t, hb * P:(hb + 1) * P], vx[:, t, hb, :], start=t == 0, stop=t == NT - 1)
                ins.then_inc(kvm_ps, 1)
                pe.wait_ge(kvm_ready, n * 2 + 2)
                for t in range(NT):
                    if t >= 2:
                        pe.wait_ge(o_ready, n * NT + t - 1)
                    for hb in range(DB):
                        ins = mm(bank(t % 2, hb * NB, (hb + 1) * NB), qT[:, hb, t * P:(t + 1) * P], kvm[:, hb, :], start=True, stop=True)
                    ins.then_inc(att_ps, 1)
                    if t == 0:
                        pe.wait_ge(ssq_ready, n + 1)
                    if t >= 1:
                        out_tile(pe, n, t - 1)
                out_tile(pe, n, NT - 1)
                pe.wait_ge(xn_ready, n * 2 * NT + 2 * NT)
                for c in range(DB):
                    for t in range(NT):
                        ins = nc.tensor.transpose(bank(6 + c, t * P, (t + 1) * P), xn[:, t, c * P:(c + 1) * P], eye)
                    ins.then_inc(xT_ps, 1)
                pe.wait_ge(xT_ready, n * 4 + 4)
                pe.wait_ge(o_ready, n * NT + NT)
                for m in range(HB):
                    if m >= 2:
                        pe.wait_ge(g_ready, n * HB + m - 1)
                    for c in range(DB):
                        ins = mm(bank(m % 2), wg[:, c, m * P:(m + 1) * P], xT[:, c, :], start=c == 0, stop=c == DB - 1)
                    ins.then_inc(g_ps, 1)
                    if m >= 2:
                        pe.wait_ge(h_ready, n * HB + m - 1)
                    for c in range(DB):
                        ins = mm(bank(2 + m % 2), wu[:, c, m * P:(m + 1) * P], xT[:, c, :], start=c == 0, stop=c == DB - 1)
                    ins.then_inc(u_ps, 1)
                pe.wait_ge(h_ready, n * HB + HB)
                for t in range(NT):
                    for m in range(HB):
                        ins = mm(bank(4 + t, 0, D), hT[:, m, t * P:(t + 1) * P], wd[:, m, :], start=m == 0, stop=m == HB - 1)
                    ins.then_inc(y_ps, 1)


def program(nc, A, out):
    with ExitStack() as ctx:
        mk = Maker(nc, ctx)
        const = mk.sb("const", [P, C_END])
        resid = mk.sb("resid", [P, B * NT, D])
        ps = ctx.enter_context(nc.psum_tensor("ps", [P, 8, 512], F32))
        idx_dram = nc.dram_tensor("idx_dram", [B * E, CAP], F32).ap()
        x_in = A["L0_attn_hidden_states"].rearrange("b (t p) d -> p (b t) d", p=P)
        got = mk.sem("got")
        with nc.Block() as block:
            @block.sync
            def _(sp):
                sp.dma_start(const[:], A["const"]).then_inc(got, 16)
                for b in range(B):
                    sp.dma_start(resid[:, b * NT:(b + 1) * NT, :], x_in[:, b * NT:(b + 1) * NT, :]).then_inc(got, 16)
                sp.wait_ge(got, 16 * (B + 1))
        attention0(nc, A, const, resid, ps)
        slots = mk.sb("slots", [P, E, DB * B * CAP])
        prob = mk.sb("prob", [P, NT, B * E])
        mean_all, rstd_all = mk.sb("mean_all", [P, B * NT]), mk.sb("rstd_all", [P, B * NT])
        idxT, gT = mk.sb("idxT", [P, B * E]), mk.sb("gT", [P, B * E])
        expert_scores(nc, A, const, resid, ps, prob, mean_all, rstd_all)
        choose_tokens(nc, const, ps, prob, idxT, gT, idx_dram)
        gather_tokens(nc, const, resid, ps, mean_all, rstd_all, idx_dram, slots)
        experts(nc, A, ps, slots)
        layer1(nc, A, const, resid, ps, slots, idxT, gT, out)


def kernel(**inputs):
    import numpy as _np
    import concourse.bacc as _bacc
    from concourse import mybir as _mybir
    from concourse.bass_utils import run_bass_kernel_spmd as _run

    nc = _bacc.Bacc("TRN2", target_bir_lowering=False, num_devices=1)
    arrays, aps = {}, {}
    for name, a in {**inputs, "const": constant_table()}.items():
        a = _np.ascontiguousarray(a)
        arrays[f"in_{name}"] = a
        aps[name] = nc.dram_tensor(f"in_{name}", a.shape, _mybir.dt.from_np(a.dtype), kind="ExternalInput").ap()
    out = nc.dram_tensor("out_0", (B, L, D), F32, kind="ExternalOutput").ap()
    program(nc, aps, out)
    return _run(nc, [arrays], core_ids=[0]).results[0]["out_0"]
```

```python
import concourse.bass as bass
from concourse import mybir
from contextlib import ExitStack

F32 = mybir.dt.float32
I32 = mybir.dt.int32
U32 = mybir.dt.uint32
ALU = mybir.AluOpType
ACT = mybir.ActivationFunctionType
AX = mybir.AxisListType

P = 128
B, L, D = 8, 512, 256
NT = L // P
DB = D // P
H, DK = 4, 64
E, CAP = 8, 2 * L // 8
F0 = 1024
H1, DH1 = 16, 16
F1 = 768
LEVELS = 7
TAPS_S, TAPS_L = 3, 31

C_EYE = 0
C_LEVEL = C_EYE + P
C_UP1 = C_LEVEL + LEVELS * P
C_CAUSAL = C_UP1 + P
C_HEADS = C_CAUSAL + P
C_PAIR = C_HEADS + P + 8
C_TOK = C_PAIR + P
C_TOKID = C_TOK + L
C_ONE = C_TOKID + NT
C_MHALF = C_ONE + P
C_END = C_MHALF + 32


def constant_table():
    import numpy as np
    i = np.arange(P)
    t = np.zeros((P, C_END), np.float32)
    t[:, C_EYE:C_EYE + P] = np.eye(P)
    for n in range(LEVELS):
        s = 1 << n
        low = (i[:, None] // (2 * s) == i[None] // (2 * s)) & (i[:, None] // s % 2 == 1) & (i[None] // s % 2 == 0)
        t[:, C_LEVEL + n * P:C_LEVEL + (n + 1) * P] = -1.0 * low
        if n == 0:
            t[:, C_UP1:C_UP1 + P] = -1.0 * low.T
    t[:, C_CAUSAL:C_CAUSAL + P] = i[:, None] <= i[None]
    t[:, C_HEADS:C_HEADS + P] = i[:, None] // DH1 == i[None] // DH1
    t[:, C_HEADS + P:C_HEADS + P + 8] = i[:, None] // DH1 == np.arange(8)[None]
    t[:, C_PAIR:C_PAIR + P] = i[:, None] // DK == i[None] // DK
    t[:, C_TOK:C_TOK + L] = np.arange(L)[None]
    t[:, C_TOKID:C_TOKID + NT] = i[:, None] + P * np.arange(NT)[None]
    t[:, C_ONE:C_ONE + P] = 1.0
    t[:, C_MHALF:C_MHALF + 32] = -0.5
    return t


def spread(ap, axis, n):
    shape = list(ap.shape)
    shape.insert(axis, n)
    return ap.unsqueeze(axis).broadcast_to(shape)


class Maker:

    def __init__(self, nc, ctx, prefix=""):
        self.nc, self.ctx, self.prefix = nc, ctx, prefix

    def sb(self, name, shape, dt=F32):
        return self.ctx.enter_context(self.nc.sbuf_tensor(self.prefix + name, shape, dt))

    def sem(self, name):
        return self.ctx.enter_context(self.nc.semaphore(self.prefix + name))


MERGE = 7


def merge_stats(nc, dve, stats, mean, var, done, i):
    ev, od = stats[:, :, 1], stats[:, :, 4]
    nc.vector.tensor_tensor(mean[:], ev, od, ALU.add).then_inc(done, 1)
    nc.vector.tensor_tensor(var[:, 1, :], ev, od, ALU.subtract).then_inc(done, 1)
    nc.vector.tensor_tensor(var[:, 2, :], stats[:, :, 2], stats[:, :, 5], ALU.add).then_inc(done, 1)
    dve.wait_ge(done, i * MERGE + 3)
    nc.vector.tensor_scalar(mean[:], mean[:], 0.5, None, ALU.mult).then_inc(done, 1)
    nc.vector.tensor_scalar(var[:, 2, :], var[:, 2, :], 1.0 / D, 1e-5, ALU.mult, ALU.add).then_inc(done, 1)
    nc.vector.tensor_tensor(var[:, 1, :], var[:, 1, :], var[:, 1, :], ALU.mult).then_inc(done, 1)
    dve.wait_ge(done, i * MERGE + 6)
    nc.vector.scalar_tensor_tensor(var[:, 0, :], var[:, 1, :], 0.25, var[:, 2, :], ALU.mult, ALU.add).then_inc(done, 1)


def attention0(nc, A, const, resid, ps, prob, mean_all, rstd_all):
    with ExitStack() as ctx:
        mk = Maker(nc, ctx, "a0_")
        sb, sem = mk.sb, mk.sem
        eye = const[:, C_EYE:C_EYE + P]
        eye4 = spread(eye, 1, H)
        level = [spread(const[:, C_LEVEL + n * P:C_LEVEL + (n + 1) * P], 1, H) for n in range(LEVELS)]
        up1 = spread(const[:, C_UP1:C_UP1 + P], 1, H)
        causal = spread(const[:, C_CAUSAL:C_CAUSAL + P], 1, 2)
        same_head = spread(const[:, C_PAIR:C_PAIR + P], 1, DB)
        mhalf = const[:, C_MHALF:C_MHALF + 32]

        w_qkv = sb("w_qkv", [P, DB, 3 * D])
        w_beta = sb("w_beta", [P, DB, P])
        w_route = sb("w_route", [P, DB, P])
        w_f2 = sb("w_f2", [P, 4, P])
        conv_w = sb("conv_w", [P, 6, 4])
        fir_sw = sb("fir_sw", [P, DB, TAPS_S])
        fir_lw = sb("fir_lw", [P, DB, TAPS_L])
        w_f1 = sb("w_f1", [P, 8, 2 * D])
        b_f1 = sb("b_f1", [P, 4])
        b_f2 = sb("b_f2", [P, 16])
        rtau = sb("rtau", [P, H])
        normw = sb("normw", [P, 1])
        w_o = sb("w_o", [P, DB, D])
        small_w = sb("small_w", [P, DB, H])
        small_f = sb("small_f", [P, 4, 16])

        stats = sb("stats", [P, NT, 6])
        mean = sb("mean", [P, NT])
        var = sb("var", [P, 3, NT])
        rstd = sb("rstd", [P, NT])
        g_stats = sb("g_stats", [P, NT, 6])
        g_mean = sb("g_mean", [P, NT])
        g_var = sb("g_var", [P, 3, NT])
        g_rstd = sb("g_rstd", [P, NT])
        xn = sb("xn", [P, NT, D])
        xT = sb("xT", [P, DB, L])
        qkv = sb("qkv", [P, 6, L])
        ez = sb("ez", [P, NT * H])
        beta = sb("beta", [P, NT * H])
        sq = sb("sq", [P, 512])
        ss = sb("ss", [P, NT * 8])
        rs = sb("rs", [P, NT * 8])
        kz = sb("kz", [P, NT, H * P])
        qn = sb("qn", [P, NT, D])
        dv = sb("dv", [P, NT, 2, D])
        vk = sb("vk", [P, NT, 2, D])
        kT = [[sb(f"kT{t}{hb}", [P, 4, P]) for hb in range(DB)] for t in range(NT)]
        hidT = sb("hidT", [P, 4, L])
        AT = [hidT[:, t, :].rearrange("p (h c) -> p h c", h=H) for t in range(NT)]
        loc = [sb(f"loc{t}", [P, H, P]) for t in range(NT)]
        TT = [sb(f"TT{t}", [P, H, P]) for t in range(NT)]
        T = [sb(f"T{g}", [P, H, P]) for g in range(2)]
        X = [sb(f"X{g}", [P, H, P]) for g in range(2)]
        mixa = [T[g][:].rearrange("p h c -> p (h c)").rearrange("p (k d) -> p k d", k=2) for g in range(2)]
        mixb = [X[g][:].rearrange("p h c -> p (h c)").rearrange("p (k d) -> p k d", k=2) for g in range(2)]
        rT = [T[g][:].rearrange("p h c -> p (h c)") for g in range(2)]
        w_tok = [sb(f"w_tok{g}", [P, D]) for g in range(2)]
        nwT = [sb(f"nwT{t}", [P, DB, P]) for t in range(NT)]
        uadj = sb("uadj", [P, NT, D])
        S = sb("S", [P, DB, P])
        dT = sb("dT", [P, DB, L])
        firT = sb("firT", [P, 2, DB, L])
        lg = sb("lg", [P, NT * H, 4])
        mx = sb("mx", [P, NT * H])
        ex = sb("ex", [P, NT * H, 4])
        sm = sb("sm", [P, NT * H])
        pv = sb("pv", [P, NT * H])
        wt = sb("wt", [P, NT * H, 4])
        o = sb("o", [P, NT, D])
        so = sb("so", [P, NT * H])
        ro = sb("ro", [P, NT * H])
        oT = [sb(f"oT{t}", [P, DB, P]) for t in range(2)]
        sc = sb("sc", [P, NT, E])
        g_top, g_den = sb("g_top", [P, NT]), sb("g_den", [P, NT])
        g_ex = sb("g_ex", [P, NT, E])
        w_rows = sb("w_rows", [E, D])

        loaded, prepared, prep, pads = sem("loaded"), sem("prepared"), sem("prep"), sem("pads")
        tau_exp, route_ps = sem("tau_exp"), sem("route_ps")
        stat_done, mean_ready, rstd_ready, xn_ready = (sem(n) for n in ("stat_done", "mean_ready", "rstd_ready", "xn_ready"))
        xT_ps, xT_ready = sem("xT_ps"), sem("xT_ready")
        proj_ps, tap3_done, conv_done, silu_done = sem("proj_ps"), sem("tap3_done"), sem("conv_done"), sem("silu_done")
        z_ps, ez_ready, beta_ready = sem("z_ps"), sem("ez_ready"), sem("beta_ready")
        kq_ps, sq_ready, ss_ready, rs_ready, kqn_ready = (sem(n) for n in ("kq_ps", "sq_ready", "ss_ready", "rs_ready", "kqn_ready"))
        v_ps, v_ready, vk_ready = sem("v_ps"), sem("v_ready"), sem("vk_ready")
        kT_ps, kT_ready, al_ps, AT_ready, loc_ready = (sem(n) for n in ("kT_ps", "kT_ready", "al_ps", "AT_ready", "loc_ready"))
        tt1_ready, t1_ps, t1_ready = sem("tt1_ready"), sem("t1_ps"), sem("t1_ready")
        x_ps, x_ready, t_ps, t_ready, tt_ps, tt_ready = (
            sem(n) for n in ("x_ps", "x_ready", "t_ps", "t_ready", "tt_ps", "tt_ready"))
        uw_ps, uw_ready, wT_ps, wT_ready = sem("uw_ps"), sem("uw_ready"), sem("wT_ps"), sem("wT_ready")
        ws_ps, u_ready, o_ps, o_ready, s_ps, s_ready, d_ps, d_ready = (
            sem(n) for n in ("ws_ps", "u_ready", "o_ps", "o_ready", "s_ps", "s_ready", "d_ps", "d_ready"))
        fir_step = sem("fir_step")
        hid_ps, hid_ready, lg_ps = sem("hid_ps"), sem("hid_ready"), sem("lg_ps")
        ml_ready, ex_ready, wt_ready = sem("ml_ready"), sem("ex_ready"), sem("wt_ready")
        f_ps, mixa_ready, mixb_ready, mix_ready, osq_ready = (
            sem(n) for n in ("f_ps", "mixa_ready", "mixb_ready", "mix_ready", "osq_ready"))
        so_ready, ro_ready, on_ready = sem("so_ready"), sem("ro_ready"), sem("on_ready")
        oT_ps, oT_ready, y_ps, resid_done = sem("oT_ps"), sem("oT_ready"), sem("y_ps"), sem("resid_done")
        g_stat, g_mean_ready, g_rstd_ready, g_xn_ready, rT_ps, rT_ready, sc_ps, sc_ready, g_ex_ready, g_den_ready, prob_done = (
            sem(n) for n in ("g_stat", "g_mean_ready", "g_rstd_ready", "g_xn_ready", "rT_ps", "rT_ready", "sc_ps", "sc_ready",
                             "g_ex_ready", "g_den_ready", "prob_done"))

        def bank(n, lo=0, hi=512):
            return ps[:, n, lo:hi]

        def by_head(ap):
            return ap.rearrange("p (h c) -> p h c", h=H)

        def rows(i, t):
            return resid[:, bass.ds(i * NT + t, 1), :].rearrange("p a d -> p (a d)")

        def k_of(t):
            v = kz[:, t, :].rearrange("p (k a c) -> p k a c", k=2, a=4)
            return v[:, :, 0:4:3, 0:DK]

        NLOAD = 18
        NFIR = 2 * (TAPS_S + TAPS_L)
        block = ctx.enter_context(nc.Block())

        @block.sync
        def _(sp):
            with nc.allow_non_contiguous_dma(reason="small parameters"):
                for j, n in enumerate(("W_q", "W_k", "W_v")):
                    sp.dma_start(w_qkv[:, :, j * D:(j + 1) * D],
                                 A["L0_attn_" + n].rearrange("(c p) n -> p c n", p=P)).then_inc(loaded, 16)
                sp.dma_start(small_w[:], A["L0_attn_W_b"].rearrange("(c p) n -> p c n", p=P)).then_inc(loaded, 16)
                for j, n in enumerate("qkv"):
                    sp.dma_start(conv_w[:, 2 * j:2 * j + 2, :],
                                 A[f"L0_attn_conv_w_{n}"].rearrange("(c p) k -> p c k", p=P)).then_inc(loaded, 16)
                sp.dma_start(fir_sw[:], A["L0_attn_fir_short_w"].rearrange("h d k -> (h d) k")
                             .rearrange("(c p) k -> p c k", p=P)).then_inc(loaded, 16)
                sp.dma_start(fir_lw[:], A["L0_attn_fir_long_w"].rearrange("h d k -> (h d) k")
                             .rearrange("(c p) k -> p c k", p=P)).then_inc(loaded, 16)
                sp.dma_start(w_f1[:], A["L0_attn_W_fuse1"].rearrange("(c p) n -> p c n", p=P)).then_inc(loaded, 16)
                sp.dma_start(b_f1[:], A["L0_attn_b_fuse1"].rearrange("(c p) -> p c", p=P)).then_inc(loaded, 16)
                sp.dma_start(small_f[:], A["L0_attn_W_fuse2"].rearrange("(c p) n -> p c n", p=P)).then_inc(loaded, 16)
                sp.dma_start(b_f2[:], A["L0_attn_b_fuse2"].unsqueeze(0).broadcast_to([P, 16])).then_inc(loaded, 16)
                sp.dma_start(rtau[:], A["L0_attn_others_log_tau"].unsqueeze(0).broadcast_to([P, H])).then_inc(loaded, 16)
                for half in range(2):
                    sp.dma_start(normw[64 * half:64 * half + 64, :],
                                 A["L0_attn_norm_w"].unsqueeze(1)).then_inc(loaded, 16)
                sp.dma_start(w_o[:], A["L0_attn_W_o"].rearrange("(c p) n -> p c n", p=P)).then_inc(loaded, 16)
                sp.dma_start(w_rows[:], A["L0_ffn_gate_w"]).then_inc(loaded, 16)

        def fir_order(k):
            if k < 4 * TAPS_S:
                return k // 2 % 2, k % 2, k // 4, 4
            k -= 4 * TAPS_S
            return 1, k % 2, TAPS_S + k // 2, 2

        @block.vector
        def _(dve):
            nc.vector.memset(kz[:].rearrange("p t c -> p (t c)"), 0.0).then_inc(pads, 1)
            nc.vector.memset(w_beta[:].rearrange("p c n -> p (c n)"), 0.0).then_inc(pads, 1)
            nc.vector.memset(w_route[:].rearrange("p c n -> p (c n)"), 0.0).then_inc(pads, 1)
            nc.vector.memset(w_f2[:].rearrange("p c n -> p (c n)"), 0.0).then_inc(pads, 1)
            dve.wait_ge(loaded, 16 * NLOAD)
            dve.wait_ge(pads, 4)
            nc.vector.tensor_copy(w_beta[:, :, 0:H], small_w[:]).then_inc(prepared, 1)
            nc.vector.tensor_copy(w_f2[:, :, 0:16], small_f[:]).then_inc(prepared, 1)
            nc.vector.tensor_scalar(w_o[:].rearrange("p c n -> p (c n)"), w_o[:].rearrange("p c n -> p (c n)"),
                                    normw[:, 0:1], None, ALU.mult).then_inc(prepared, 1)
            dve.wait_ge(route_ps, 1)
            nc.vector.tensor_copy(w_route[:, :, 0:E], bank(3, 0, DB * E).rearrange("p (c e) -> p c e", c=DB)).then_inc(prepared, 1)
            dve.wait_ge(tau_exp, 1)
            nc.vector.reciprocal(rtau[:], rtau[:]).then_inc(prep, 1)
            dve.wait_ge(prep, 1)

            def norm_in(b, route=None):
                for t in range(NT):
                    nc.vector.bn_stats(stats[:, t, :], rows(b, t)).then_inc(stat_done, 1)
                dve.wait_ge(stat_done, b * NT + NT)
                merge_stats(nc, dve, stats, mean, var, mean_ready, b)
                dve.wait_ge(mean_ready, b * MERGE + MERGE)
                dve.wait_ge(rstd_ready, b + 1)
                if route is not None:
                    dve.wait_ge(rT_ps, route * 2 + 2)
                for t in range(NT):
                    nc.vector.tensor_scalar(xn[:, t, :], rows(b, t), mean[:, t:t + 1], rstd[:, t:t + 1],
                                            ALU.subtract, ALU.mult).then_inc(xn_ready, 1)

            def conv(b, m):
                dve.wait_ge(tap3_done, b * 6 + m + 1)
                for s in range(1, 4):
                    if s > 1:
                        dve.wait_ge(conv_done, b * 18 + 3 * m + s - 1)
                    nc.vector.scalar_tensor_tensor(
                        qkv[:, m, s:], bank(m % 3, 0, L - s), conv_w[:, m, 3 - s:4 - s],
                        qkv[:, m, s:], ALU.mult, ALU.add).then_inc(conv_done, 1)

            def fir(b, lo, hi):
                for k in range(lo, hi):
                    kind, c, s, back = fir_order(k)
                    w = (fir_sw, fir_lw)[kind]
                    n = (TAPS_S, TAPS_L)[kind]
                    v = qkv[:, 4 + c, 0:L - s]
                    if k == 0:
                        dve.wait_ge(silu_done, b * 6 + 6)
                    if s == 0:
                        nc.vector.tensor_scalar(firT[:, kind, c, :], v, w[:, c, n - 1:n], None, ALU.mult).then_inc(fir_step, 1)
                    else:
                        dve.wait_ge(fir_step, b * NFIR + k - back + 1)
                        nc.vector.scalar_tensor_tensor(firT[:, kind, c, s:], v, w[:, c, n - 1 - s:n - s],
                                                       firT[:, kind, c, s:], ALU.mult, ALU.add).then_inc(fir_step, 1)

            def route_stats(b):
                for t in range(NT):
                    nc.vector.bn_stats(g_stats[:, t, :], rows(b, t)).then_inc(g_stat, 1)
                dve.wait_ge(g_stat, b * NT + NT)
                merge_stats(nc, dve, g_stats, g_mean, g_var, g_mean_ready, b)

            def route_norm(b):
                dve.wait_ge(g_mean_ready, b * MERGE + MERGE)
                dve.wait_ge(g_rstd_ready, b + 1)
                for t in range(NT):
                    nc.vector.tensor_scalar(xn[:, t, :], rows(b, t), g_mean[:, t:t + 1], g_rstd[:, t:t + 1],
                                            ALU.subtract, ALU.mult).then_inc(g_xn_ready, 1)
                nc.vector.tensor_copy(mean_all[:, bass.ds(b * NT, NT)], g_mean[:]).then_inc(prob_done, 1)
                nc.vector.tensor_copy(rstd_all[:, bass.ds(b * NT, NT)], g_rstd[:]).then_inc(prob_done, 1)

            def route_scores(b):
                dve.wait_ge(sc_ps, b + 1)
                nc.vector.tensor_copy(sc[:], bank(7).rearrange("p (t e) -> p t e", t=NT)[:, :, 0:E]).then_inc(sc_ready, 1)
                dve.wait_ge(sc_ready, b * 3 + 1)
                nc.vector.reduce_max(g_top[:], sc[:], axis=AX.X).then_inc(sc_ready, 1)
                dve.wait_ge(sc_ready, b * 3 + 2)
                nc.vector.tensor_tensor(sc[:], sc[:], spread(g_top[:], 2, E), ALU.subtract).then_inc(sc_ready, 1)

            def route_prob(b):
                dve.wait_ge(g_ex_ready, b + 1)
                nc.vector.reduce_sum(g_den[:], g_ex[:], axis=AX.X).then_inc(g_den_ready, 1)
                dve.wait_ge(g_den_ready, b * 2 + 1)
                nc.vector.reciprocal(g_den[:], g_den[:]).then_inc(g_den_ready, 1)
                dve.wait_ge(g_den_ready, b * 2 + 2)
                nc.vector.tensor_tensor(prob[:, :, bass.ds(b * E, E)], g_ex[:], spread(g_den[:], 2, E), ALU.mult).then_inc(prob_done, 1)

            def main(b, route, norm_next):
                slot = 0
                for p2 in range(2):
                    for lv in range(1, LEVELS):
                        for g in range(2):
                            n = p2 * 12 + (lv - 1) * 2 + g + 1
                            dve.wait_ge(x_ps, b * 24 + n)
                            nc.vector.tensor_tensor(X[g][:], by_head(bank(g)), level[lv], ALU.mult).then_inc(x_ready, 1)
                        fir(b, slot * NFIR // 12, (slot + 1) * NFIR // 12)
                        slot += 1
                if route is not None:
                    route_stats(route)
                    route_norm(route)
                for t in range(NT):
                    if t:
                        dve.wait_ge(ws_ps, b * 3 + t)
                        dve.wait_ge(uw_ready, b * 8 + 8)
                        nc.vector.tensor_tensor(uadj[:, t, :], bank(4, 0, D), uadj[:, t, :], ALU.add).then_inc(u_ready, 1)
                    if t < NT - 1:
                        dve.wait_ge(s_ps, b * 3 + t + 1)
                        nc.vector.tensor_tensor(S[:], bank(6, 0, D).rearrange("p (a c) -> p a c", a=DB), same_head, ALU.mult).then_inc(s_ready, 1)
                if norm_next is not None:
                    norm_in(norm_next, route)
                if route is not None:
                    route_scores(route)

            def softmax_in(b, base):
                def step(ins):
                    base[0] += 1
                    ins.then_inc(ml_ready, 1)
                    dve.wait_ge(ml_ready, b * 11 + base[0])

                dve.wait_ge(lg_ps, b + 1)
                step(nc.vector.tensor_tensor(lg[:].rearrange("p (t h) c -> p t (h c)", t=NT),
                                             bank(6).rearrange("p (t c) -> p t c", t=NT)[:, :, 0:16], spread(b_f2[:], 1, NT), ALU.add))
                rt = spread(spread(rtau[:], 1, NT), 3, 3)
                l3 = lg[:, :, 0:3]
                step(nc.vector.tensor_tensor(l3.rearrange("p (t h) c -> p t h c", t=NT), l3.rearrange("p (t h) c -> p t h c", t=NT), rt, ALU.mult))
                step(nc.vector.reduce_max(mx[:], l3, axis=AX.X))
                step(nc.vector.tensor_tensor(l3, l3, spread(mx[:], 2, 3), ALU.subtract))

                def rest():
                    dve.wait_ge(ex_ready, 2 * b + 2)
                    step(nc.vector.reduce_sum(sm[:], ex[:, :, 0:3], axis=AX.X))
                    step(nc.vector.reciprocal(sm[:], sm[:]))
                    step(nc.vector.tensor_scalar(pv[:], ex[:, :, 3], 1.0, None, ALU.add))
                    step(nc.vector.reciprocal(pv[:], pv[:]))
                    step(nc.vector.tensor_scalar(mx[:], pv[:], 0.1 - 0.01, 1.0 - 0.1, ALU.mult, ALU.add))
                    step(nc.vector.tensor_tensor(pv[:], pv[:], mx[:], ALU.mult))
                    nc.vector.tensor_copy(wt[:, :, 3], pv[:]).then_inc(wt_ready, 1)
                    step(nc.vector.tensor_scalar(mx[:], pv[:], -1.0, 1.0, ALU.mult, ALU.add))
                    assert base[0] == 11
                    nc.vector.tensor_tensor(sm[:], sm[:], mx[:], ALU.mult).then_inc(wt_ready, 1)
                    dve.wait_ge(wt_ready, b * 3 + 2)
                    nc.vector.tensor_tensor(wt[:, :, 0:3], ex[:, :, 0:3], spread(sm[:], 2, 3), ALU.mult).then_inc(wt_ready, 1)
                    dve.wait_ge(wt_ready, b * 3 + 3)
                return rest

            def mix(b, t):
                dve.wait_ge(f_ps, b * 4 + t + 1)
                if t >= 2:
                    dve.wait_ge(mix_ready, b * 8 + 2 * (t - 2) + 2)
                w2 = wt[:, H * t:H * t + H, 0:2].rearrange("p h k -> p k h")
                nc.vector.tensor_tensor(mixa[t % 2].rearrange("p k (h c) -> p k h c", h=H),
                                        bank(4 + t % 2).rearrange("p (k h c) -> p k h c", k=2, h=H),
                                        spread(w2, 3, DK), ALU.mult).then_inc(mixa_ready, 1)

            def mix_sum(b, t):
                dve.wait_ge(mixa_ready, b * 4 + t + 1)
                dve.wait_ge(mixb_ready, b * 4 + t + 1)
                nc.vector.tensor_tensor(mixa[t % 2], mixa[t % 2], mixb[t % 2], ALU.add).then_inc(mix_ready, 1)
                dve.wait_ge(mix_ready, b * 8 + 2 * t + 1)
                nc.vector.tensor_tensor(o[:, t, :], mixa[t % 2][:, 0, :], mixa[t % 2][:, 1, :], ALU.add).then_inc(mix_ready, 1)

            def join(tail, route, front):
                if tail is not None:
                    rest = softmax_in(tail, [0])
                if route is not None:
                    route_prob(route)
                if front is not None:
                    conv(front, 0)
                    conv(front, 1)
                if tail is not None:
                    rest()
                    mix(tail, 0)
                    mix(tail, 1)
                if front is not None:
                    conv(front, 2)
                    dve.wait_ge(ez_ready, front + 1)
                    nc.vector.tensor_scalar(beta[:], ez[:], 1.0, None, ALU.add).then_inc(beta_ready, 1)
                    dve.wait_ge(beta_ready, 2 * front + 1)
                    nc.vector.reciprocal(beta[:], beta[:]).then_inc(beta_ready, 1)
                if tail is not None:
                    mix_sum(tail, 0)
                    mix_sum(tail, 1)
                if front is not None:
                    conv(front, 3)
                if tail is not None:
                    mix(tail, 2)
                    mix(tail, 3)
                if front is not None:
                    conv(front, 4)
                    conv(front, 5)
                    for t in range(NT):
                        dve.wait_ge(sq_ready, front * 4 + t + 1)
                        nc.vector.reduce_sum(ss[:, 8 * t:8 * t + 8], sq[:].rearrange("p (h c) -> p h c", c=DK),
                                             axis=AX.X).then_inc(ss_ready, 1)
                    dve.wait_ge(ss_ready, front * 5 + 4)
                    nc.vector.tensor_scalar(ss[:], ss[:], 1e-6, None, ALU.add).then_inc(ss_ready, 1)
                if tail is not None:
                    mix_sum(tail, 2)
                    mix_sum(tail, 3)
                if front is not None:
                    dve.wait_ge(rs_ready, front + 1)
                    for t in range(NT):
                        ks = spread(rs[:, 8 * t:8 * t + 4].rearrange("p (k a) -> p k a", k=2), 3, DK)
                        nc.vector.tensor_tensor(k_of(t), bank(t, 0, D).rearrange("p (k a c) -> p k a c", k=2, a=2), ks, ALU.mult).then_inc(kqn_ready, 1)
                        nc.vector.tensor_tensor(by_head(qn[:, t, :]), by_head(bank(t, D, 2 * D)),
                                                spread(rs[:, 8 * t + 4:8 * t + 8], 2, DK), ALU.mult).then_inc(kqn_ready, 1)
                if tail is not None:
                    for t in range(NT):
                        dve.wait_ge(osq_ready, tail * 4 + t + 1)
                        nc.vector.reduce_sum(so[:, H * t:H * t + H], by_head(mixb[t % 2][:, t // 2, :]), axis=AX.X).then_inc(so_ready, 1)
                    dve.wait_ge(so_ready, tail * 5 + 4)
                    nc.vector.tensor_scalar(so[:], so[:], 1.0 / DK, 1e-5, ALU.mult, ALU.add).then_inc(so_ready, 1)
                    dve.wait_ge(ro_ready, tail + 1)
                    for t in range(NT):
                        nc.vector.tensor_tensor(by_head(o[:, t, :]), by_head(o[:, t, :]),
                                                spread(ro[:, H * t:H * t + H], 2, DK), ALU.mult).then_inc(on_ready, 1)
                    for t in range(NT):
                        dve.wait_ge(y_ps, tail * 4 + t + 1)
                        nc.vector.tensor_tensor(rows(tail, t), bank(6 + t % 2, D, 2 * D), rows(tail, t), ALU.add).then_inc(resid_done, 1)
                if front is not None:
                    for t in range(NT):
                        if tail is not None and t == 0:
                            dve.wait_ge(resid_done, tail * NT + NT)
                        dve.wait_ge(AT_ready, front * 4 + t + 1)
                        for k in range(2):
                            ins = nc.vector.tensor_tensor(loc[t][:, 2 * k:2 * k + 2, :],
                                                          bank(2 * (t % 2) + k).rearrange("p (a c) -> p a c", a=2)[:, :, P:2 * P], causal, ALU.mult)
                        ins.then_inc(loc_ready, 1)

            def flush(r):
                dve.wait_ge(resid_done, r * NT + NT)
                route_stats(r)
                route_norm(r)
                route_scores(r)
                route_prob(r)

            norm_in(0)
            join(None, None, 0)
            main(0, None, 1)
            join(0, None, 1)
            main(1, 0, 2)
            with dve.Fori(0, B - 3) as i:
                join(i + 1, i, i + 2)
                main(i + 2, i + 1, i + 3)
            join(B - 2, B - 3, B - 1)
            main(B - 1, B - 2, None)
            join(B - 1, B - 2, None)
            flush(B - 1)

        @block.gpsimd
        def _(pool):
            def norm_in(b):
                pool.wait_ge(mean_ready, b * MERGE + MERGE)
                pool.tensor_tensor(rstd[:], var[:, 0, :], mhalf[:, 0:NT], ALU.pow).then_inc(rstd_ready, 1)

            def main(b, route, norm_next):
                for p2 in range(2):
                    for g in range(2):
                        t = 2 * p2 + g
                        if p2:
                            tt1(b, t)
                if route is not None:
                    pool.wait_ge(g_mean_ready, route * MERGE + MERGE)
                    pool.tensor_tensor(g_rstd[:], g_var[:, 0, :], mhalf[:, 0:NT], ALU.pow).then_inc(g_rstd_ready, 1)
                if norm_next is not None:
                    norm_in(norm_next)

            def tt1(b, t):
                pool.wait_ge(AT_ready, b * 4 + t + 1)
                pool.tensor_tensor(TT[t][:], AT[t], up1, ALU.mult).then_inc(tt1_ready, 1)
                pool.wait_ge(tt1_ready, b * 8 + 2 * t + 1)
                pool.tensor_tensor(TT[t][:], TT[t][:], eye4, ALU.add).then_inc(tt1_ready, 1)

            def mixb_of(b, t):
                pool.wait_ge(o_ready, b * 8 + 8)
                if t >= 2:
                    pool.wait_ge(mix_ready, b * 8 + 2 * (t - 2) + 1)
                pool.tensor_tensor(mixb[t % 2].rearrange("p k (h c) -> p k h c", h=H),
                                   dv[:, t, :, :].rearrange("p k (h c) -> p k h c", h=H),
                                   spread(wt[:, H * t:H * t + H, 2:4].rearrange("p h k -> p k h"), 3, DK),
                                   ALU.mult).then_inc(mixb_ready, 1)

            def join(tail, route, front):
                if tail is not None:
                    pool.wait_ge(wt_ready, tail * 3 + 3)
                    for t in range(NT):
                        mixb_of(tail, t)
                if front is not None:
                    pool.wait_ge(ss_ready, front * 5 + 5)
                    pool.tensor_tensor(rs[:], ss[:], mhalf[:, 0:32], ALU.pow).then_inc(rs_ready, 1)
                    pool.wait_ge(v_ready, front * 2 + 2)
                    for t in range(NT):
                        bt = spread(beta[:, H * t:H * t + H], 2, DK)
                        pool.wait_ge(kqn_ready, front * 8 + 2 * t + 1)
                        pool.tensor_tensor(vk[:, t, 1, :].rearrange("p (k a c) -> p k a c", k=2, a=2), k_of(t),
                                           bt.rearrange("p (k a) c -> p k a c", k=2), ALU.mult).then_inc(vk_ready, 1)
                        pool.tensor_tensor(by_head(vk[:, t, 0, :]), by_head(dv[:, t, 1, :]), bt, ALU.mult).then_inc(vk_ready, 1)
                if tail is not None:
                    pool.wait_ge(so_ready, tail * 5 + 5)
                    pool.tensor_tensor(ro[:], so[:], mhalf[:, 0:NT * H], ALU.pow).then_inc(ro_ready, 1)
                if front is not None:
                    for t in range(2):
                        tt1(front, t)

            def flush(r):
                pool.wait_ge(g_mean_ready, r * MERGE + MERGE)
                pool.tensor_tensor(g_rstd[:], g_var[:, 0, :], mhalf[:, 0:NT], ALU.pow).then_inc(g_rstd_ready, 1)

            norm_in(0)
            join(None, None, 0)
            main(0, None, 1)
            join(0, None, 1)
            main(1, 0, 2)
            with pool.Fori(0, B - 3) as i:
                join(i + 1, i, i + 2)
                main(i + 2, i + 1, i + 3)
            join(B - 2, B - 3, B - 1)
            main(B - 1, B - 2, None)
            join(B - 1, B - 2, None)
            flush(B - 1)

        @block.scalar
        def _(act):
            act.wait_ge(loaded, 16 * NLOAD)
            nc.scalar.activation(rtau[:], rtau[:], ACT.Exp).then_inc(tau_exp, 1)

            def main(b, route, norm_next):
                for p2 in range(2):
                    for g in range(2):
                        act.wait_ge(t1_ps, b * 4 + 2 * p2 + g + 1)
                        nc.scalar.activation(T[g][:], by_head(bank(4 + g)), ACT.Copy).then_inc(t1_ready, 1)
                    for lv in range(1, LEVELS):
                        if lv < LEVELS - 1:
                            for g in range(2):
                                act.wait_ge(t_ps, b * 20 + p2 * 10 + (lv - 1) * 2 + g + 1)
                                nc.scalar.activation(T[g][:], by_head(bank(2 + g)), ACT.Copy).then_inc(t_ready, 1)
                        for g in range(2):
                            act.wait_ge(tt_ps, b * 24 + p2 * 12 + (lv - 1) * 2 + g + 1)
                            nc.scalar.activation(TT[2 * p2 + g][:], by_head(bank(4 + g)), ACT.Copy).then_inc(tt_ready, 1)
                for t in range(NT):
                    uw = by_head(bank(6 + t % 2))
                    act.wait_ge(uw_ps, b * 4 + t + 1)
                    if t >= 2:
                        act.wait_ge(wT_ps, b * 4 + t - 1)
                    nc.scalar.activation(by_head(w_tok[t % 2][:]), uw[:, :, DK:2 * DK], ACT.Copy, scale=-1.0).then_inc(uw_ready, 1)
                    nc.scalar.activation(by_head(uadj[:, t, :]), uw[:, :, 0:DK], ACT.Copy).then_inc(uw_ready, 1)
                    if t % 2:
                        for s in (t - 1, t):
                            act.wait_ge(wT_ps, b * 4 + s + 1)
                            nc.scalar.activation(nwT[s][:].rearrange("p a c -> p (a c)"), bank(4 + s % 2, 0, D), ACT.Copy).then_inc(wT_ready, 1)
                for t in range(NT):
                    act.wait_ge(o_ps, b * 4 + t + 1)
                    nc.scalar.activation(dT[:, :, t * P:(t + 1) * P], bank(5, 0, D).rearrange("p (a c) -> p a c", a=DB), ACT.Copy).then_inc(o_ready, 1)
                    if route is not None and t >= 2:
                        c = t - 2
                        act.wait_ge(rT_ps, route * 2 + c + 1)
                        nc.scalar.activation(rT[c], bank(7), ACT.Copy).then_inc(rT_ready, 1)
                for j in range(2):
                    act.wait_ge(d_ps, b * 2 + j + 1)
                    for k in range(2):
                        nc.scalar.activation(dv[:, 2 * j + k, 0, :], bank(4 + j, k * D, (k + 1) * D), ACT.Copy).then_inc(o_ready, 1)
                for m in range(4):
                    act.wait_ge(hid_ps, b * 4 + m + 1)
                    nc.scalar.activation(hidT[:, m, :], bank(m), ACT.Gelu, bias=b_f1[:, m:m + 1]).then_inc(hid_ready, 1)

            def join(tail, route, front):
                if front is not None:
                    for c in range(DB):
                        act.wait_ge(xT_ps, front * 2 + c + 1)
                        nc.scalar.activation(xT[:, c, :], bank(c), ACT.Copy).then_inc(xT_ready, 1)
                if route is not None:
                    act.wait_ge(sc_ready, route * 3 + 3)
                    nc.scalar.activation(g_ex[:], sc[:], ACT.Exp).then_inc(g_ex_ready, 1)
                if tail is not None:
                    act.wait_ge(ml_ready, tail * 11 + 4)
                    nc.scalar.activation(ex[:, :, 0:3], lg[:, :, 0:3], ACT.Exp).then_inc(ex_ready, 1)
                    nc.scalar.activation(ex[:, :, 3], lg[:, :, 3], ACT.Exp, scale=-1.0).then_inc(ex_ready, 1)
                if front is not None:
                    act.wait_ge(z_ps, front + 1)
                    nc.scalar.activation(ez[:].rearrange("p (t h) -> p t h", t=NT), bank(3).rearrange("p (t h) -> p t h", t=NT)[:, :, 0:H],
                                         ACT.Exp, scale=-1.0).then_inc(ez_ready, 1)
                    for m in range(7):
                        if m < 6:
                            act.wait_ge(proj_ps, front * 6 + m + 1)
                            nc.scalar.activation(qkv[:, m, :], bank(m % 3), ACT.Copy, scale=conv_w[:, m, 3:4]).then_inc(tap3_done, 1)
                        if m >= 1:
                            act.wait_ge(conv_done, front * 18 + 3 * m)
                            nc.scalar.activation(qkv[:, m - 1, :], qkv[:, m - 1, :], ACT.Silu).then_inc(silu_done, 1)
                    for t in range(NT):
                        act.wait_ge(kq_ps, front * 4 + t + 1)
                        act.wait_ge(ss_ready, front * 5 + t)
                        nc.scalar.activation(sq[:], bank(t), ACT.Square).then_inc(sq_ready, 1)
                    if tail is not None:
                        act.wait_ge(mixb_ready, tail * 4 + 4)
                    for j in range(2):
                        act.wait_ge(v_ps, front * 2 + j + 1)
                        nc.scalar.activation(dv[:, 2 * j:2 * j + 2, 1, :], bank(4 + j).rearrange("p (t c) -> p t c", t=2), ACT.Copy).then_inc(v_ready, 1)
                if tail is not None:
                    for t in range(NT):
                        act.wait_ge(mix_ready, tail * 8 + 8)
                        nc.scalar.activation(mixb[t % 2][:, t // 2, :], o[:, t, :], ACT.Square).then_inc(osq_ready, 1)
                    for t in range(NT):
                        act.wait_ge(oT_ps, tail * 4 + t + 1)
                        if t >= 2:
                            act.wait_ge(y_ps, tail * 4 + t - 1)
                        nc.scalar.activation(oT[t % 2][:].rearrange("p a c -> p (a c)"), bank(6 + t % 2, 0, D), ACT.Copy).then_inc(oT_ready, 1)
                if front is not None:
                    for t in range(NT):
                        for hb in range(DB):
                            act.wait_ge(kT_ps, front * 8 + 2 * t + hb + 1)
                            nc.scalar.activation(kT[t][hb][:].rearrange("p a c -> p (a c)"), bank(6 + hb), ACT.Copy).then_inc(kT_ready, 1)
                        act.wait_ge(al_ps, front * 4 + t + 1)
                        for k in range(2):
                            ins = nc.scalar.activation(AT[t][:, 2 * k:2 * k + 2, :], bank(2 * (t % 2) + k).rearrange("p (a c) -> p a c", a=2)[:, :, 0:P], ACT.Copy)
                        ins.then_inc(AT_ready, 1)

            def flush(r):
                for c in range(DB):
                    act.wait_ge(rT_ps, r * 2 + c + 1)
                    nc.scalar.activation(rT[c], bank(7), ACT.Copy).then_inc(rT_ready, 1)
                act.wait_ge(sc_ready, r * 3 + 3)
                nc.scalar.activation(g_ex[:], sc[:], ACT.Exp).then_inc(g_ex_ready, 1)

            join(None, None, 0)
            main(0, None, 1)
            join(0, None, 1)
            main(1, 0, 2)
            with act.Fori(0, B - 3) as i:
                join(i + 1, i, i + 2)
                main(i + 2, i + 1, i + 3)
            join(B - 2, B - 3, B - 1)
            main(B - 1, B - 2, None)
            join(B - 1, B - 2, None)
            flush(B - 1)

        @block.tensor
        def _(pe):
            mm = nc.tensor.matmul
            pe.wait_ge(loaded, 16 * NLOAD)
            for c in range(DB):
                ins = nc.tensor.transpose(bank(3, c * E, (c + 1) * E), w_rows[:, c * P:(c + 1) * P], const[0:E, C_EYE:C_EYE + E])
            ins.then_inc(route_ps, 1)
            pe.wait_ge(prepared, 4)

            def x_of(b, p2, lv, g):
                t = 2 * p2 + g
                if lv == 1:
                    pe.wait_ge(t1_ready, b * 4 + t + 1)
                else:
                    pe.wait_ge(t_ready, b * 20 + p2 * 10 + (lv - 2) * 2 + g + 1)
                for h in range(H):
                    ins = mm(bank(g, h * P, (h + 1) * P), AT[t][:, h, :], T[g][:, h, :], start=True, stop=True)
                ins.then_inc(x_ps, 1)

            def inverse(b, p2):
                for g in range(2):
                    t = 2 * p2 + g
                    pe.wait_ge(tt1_ready, b * 8 + 2 * t + 2)
                    if p2:
                        pe.wait_ge(tt_ready, b * 24 + 10 + g + 1)
                    for h in range(H):
                        ins = nc.tensor.transpose(bank(4 + g, h * P, (h + 1) * P), TT[t][:, h, :], eye)
                    ins.then_inc(t1_ps, 1)
                if p2 == 0:
                    pe.wait_ge(loc_ready, b * 4 + 4)
                for g in range(2):
                    x_of(b, p2, 1, g)
                for lv in range(1, LEVELS):
                    last = lv == LEVELS - 1
                    for g in range(2):
                        t = 2 * p2 + g
                        if lv == 1:
                            mm(bank(2 + g), eye, T[g][:].rearrange("p h c -> p (h c)"), start=True, stop=False, skip_group_check=True)
                        if lv > 1:
                            pe.wait_ge(tt_ready, b * 24 + p2 * 12 + (lv - 2) * 2 + g + 1)
                        if last:
                            mm(bank(4 + g), eye, TT[t][:].rearrange("p h c -> p (h c)"), start=True, stop=False, skip_group_check=True)
                        pe.wait_ge(x_ready, b * 24 + p2 * 12 + (lv - 1) * 2 + g + 1)
                        for h in range(H):
                            if last:
                                ins = mm(bank(4 + g, h * P, (h + 1) * P), X[g][:, h, :], TT[t][:, h, :],
                                         start=False, stop=h == H - 1, skip_group_check=True)
                            else:
                                ins = mm(bank(2 + g, h * P, (h + 1) * P), TT[t][:, h, :], X[g][:, h, :],
                                         start=False, stop=lv == LEVELS - 2 and h == H - 1, skip_group_check=True)
                        ins.then_inc(tt_ps if last else t_ps, 1)
                    if not last:
                        for g in range(2):
                            pe.wait_ge(t_ready, b * 20 + p2 * 10 + (lv - 1) * 2 + g + 1)
                            for h in range(H):
                                ins = nc.tensor.transpose(bank(4 + g, h * P, (h + 1) * P), T[g][:, h, :], eye)
                            ins.then_inc(tt_ps, 1)
                            x_of(b, p2, lv + 1, g)

            def u_w(b, t):
                pe.wait_ge(tt_ready, b * 24 + (t // 2) * 12 + 10 + t % 2 + 1)
                pe.wait_ge(uw_ready, b * 8 + (2 * (t - 1) if t >= 2 else 0))
                for h in range(H):
                    ins = mm(bank(6 + t % 2, h * P, (h + 1) * P), TT[t][:, h, :], vk[:, t, :, h * DK:(h + 1) * DK], start=True, stop=True)
                ins.then_inc(uw_ps, 1)

            def w_T(b, t):
                pe.wait_ge(uw_ready, b * 8 + 2 * t + 1)
                if t >= 2:
                    pe.wait_ge(wT_ready, b * 4 + t - 1)
                for hb in range(DB):
                    ins = nc.tensor.transpose(bank(4 + t % 2, hb * P, (hb + 1) * P), w_tok[t % 2][:, hb * P:(hb + 1) * P], eye)
                ins.then_inc(wT_ps, 1)

            gate_in = [xT[:, 0, :], xT[:, 1, :], firT[:, 0, 0, :], firT[:, 0, 1, :], firT[:, 1, 0, :], firT[:, 1, 1, :],
                       dT[:, 0, :], dT[:, 1, :]]

            def hidden(m, lo, hi):
                for c in range(lo, hi):
                    ins = mm(bank(m), w_f1[:, c, m * P:(m + 1) * P], gate_in[c], start=c == 0, stop=c == 7)
                return ins

            def route_T(r, c):
                pe.wait_ge(g_xn_ready, r * 4 + 4)
                if c:
                    pe.wait_ge(rT_ready, r * 2 + c)
                for t in range(NT):
                    ins = nc.tensor.transpose(bank(7, t * P, (t + 1) * P), xn[:, t, c * P:(c + 1) * P], eye)
                ins.then_inc(rT_ps, 1)

            def route_scores(r):
                pe.wait_ge(rT_ready, r * 2 + 2)
                for t in range(NT):
                    for c in range(DB):
                        ins = mm(bank(7, t * P, (t + 1) * P), rT[c][:, t * P:(t + 1) * P], w_route[:, c, :], start=c == 0, stop=c == DB - 1)
                ins.then_inc(sc_ps, 1)

            def scan_ws(b, t):
                pe.wait_ge(s_ready, b * 3 + t)
                pe.wait_ge(wT_ready, b * 4 + 4)
                if t >= 2:
                    pe.wait_ge(u_ready, b * 3 + t - 1)
                for hb in range(DB):
                    ins = mm(bank(4, hb * P, (hb + 1) * P), nwT[t][:, hb, :], S[:, hb, :], start=True, stop=True)
                ins.then_inc(ws_ps, 1)

            def scan_out(b, t):
                if t:
                    pe.wait_ge(o_ready, b * 8 + t)
                    pe.wait_ge(u_ready, b * 3 + t)
                else:
                    pe.wait_ge(wT_ready, b * 4 + 4)
                    pe.wait_ge(uw_ready, b * 8 + 8)
                for hb in range(DB):
                    if t:
                        mm(bank(5, hb * P, (hb + 1) * P), S[:, hb, :], kT[t][hb][:, 3, :], start=True, stop=False, skip_group_check=True)
                    for a in range(2):
                        h = 2 * hb + a
                        ins = mm(ps[64 * a:64 * a + 64, 5, hb * P:(hb + 1) * P], uadj[:, t, h * DK:(h + 1) * DK], loc[t][:, h, :],
                                 start=t == 0, stop=True, skip_group_check=True)
                ins.then_inc(o_ps, 1)
                if t < NT - 1:
                    for hb in range(DB):
                        for a in range(2):
                            ins = mm(bank(6, hb * P, (hb + 1) * P), kz[:, t, (2 * hb + a) * P:(2 * hb + a + 1) * P], uadj[:, t, hb * P:(hb + 1) * P],
                                     start=t == 0 and hb == 0 and a == 0, stop=t == NT - 2 and hb == DB - 1 and a == 1, skip_group_check=True)
                    ins.then_inc(s_ps, 1)

            def main(b, route, norm_next):
                inverse(b, 0)
                inverse(b, 1)
                u_w(b, 0)
                u_w(b, 1)
                pe.wait_ge(fir_step, b * NFIR + NFIR)
                hidden(0, 0, 6)
                w_T(b, 0)
                w_T(b, 1)
                u_w(b, 2)
                u_w(b, 3)
                hidden(1, 0, 6)
                w_T(b, 2)
                w_T(b, 3)
                pe.wait_ge(t_ready, b * 20 + 20)
                hidden(2, 0, 2)
                scan_out(b, 0)
                hidden(2, 2, 4)
                scan_ws(b, 1)
                hidden(2, 4, 6)
                scan_out(b, 1)
                hidden(3, 0, 2)
                scan_ws(b, 2)
                hidden(3, 2, 4)
                scan_out(b, 2)
                if route is not None:
                    route_T(route, 0)
                hidden(3, 4, 5)
                scan_ws(b, 3)
                hidden(3, 5, 6)
                if route is not None:
                    route_T(route, 1)
                scan_out(b, 3)
                pe.wait_ge(o_ready, b * 8 + 4)
                for m in range(4):
                    hidden(m, 6, 8).then_inc(hid_ps, 1)
                for j in range(2):
                    for k in range(2):
                        t = 2 * j + k
                        for hb in range(DB):
                            ins = nc.tensor.transpose(bank(4 + j, k * D + hb * P, k * D + (hb + 1) * P), dT[:, hb, t * P:(t + 1) * P], eye)
                    ins.then_inc(d_ps, 1)
                if route is not None:
                    route_scores(route)
                pe.wait_ge(s_ready, b * 3 + 3)
                for t in range(NT):
                    for c in range(4):
                        if t == 0:
                            pe.wait_ge(hid_ready, b * 4 + c + 1)
                        ins = mm(bank(6, t * P, (t + 1) * P), hidT[:, c, t * P:(t + 1) * P], w_f2[:, c, :], start=c == 0, stop=c == 3)
                ins.then_inc(lg_ps, 1)

            def f_of(b, t):
                if t < 2:
                    pe.wait_ge(o_ready, b * 8 + 8)
                else:
                    pe.wait_ge(mixa_ready, b * 4 + t - 1)
                for kind in range(2):
                    for c in range(DB):
                        ins = nc.tensor.transpose(bank(4 + t % 2, (2 * kind + c) * P, (2 * kind + c + 1) * P), firT[:, kind, c, t * P:(t + 1) * P], eye)
                ins.then_inc(f_ps, 1)

            def project(b, m):
                if m >= 3:
                    pe.wait_ge(conv_done, b * 18 + 3 * (m - 2))
                else:
                    pe.wait_ge(xT_ready, b * 2 + 2)
                for c in range(DB):
                    ins = mm(bank(m % 3), w_qkv[:, c, m * P:(m + 1) * P], xT[:, c, :], start=c == 0, stop=c == DB - 1)
                ins.then_inc(proj_ps, 1)

            def join(tail, route, front):
                if front is not None:
                    pe.wait_ge(xn_ready, front * 4 + 4)
                    for c in range(DB):
                        for t in range(NT):
                            ins = nc.tensor.transpose(bank(c, t * P, (t + 1) * P), xn[:, t, c * P:(c + 1) * P], eye)
                        ins.then_inc(xT_ps, 1)
                if tail is not None:
                    f_of(tail, 0)
                    f_of(tail, 1)
                if front is not None:
                    pe.wait_ge(xT_ready, front * 2 + 2)
                    for t in range(NT):
                        for c in range(DB):
                            ins = mm(bank(3, t * P, (t + 1) * P), xT[:, c, t * P:(t + 1) * P], w_beta[:, c, :], start=c == 0, stop=c == DB - 1)
                    ins.then_inc(z_ps, 1)
                    for m in range(3):
                        project(front, m)
                if front is not None:
                    for m in range(3, 5):
                        project(front, m)
                if tail is not None:
                    f_of(tail, 2)
                    f_of(tail, 3)
                if front is not None:
                    project(front, 5)
                    pe.wait_ge(silu_done, front * 6 + 4)
                    pe.wait_ge(ez_ready, front + 1)
                    pe.wait_ge(conv_done, front * 18 + 18)
                    for t in range(NT):
                        for c in range(4):
                            ins = nc.tensor.transpose(bank(t, c * P, (c + 1) * P), qkv[:, (c + 2) % 4, t * P:(t + 1) * P], eye)
                        ins.then_inc(kq_ps, 1)
                    if tail is not None:
                        pe.wait_ge(mixa_ready, tail * 4 + 4)
                    pe.wait_ge(silu_done, front * 6 + 6)
                    for t in range(NT):
                        for c in range(2):
                            ins = nc.tensor.transpose(bank(4 + t // 2, (t % 2) * D + c * P, (t % 2) * D + (c + 1) * P),
                                                      qkv[:, 4 + c, t * P:(t + 1) * P], eye)
                        if t % 2:
                            ins.then_inc(v_ps, 1)
                if tail is not None:
                    pe.wait_ge(ml_ready, tail * 11 + 1)
                    if route is not None:
                        pe.wait_ge(sc_ready, route * 3 + 1)
                    for t in range(NT + 1):
                        if t < NT:
                            pe.wait_ge(on_ready, tail * 4 + t + 1)
                            if t >= 2:
                                pe.wait_ge(resid_done, tail * 4 + t - 1)
                            for c in range(DB):
                                ins = nc.tensor.transpose(bank(6 + t % 2, c * P, (c + 1) * P), o[:, t, c * P:(c + 1) * P], eye)
                            ins.then_inc(oT_ps, 1)
                        if t >= 1:
                            s = t - 1
                            pe.wait_ge(oT_ready, tail * 4 + s + 1)
                            for c in range(DB):
                                ins = mm(bank(6 + s % 2, D, 2 * D), oT[s % 2][:, c, :], w_o[:, c, :], start=c == 0, stop=c == 1)
                            ins.then_inc(y_ps, 1)
                if front is not None:
                    if tail is not None:
                        pe.wait_ge(resid_done, tail * 4 + 4)
                    for t in range(NT):
                        pe.wait_ge(vk_ready, front * 8 + 2 * t + 1)
                        pe.wait_ge(kqn_ready, front * 8 + 8)
                        if t:
                            pe.wait_ge(kT_ready, front * 8 + 2 * t)
                        for hb in range(DB):
                            for n, src in enumerate((kz[:, t, hb * 2 * P:hb * 2 * P + P], kz[:, t, hb * 2 * P + P:(hb + 1) * 2 * P],
                                                     vk[:, t, 1, hb * P:(hb + 1) * P], qn[:, t, hb * P:(hb + 1) * P])):
                                ins = nc.tensor.transpose(bank(6 + hb, n * P, (n + 1) * P), src, eye)
                            ins.then_inc(kT_ps, 1)
                        pe.wait_ge(kT_ready, front * 8 + 2 * t + 2)
                        if t >= 2:
                            pe.wait_ge(loc_ready, front * 4 + t - 1)
                        for h in range(H):
                            k4 = kT[t][h // 2]
                            ins = mm(bank(2 * (t % 2) + h // 2, (h % 2) * 2 * P, (h % 2 + 1) * 2 * P),
                                     k4[:, h % 2, :], k4[:, 2:4, :], start=True, stop=True)
                        ins.then_inc(al_ps, 1)

            def flush(r):
                route_T(r, 0)
                route_T(r, 1)
                route_scores(r)

            join(None, None, 0)
            main(0, None, 1)
            join(0, None, 1)
            main(1, 0, 2)
            with pe.Fori(0, B - 3) as i:
                join(i + 1, i, i + 2)
                main(i + 2, i + 1, i + 3)
            join(B - 2, B - 3, B - 1)
            main(B - 1, B - 2, None)
            join(B - 1, B - 2, None)
            flush(B - 1)


def choose_tokens(nc, const, ps, prob, idxT, gT, idx_dram):
    R = B * E
    with ExitStack() as ctx:
        mk = Maker(nc, ctx, "ch_")
        sb, sem = mk.sb, mk.sem
        work = sb("work", [R, L])
        vals = sb("vals", [R, CAP])
        idx = sb("idx", [R, CAP], U32)
        idxf = sb("idxf", [R, CAP])
        rows_ps, found, moved, idx_out, back_ps = (sem(n) for n in ("rows_ps", "found", "moved", "idx_out", "back_ps"))
        block = ctx.enter_context(nc.Block())

        @block.vector
        def _(dve):
            n = [0]

            def chain(ins):
                n[0] += 1
                ins.then_inc(found, 1)
                dve.wait_ge(found, n[0])

            dve.wait_ge(rows_ps, 1)
            chain(nc.vector.tensor_copy(work[:], ps[0:R, 0, :]))
            for r in range(CAP // 8):
                v = vals[:, 8 * r:8 * r + 8]
                chain(nc.vector.max(v, work[:]))
                chain(nc.vector.max_index(idx[:, 8 * r:8 * r + 8], v, work[:]))
                chain(nc.vector.match_replace(work[:], v, work[:], -1.0))
            nc.vector.tensor_copy(idxf[:], idx[:]).then_inc(moved, 1)
            dve.wait_ge(back_ps, 1)
            nc.vector.tensor_copy(idxT[:], ps[:, 1, 0:R]).then_inc(moved, 1)
            nc.vector.tensor_copy(gT[:], ps[:, 1, P:P + R]).then_inc(moved, 1)

        @block.sync
        def _(sp):
            sp.wait_ge(moved, 1)
            sp.dma_start(idx_dram, idxf[:]).then_inc(idx_out, 16)
            sp.wait_ge(idx_out, 16)

        @block.tensor
        def _(pe):
            for t in range(NT):
                ins = nc.tensor.transpose(ps[0:R, 0, t * P:(t + 1) * P], prob[:, t, :], const[:, C_EYE:C_EYE + P])
            ins.then_inc(rows_ps, 1)
            pe.wait_ge(moved, 1)
            nc.tensor.transpose(ps[:, 1, 0:R], idxf[:], const[0:R, C_EYE:C_EYE + R])
            nc.tensor.transpose(ps[:, 1, P:P + R], vals[:], const[0:R, C_EYE:C_EYE + R]).then_inc(back_ps, 1)


def gather_tokens(nc, const, resid, ps, mean_all, rstd_all, idx_dram, slots):
    with ExitStack() as ctx:
        mk = Maker(nc, ctx, "ga_")
        sb, sem = mk.sb, mk.sem
        idxb = [sb(f"idxb{j}", [P, E * CAP]) for j in range(2)]
        xn = [[sb(f"xn{j}{t}", [P, D]) for t in range(NT)] for j in range(2)]
        pick = [sb(f"pick{j}", [P, NT, E * CAP]) for j in range(2)]
        st = [[sb(f"m{j}", [P, NT]), sb(f"r{j}", [P, NT])] for j in range(2)]
        idx_in, stat_ready, in_ready, out_ps, out_ready = ([sem(f"{n}{j}") for j in range(2)] for n in ("idx_in", "stat_ready", "in_ready", "out_ps", "out_ready"))
        rows = idx_dram.rearrange("(n e) s -> n (e s)", e=E)
        block = ctx.enter_context(nc.Block())

        @block.sync
        def _(sp):
            with sp.Fori(0, B // 2) as i:
                for j in range(2):
                    sp.wait_ge(in_ready[j], i * 2 * NT)
                    sp.dma_start(idxb[j][:], rows[bass.ds(2 * i + j, 1), :].broadcast_to([P, E * CAP])).then_inc(idx_in[j], 16)

        @block.vector
        def _(dve):
            with dve.Fori(0, B // 2) as i:
                for j in range(2):
                    nc.vector.tensor_copy(st[j][0][:], mean_all[:, bass.ds((2 * i + j) * NT, NT)]).then_inc(stat_ready[j], 1)
                    nc.vector.tensor_copy(st[j][1][:], rstd_all[:, bass.ds((2 * i + j) * NT, NT)]).then_inc(stat_ready[j], 1)
                    dve.wait_ge(stat_ready[j], i * 2 + 2)
                    dve.wait_ge(out_ps[j], i * 4)
                    dve.wait_ge(idx_in[j], i * 16 + 16)
                    for t in range(NT):
                        nc.vector.tensor_scalar(xn[j][t][:], resid[:, bass.ds((2 * i + j) * NT + t, 1), :].rearrange("p a d -> p (a d)"),
                                                st[j][0][:, t:t + 1], st[j][1][:, t:t + 1], ALU.subtract, ALU.mult).then_inc(in_ready[j], 1)
                        nc.vector.tensor_scalar(pick[j][:, t, :], idxb[j][:], const[:, C_TOKID + t:C_TOKID + t + 1], None,
                                                ALU.is_equal).then_inc(in_ready[j], 1)

        @block.scalar
        def _(act):
            with act.Fori(0, B // 2) as i:
                for j in range(2):
                    for half in range(2):
                        for c in range(DB):
                            act.wait_ge(out_ps[j], i * 4 + 2 * half + c + 1)
                            dst = slots[:, 4 * half:4 * half + 4, bass.ds(c * B * CAP + (2 * i + j) * CAP, CAP)]
                            nc.scalar.activation(dst, ps[:, 4 * j + 2 * half + c, :].rearrange("p (e s) -> p e s", e=4),
                                                 ACT.Copy).then_inc(out_ready[j], 1)

        @block.tensor
        def _(pe):
            with pe.Fori(0, B // 2) as i:
                for j in range(2):
                    pe.wait_ge(out_ready[j], i * 4)
                    pe.wait_ge(in_ready[j], i * 2 * NT + 2 * NT)
                    for half in range(2):
                        for c in range(DB):
                            for t in range(NT):
                                ins = nc.tensor.matmul(ps[:, 4 * j + 2 * half + c, :], xn[j][t][:, c * P:(c + 1) * P],
                                                       pick[j][:, t, half * 512:(half + 1) * 512], start=t == 0, stop=t == NT - 1)
                            ins.then_inc(out_ps[j], 1)


def experts(nc, A, ps, slots):
    FB = F0 // P
    with ExitStack() as ctx:
        mk = Maker(nc, ctx, "ex_")
        sb, sem = mk.sb, mk.sem
        w1 = [sb(f"w1_{j}", [P, DB, F0]) for j in range(2)]
        w2 = [sb(f"w2_{j}", [P, FB, D]) for j in range(2)]
        hT = [sb(f"hT{half}", [P, FB, 512]) for half in range(2)]
        w_in, dn_ps = ([sem(f"{n}{j}") for j in range(2)] for n in ("w_in", "dn_ps"))
        up_ps, up_ready, dn_ready = sem("up_ps"), sem("up_ready"), sem("dn_ready")
        w1_dram = A["L0_ffn_w1"].rearrange("e (c p) f -> p e c f", p=P)
        w2_dram = A["L0_ffn_w2"].rearrange("e (c p) d -> p e c d", p=P)
        block = ctx.enter_context(nc.Block())

        @block.sync
        def _(sp):
            with sp.Fori(0, E // 2) as i:
                for j in range(2):
                    sp.wait_ge(dn_ps[j], i * B)
                    e = bass.ds(2 * i + j, 1)
                    sp.dma_start(w1[j][:], w1_dram[:, e, :, :].rearrange("p a c f -> p (a c) f")).then_inc(w_in[j], 16)
                    sp.dma_start(w2[j][:], w2_dram[:, e, :, :].rearrange("p a c f -> p (a c) f")).then_inc(w_in[j], 16)

        @block.tensor
        def _(pe):
            with pe.Fori(0, E // 2) as i:
                for j in range(2):
                    up, dn = i * 4 * FB + j * 2 * FB, i * 2 * B + j * B
                    pe.wait_ge(w_in[j], i * 32 + 32)
                    for half in range(2):
                        for f in range(FB):
                            n = half * FB + f
                            if n >= 4:
                                pe.wait_ge(up_ready, up + n - 3)
                            for c in range(DB):
                                ins = nc.tensor.matmul(ps[:, n % 4, :], w1[j][:, c, f * P:(f + 1) * P],
                                                       slots[:, bass.ds(2 * i + j, 1), c * B * CAP + half * 512:c * B * CAP + half * 512 + 512].rearrange("p a s -> p (a s)"),
                                                       start=c == 0, stop=c == DB - 1)
                            ins.then_inc(up_ps, 1)
                    for n in range(B):
                        half = n // 4
                        if n % 4 == 0:
                            pe.wait_ge(up_ready, up + (half + 1) * FB)
                        if n >= 4:
                            pe.wait_ge(dn_ready, dn + n - 3)
                        else:
                            pe.wait_ge(dn_ready, dn)
                        for f in range(FB):
                            ins = nc.tensor.matmul(ps[:, 4 + n % 4, 0:D], hT[half][:, f, (n % 4) * CAP:(n % 4 + 1) * CAP], w2[j][:, f, :],
                                                   start=f == 0, stop=f == FB - 1)
                        ins.then_inc(dn_ps[j], 1)

        @block.scalar
        def _(act):
            with act.Fori(0, E // 2) as i:
                for j in range(2):
                    up, dn = i * 4 * FB + j * 2 * FB, i * 2 * B + j * B
                    for half in range(2):
                        act.wait_ge(dn_ps[1 - j], (i + j) * B)
                        for f in range(FB):
                            n = half * FB + f
                            act.wait_ge(up_ps, up + n + 1)
                            nc.scalar.activation(hT[half][:, f, :], ps[:, n % 4, :], ACT.Gelu).then_inc(up_ready, 1)

        @block.vector
        def _(dve):
            with dve.Fori(0, E // 2) as i:
                for j in range(2):
                    up, dn = i * 4 * FB + j * 2 * FB, i * 2 * B + j * B
                    for n in range(B):
                        dve.wait_ge(dn_ps[j], i * B + n + 1)
                        nc.vector.tensor_copy(slots[:, bass.ds(2 * i + j, 1), n * D:(n + 1) * D].rearrange("p a d -> p (a d)"),
                                              ps[:, 4 + n % 4, 0:D]).then_inc(dn_ready, 1)


def layer1(nc, A, const, resid, ps, slots, idxT, gT, out):
    HB = F1 // P
    NB = P + 8
    with ExitStack() as ctx:
        mk = Maker(nc, ctx, "l1_")
        sb, sem = mk.sb, mk.sem
        eye = const[:, C_EYE:C_EYE + P]
        mhalf = const[:, C_MHALF:C_MHALF + NT]
        one_row = const[0:1, C_ONE:C_ONE + P]
        one_col = const[:, C_ONE:C_ONE + 1]
        heads = const[:, C_HEADS:C_HEADS + NB]
        wqkv = sb("wqkv", [P, DB, 3 * D])
        qnw = sb("qnw", [P, DB])
        knw = sb("knw", [P, D])
        wout = sb("wout", [P, DB, D])
        bout = sb("bout", [1, D])
        wg, wu = sb("wg", [P, DB, F1]), sb("wu", [P, DB, F1])
        wd = sb("wd", [P, HB, D])
        idxn, gn = sb("idxn", [P, E]), sb("gn", [P, E])
        put = sb("put", [P, E, L])
        xw = sb("xw", [P, NT, D])
        stats = sb("stats", [P, NT, 6])
        mean, var, rstd = sb("mean", [P, NT]), sb("var", [P, 3, NT]), sb("rstd", [P, NT])
        xn = sb("xn", [P, NT, D])
        xT = sb("xT", [P, DB, L])
        qT = sb("qT", [P, DB, L])
        sqq = xn[:].rearrange("p t d -> p (t d)").rearrange("p (c l) -> p c l", c=DB)
        sqk = sb("sqk", [P, D])
        ssk, ssq = sb("ssk", [P, NT]), sb("ssq", [P, NT])
        rk, rq = sb("rk", [P, NT]), sb("rq", [P, NT])
        k2 = sb("k2", [P, NT, D])
        vx = sb("vx", [P, NT, DB, NB])
        kvm = sb("kvm", [P, DB, NB])
        nrm = sb("nrm", [P, 2, DB, 8])
        o = sb("o", [P, 2, D])
        oT = [sb(f"oT{t}", [P, DB, P]) for t in range(2)]
        gs = sb("gs", [P, 2, 512])
        hT = sb("hT", [P, HB, L])
        yo = sb("yo", [P, 2, NT, D])
        raw = put[:].rearrange("p e l -> p (e l)")[:, 0:HB * D].bitcast(I32)
        rawf = hT[:].rearrange("p m l -> p (m l)")[:, 0:HB * D]

        loaded, raw_in, raw_ready, raw_ps, raw_done, ones_set = (
            sem(n) for n in ("loaded", "raw_in", "raw_ready", "raw_ps", "raw_done", "ones_set"))
        small, put_ready, add_ps, xw_ready = sem("small"), sem("put_ready"), sem("add_ps"), sem("xw_ready")
        stat_done, mean_ready, rstd_ready, xn_ready, xT_ps, xT_ready = (
            sem(n) for n in ("stat_done", "mean_ready", "rstd_ready", "xn_ready", "xT_ps", "xT_ready"))
        kv_ps, v_ready, ssk_ready, rk_ready, kk_ready, k2_ready = (
            sem(n) for n in ("kv_ps", "v_ready", "ssk_ready", "rk_ready", "kk_ready", "k2_ready"))
        q_ps, q_ready, ssq_ps, ssq_ready, rq_ready, kvm_ps, kvm_ready = (
            sem(n) for n in ("q_ps", "q_ready", "ssq_ps", "ssq_ready", "rq_ready", "kvm_ps", "kvm_ready"))
        att_ps, nrm_step, o_ready, oT_ps, oT_ready, wo_ps = (
            sem(n) for n in ("att_ps", "nrm_step", "o_ready", "oT_ps", "oT_ready", "wo_ps"))
        g_ps, g_ready, u_ps, h_ready, y_ps, y_ready = (
            sem(n) for n in ("g_ps", "g_ready", "u_ps", "h_ready", "y_ps", "y_ready"))
        stored = [sem(f"stored{j}") for j in range(2)]
        mm = nc.tensor.matmul
        block = ctx.enter_context(nc.Block())

        def bank(n, lo=0, hi=512):
            return ps[:, n, lo:hi]

        out_v = out.rearrange("b (t p) d -> p b t d", p=P)
        ints = [("L1_ffn_w_gate", HB, D), ("L1_ffn_w_up", HB, D), ("L1_ffn_w_down", DB, F1)]

        @block.sync
        def _(sp):
            with nc.allow_non_contiguous_dma(reason="small parameters"):
                sp.dma_start(wqkv[:], A["L1_attn_W_qkv"].rearrange("(c p) n -> p c n", p=P)).then_inc(loaded, 16)
                sp.dma_start(qnw[:], A["L1_attn_qn_w"].rearrange("(c p) -> p c", p=P)).then_inc(loaded, 16)
                sp.dma_start(knw[:], A["L1_attn_kn_w"].unsqueeze(0).broadcast_to([P, D])).then_inc(loaded, 16)
                sp.dma_start(wout[:], A["L1_attn_W_out"].rearrange("(c p) n -> p c n", p=P)).then_inc(loaded, 16)
                sp.dma_start(bout[:], A["L1_attn_b_out"].unsqueeze(0)).then_inc(loaded, 16)
            for n, (name, rb, cols) in enumerate(ints):
                if n:
                    sp.wait_ge(raw_ready, n)
                sp.dma_start(raw.rearrange("p (r c) -> p r c", r=rb), A[name].rearrange("(r p) c -> p r c", p=P)).then_inc(raw_in, 16)
            with sp.Fori(0, B // 2) as i:
                for j in range(2):
                    sp.wait_ge(y_ready, i * 2 * NT + (j + 1) * NT)
                    sp.dma_start(out_v[:, bass.ds(2 * i + j, 1), :, :].rearrange("p a t d -> p (a t) d"), yo[:, j, :, :]).then_inc(stored[j], 16)
            for j in range(2):
                sp.wait_ge(stored[j], 16 * (B // 2))

        def norm(dve, base, half):
            for t in range(NT):
                nc.vector.bn_stats(stats[:, t, :], xw[:, t, :]).then_inc(stat_done, 1)
            dve.wait_ge(stat_done, base * 2 * NT + (half + 1) * NT)
            merge_stats(nc, dve, stats, mean, var, mean_ready, base * 2 + half)
            dve.wait_ge(rstd_ready, base * 2 + half + 1)
            for t in range(NT):
                nc.vector.tensor_scalar(xn[:, t, :], xw[:, t, :], mean[:, t:t + 1], rstd[:, t:t + 1], ALU.subtract, ALU.mult).then_inc(xn_ready, 1)

        @block.vector
        def _(dve):
            nc.vector.memset(vx[:, :, :, P:NB].rearrange("p a b c -> p (a b) c"), 1.0).then_inc(ones_set, 1)
            for n, (name, rb, cols) in enumerate(ints):
                dve.wait_ge(raw_in, 16 * n + 16)
                if n:
                    dve.wait_ge(raw_ps, 4 * n)
                nc.vector.tensor_scalar(rawf, raw, 1.0 / 127.0, None, ALU.mult).then_inc(raw_ready, 1)
                for q in range(4):
                    dve.wait_ge(raw_ps, 4 * n + q + 1)
                    if n < 2:
                        dst = (wg, wu)[n][:, q // 2, (q % 2) * 384:(q % 2) * 384 + 384]
                    else:
                        dst = wd[:, 3 * (q // 2):3 * (q // 2) + 3, (q % 2) * P:(q % 2 + 1) * P]
                    src = bank(q, 0, 384)
                    nc.vector.tensor_copy(dst, src if n < 2 else src.rearrange("p (a c) -> p a c", a=3)).then_inc(raw_done, 1)
            dve.wait_ge(raw_done, 12)
            dve.wait_ge(loaded, 80)
            with dve.Fori(0, B // 2) as i:
                for j in range(2):
                    n = 2 * i + j
                    nc.vector.tensor_copy(idxn[:], idxT[:, bass.ds(n * E, E)]).then_inc(small, 1)
                    nc.vector.tensor_copy(gn[:], gT[:, bass.ds(n * E, E)]).then_inc(small, 1)
                    dve.wait_ge(small, n * 2 + 2)
                    dve.wait_ge(add_ps, n * NT)
                    for e in range(E):
                        nc.vector.tensor_scalar(put[:, e, :], const[:, C_TOK:C_TOK + L], idxn[:, e:e + 1], gn[:, e:e + 1],
                                                ALU.is_equal, ALU.mult).then_inc(put_ready, 1)
                    for t in range(NT):
                        dve.wait_ge(add_ps, n * NT + t + 1)
                        nc.vector.tensor_tensor(xw[:, t, :], bank(t % 2, 0, D),
                                                resid[:, bass.ds(n * NT + t, 1), :].rearrange("p a d -> p (a d)"), ALU.add).then_inc(xw_ready, 1)
                    dve.wait_ge(xw_ready, n * 2 * NT + NT)
                    norm(dve, n, 0)
                    dve.wait_ge(ssk_ready, n * (NT + 1) + NT)
                    nc.vector.tensor_scalar(ssk[:], ssk[:], 1.0 / D, 1e-6, ALU.mult, ALU.add).then_inc(ssk_ready, 1)
                    dve.wait_ge(ssq_ps, n + 1)
                    nc.vector.tensor_scalar(ssq[:], bank(2, 0, NT), 1.0 / D, 1e-6, ALU.mult, ALU.add).then_inc(ssq_ready, 1)
                    dve.wait_ge(rk_ready, n + 1)
                    dve.wait_ge(v_ready, n * NT + NT)
                    for t in range(NT):
                        nc.vector.scalar_tensor_tensor(k2[:, t, :], bank(4 + t, 0, D), rk[:, t:t + 1], knw[:], ALU.mult, ALU.mult).then_inc(kk_ready, 1)
                    dve.wait_ge(kvm_ps, n + 1)
                    for hb in range(DB):
                        nc.vector.tensor_tensor(kvm[:, hb, :], bank(3, hb * NB, (hb + 1) * NB), heads, ALU.mult).then_inc(kvm_ready, 1)
                    dve.wait_ge(rq_ready, n + 1)
                    for t in range(NT):
                        r = nrm[:, t % 2, :, :]
                        dve.wait_ge(att_ps, n * NT + t + 1)
                        att = bank(t % 2, 0, DB * NB).rearrange("p (k c) -> p k c", k=DB)
                        nc.vector.tensor_scalar(r, att[:, :, P:NB], rq[:, t:t + 1], 1e-6, ALU.mult, ALU.add).then_inc(nrm_step, 1)
                        dve.wait_ge(nrm_step, n * 3 * NT + 3 * t + 1)
                        nc.vector.reciprocal(r, r).then_inc(nrm_step, 1)
                        dve.wait_ge(nrm_step, n * 3 * NT + 3 * t + 2)
                        nc.vector.tensor_scalar(r, r, rq[:, t:t + 1], None, ALU.mult).then_inc(nrm_step, 1)
                        dve.wait_ge(nrm_step, n * 3 * NT + 3 * t + 3)
                        if t >= 2:
                            dve.wait_ge(oT_ps, n * NT + t - 1)
                        for hb in range(DB):
                            ins = nc.vector.tensor_tensor(o[:, t % 2, hb * P:(hb + 1) * P].rearrange("p (h c) -> p h c", h=8),
                                                          att[:, hb, 0:P].rearrange("p (h c) -> p h c", h=8),
                                                          spread(r[:, hb, :], 2, DH1), ALU.mult)
                        ins.then_inc(o_ready, 1)
                    for t in range(NT):
                        dve.wait_ge(wo_ps, n * NT + t + 1)
                        nc.vector.tensor_tensor(xw[:, t, :], bank(4 + t % 2, 0, D), xw[:, t, :], ALU.add).then_inc(xw_ready, 1)
                    dve.wait_ge(xw_ready, n * 2 * NT + 2 * NT)
                    norm(dve, n, 1)
                    for m in range(HB):
                        dve.wait_ge(u_ps, n * HB + m + 1)
                        dve.wait_ge(g_ready, n * HB + m + 1)
                        if m == 0:
                            dve.wait_ge(y_ps, n * NT)
                        nc.vector.tensor_tensor(hT[:, m, :], bank(2 + m % 2), gs[:, m % 2, :], ALU.mult).then_inc(h_ready, 1)
                    dve.wait_ge(stored[j], 16 * i)
                    for t in range(NT):
                        dve.wait_ge(y_ps, n * NT + t + 1)
                        nc.vector.tensor_tensor(yo[:, j, t, :], bank(4 + t, 0, D), xw[:, t, :], ALU.add).then_inc(y_ready, 1)

        @block.gpsimd
        def _(pool):
            with pool.Fori(0, B) as n:
                pool.wait_ge(mean_ready, (n * 2 + 1) * MERGE)
                pool.tensor_tensor(rstd[:], var[:, 0, :], mhalf, ALU.pow).then_inc(rstd_ready, 1)
                pool.wait_ge(ssk_ready, (n + 1) * (NT + 1))
                pool.tensor_tensor(rk[:], ssk[:], mhalf, ALU.pow).then_inc(rk_ready, 1)
                pool.wait_ge(ssq_ready, n + 1)
                pool.tensor_tensor(rq[:], ssq[:], mhalf, ALU.pow).then_inc(rq_ready, 1)
                pool.wait_ge(mean_ready, (n * 2 + 2) * MERGE)
                pool.tensor_tensor(rstd[:], var[:, 0, :], mhalf, ALU.pow).then_inc(rstd_ready, 1)

        @block.scalar
        def _(act):
            act.wait_ge(loaded, 80)
            act.wait_ge(ones_set, 1)
            with act.Fori(0, B) as n:
                for c in range(DB):
                    act.wait_ge(xT_ps, n * 4 + c + 1)
                    nc.scalar.activation(xT[:, c, :], bank(2 + c), ACT.Copy).then_inc(xT_ready, 1)
                for c in range(DB):
                    act.wait_ge(q_ps, n * 2 + c + 1)
                    nc.scalar.activation(sqq[:, c, :], bank(c), ACT.Square).then_inc(q_ready, 1)
                    nc.scalar.activation(qT[:, c, :], bank(c), ACT.Relu, scale=qnw[:, c:c + 1]).then_inc(q_ready, 1)
                for t in range(NT):
                    act.wait_ge(kv_ps, n * NT + t + 1)
                    act.wait_ge(ssk_ready, n * (NT + 1) + t)
                    nc.scalar.activation(sqk[:], bank(4 + t, 0, D), ACT.Square, accum_out=ssk[:, t:t + 1]).then_inc(ssk_ready, 1)
                    nc.scalar.activation(vx[:, t, :, 0:P], bank(4 + t, D, 2 * D).rearrange("p (k c) -> p k c", k=DB), ACT.Copy).then_inc(v_ready, 1)
                for t in range(NT):
                    act.wait_ge(kk_ready, n * NT + t + 1)
                    nc.scalar.activation(k2[:, t, :], k2[:, t, :], ACT.Relu).then_inc(k2_ready, 1)
                for t in range(NT):
                    act.wait_ge(oT_ps, n * NT + t + 1)
                    nc.scalar.activation(oT[t % 2][:].rearrange("p a c -> p (a c)"), bank(2 + t % 2, 0, D), ACT.Copy).then_inc(oT_ready, 1)
                for c in range(DB):
                    act.wait_ge(xT_ps, n * 4 + 2 + c + 1)
                    nc.scalar.activation(xT[:, c, :], bank(6 + c), ACT.Copy).then_inc(xT_ready, 1)
                for m in range(HB):
                    act.wait_ge(g_ps, n * HB + m + 1)
                    if m >= 2:
                        act.wait_ge(h_ready, n * HB + m - 1)
                    nc.scalar.activation(gs[:, m % 2, :], bank(m % 2), ACT.Silu).then_inc(g_ready, 1)

        def out_tile(pe, n, t):
            pe.wait_ge(o_ready, n * NT + t + 1)
            if t == 0:
                pe.wait_ge(kvm_ready, n * 2 + 2)
            if t >= 2:
                pe.wait_ge(oT_ready, n * NT + t - 1)
            for c in range(DB):
                ins = nc.tensor.transpose(bank(2 + t % 2, c * P, (c + 1) * P), o[:, t % 2, c * P:(c + 1) * P], eye)
            ins.then_inc(oT_ps, 1)
            pe.wait_ge(oT_ready, n * NT + t + 1)
            if t >= 2:
                pe.wait_ge(xw_ready, n * 2 * NT + NT + t - 1)
            mm(bank(4 + t % 2, 0, D), one_row, bout[:], start=True, stop=False)
            for c in range(DB):
                ins = mm(bank(4 + t % 2, 0, D), oT[t % 2][:, c, :], wout[:, c, :], start=False, stop=c == DB - 1)
            ins.then_inc(wo_ps, 1)

        @block.tensor
        def _(pe):
            for n, (name, rb, cols) in enumerate(ints):
                pe.wait_ge(raw_ready, n + 1)
                for q in range(4):
                    if n:
                        pe.wait_ge(raw_done, 4 * (n - 1) + q + 1)
                    for r in range(3):
                        if n < 2:
                            src = rawf[:, (3 * (q % 2) + r) * D + (q // 2) * P:(3 * (q % 2) + r) * D + (q // 2 + 1) * P]
                        else:
                            src = rawf[:, (q % 2) * F1 + (3 * (q // 2) + r) * P:(q % 2) * F1 + (3 * (q // 2) + r + 1) * P]
                        ins = nc.tensor.transpose(bank(q, r * P, (r + 1) * P), src, eye)
                    ins.then_inc(raw_ps, 1)
            pe.wait_ge(raw_done, 12)
            pe.wait_ge(loaded, 80)
            with pe.Fori(0, B) as n:
                pe.wait_ge(put_ready, n * E + E)
                pe.wait_ge(g_ready, n * HB)
                for t in range(NT):
                    if t >= 2:
                        pe.wait_ge(xw_ready, n * 2 * NT + t - 1)
                    for e in range(E):
                        ins = mm(bank(t % 2, 0, D), put[:, e, t * P:(t + 1) * P], slots[:, e, bass.ds(n * D, D)], start=e == 0, stop=e == E - 1)
                    ins.then_inc(add_ps, 1)
                pe.wait_ge(h_ready, n * HB)
                pe.wait_ge(xn_ready, n * 2 * NT + NT)
                for c in range(DB):
                    for t in range(NT):
                        ins = nc.tensor.transpose(bank(2 + c, t * P, (t + 1) * P), xn[:, t, c * P:(c + 1) * P], eye)
                    ins.then_inc(xT_ps, 1)
                pe.wait_ge(xw_ready, n * 2 * NT + NT)
                pe.wait_ge(xT_ready, n * 4 + 2)
                for m in range(DB):
                    for c in range(DB):
                        ins = mm(bank(m), wqkv[:, c, m * P:(m + 1) * P], xT[:, c, :], start=c == 0, stop=c == DB - 1)
                    ins.then_inc(q_ps, 1)
                pe.wait_ge(y_ready, n * NT)
                for t in range(NT):
                    for c in range(DB):
                        ins = mm(bank(4 + t), xT[:, c, t * P:(t + 1) * P], wqkv[:, c, D:3 * D], start=c == 0, stop=c == DB - 1)
                    ins.then_inc(kv_ps, 1)
                pe.wait_ge(q_ready, n * 4 + 4)
                for t in range(NT):
                    for c in range(DB):
                        ins = mm(bank(2, t, t + 1), sqq[:, c, t * P:(t + 1) * P], one_col, start=c == 0, stop=c == DB - 1)
                ins.then_inc(ssq_ps, 1)
                for hb in range(DB):
                    for t in range(NT):
                        pe.wait_ge(k2_ready, n * NT + t + 1)
                        ins = mm(bank(3, hb * NB, (hb + 1) * NB), k2[:, t, hb * P:(hb + 1) * P], vx[:, t, hb, :], start=t == 0, stop=t == NT - 1)
                ins.then_inc(kvm_ps, 1)
                pe.wait_ge(kvm_ready, n * 2 + 2)
                for t in range(NT):
                    if t >= 2:
                        pe.wait_ge(o_ready, n * NT + t - 1)
                    for hb in range(DB):
                        ins = mm(bank(t % 2, hb * NB, (hb + 1) * NB), qT[:, hb, t * P:(t + 1) * P], kvm[:, hb, :], start=True, stop=True)
                    ins.then_inc(att_ps, 1)
                    if t == 0:
                        pe.wait_ge(ssq_ready, n + 1)
                    if t >= 1:
                        out_tile(pe, n, t - 1)
                out_tile(pe, n, NT - 1)
                pe.wait_ge(xn_ready, n * 2 * NT + 2 * NT)
                for c in range(DB):
                    for t in range(NT):
                        ins = nc.tensor.transpose(bank(6 + c, t * P, (t + 1) * P), xn[:, t, c * P:(c + 1) * P], eye)
                    ins.then_inc(xT_ps, 1)
                pe.wait_ge(xT_ready, n * 4 + 4)
                pe.wait_ge(o_ready, n * NT + NT)
                for m in range(HB):
                    if m >= 2:
                        pe.wait_ge(g_ready, n * HB + m - 1)
                    for c in range(DB):
                        ins = mm(bank(m % 2), wg[:, c, m * P:(m + 1) * P], xT[:, c, :], start=c == 0, stop=c == DB - 1)
                    ins.then_inc(g_ps, 1)
                    if m >= 2:
                        pe.wait_ge(h_ready, n * HB + m - 1)
                    for c in range(DB):
                        ins = mm(bank(2 + m % 2), wu[:, c, m * P:(m + 1) * P], xT[:, c, :], start=c == 0, stop=c == DB - 1)
                    ins.then_inc(u_ps, 1)
                pe.wait_ge(h_ready, n * HB + HB)
                for t in range(NT):
                    for m in range(HB):
                        ins = mm(bank(4 + t, 0, D), hT[:, m, t * P:(t + 1) * P], wd[:, m, :], start=m == 0, stop=m == HB - 1)
                    ins.then_inc(y_ps, 1)


def program(nc, A, out):
    with ExitStack() as ctx:
        mk = Maker(nc, ctx)
        const = mk.sb("const", [P, C_END])
        resid = mk.sb("resid", [P, B * NT, D])
        ps = ctx.enter_context(nc.psum_tensor("ps", [P, 8, 512], F32))
        idx_dram = nc.dram_tensor("idx_dram", [B * E, CAP], F32).ap()
        x_in = A["L0_attn_hidden_states"].rearrange("b (t p) d -> p (b t) d", p=P)
        got = mk.sem("got")
        with nc.Block() as block:
            @block.sync
            def _(sp):
                sp.dma_start(const[:], A["const"]).then_inc(got, 16)
                for b in range(B):
                    sp.dma_start(resid[:, b * NT:(b + 1) * NT, :], x_in[:, b * NT:(b + 1) * NT, :]).then_inc(got, 16)
                sp.wait_ge(got, 16 * (B + 1))
        prob = mk.sb("prob", [P, NT, B * E])
        mean_all, rstd_all = mk.sb("mean_all", [P, B * NT]), mk.sb("rstd_all", [P, B * NT])
        attention0(nc, A, const, resid, ps, prob, mean_all, rstd_all)
        slots = mk.sb("slots", [P, E, DB * B * CAP])
        idxT, gT = mk.sb("idxT", [P, B * E]), mk.sb("gT", [P, B * E])
        choose_tokens(nc, const, ps, prob, idxT, gT, idx_dram)
        gather_tokens(nc, const, resid, ps, mean_all, rstd_all, idx_dram, slots)
        experts(nc, A, ps, slots)
        layer1(nc, A, const, resid, ps, slots, idxT, gT, out)


def kernel(**inputs):
    import numpy as _np
    import concourse.bacc as _bacc
    from concourse import mybir as _mybir
    from concourse.bass_utils import run_bass_kernel_spmd as _run

    nc = _bacc.Bacc("TRN2", target_bir_lowering=False, num_devices=1)
    arrays, aps = {}, {}
    for name, a in {**inputs, "const": constant_table()}.items():
        a = _np.ascontiguousarray(a)
        arrays[f"in_{name}"] = a
        aps[name] = nc.dram_tensor(f"in_{name}", a.shape, _mybir.dt.from_np(a.dtype), kind="ExternalInput").ap()
    out = nc.dram_tensor("out_0", (B, L, D), F32, kind="ExternalOutput").ap()
    program(nc, aps, out)
    return _run(nc, [arrays], core_ids=[0]).results[0]["out_0"]
```

```python
import concourse.bass as bass
from concourse import mybir
from contextlib import ExitStack

F32 = mybir.dt.float32
I32 = mybir.dt.int32
U32 = mybir.dt.uint32
ALU = mybir.AluOpType
ACT = mybir.ActivationFunctionType
AX = mybir.AxisListType

P = 128
B, L, D = 8, 512, 256
NT = L // P
DB = D // P
H, DK = 4, 64
E, CAP = 8, 2 * L // 8
F0 = 1024
H1, DH1 = 16, 16
F1 = 768
LEVELS = 7
TAPS_S, TAPS_L = 3, 31

C_EYE = 0
C_LEVEL = C_EYE + P
C_UP1 = C_LEVEL + LEVELS * P
C_CAUSAL = C_UP1 + P
C_HEADS = C_CAUSAL + P
C_PAIR = C_HEADS + P + 8
C_TOK = C_PAIR + P
C_TOKID = C_TOK + L
C_ONE = C_TOKID + NT
C_MHALF = C_ONE + P
C_END = C_MHALF + 32


def constant_table():
    import numpy as np
    i = np.arange(P)
    t = np.zeros((P, C_END), np.float32)
    t[:, C_EYE:C_EYE + P] = np.eye(P)
    for n in range(LEVELS):
        s = 1 << n
        low = (i[:, None] // (2 * s) == i[None] // (2 * s)) & (i[:, None] // s % 2 == 1) & (i[None] // s % 2 == 0)
        t[:, C_LEVEL + n * P:C_LEVEL + (n + 1) * P] = -1.0 * low
        if n == 0:
            t[:, C_UP1:C_UP1 + P] = -1.0 * low.T
    t[:, C_CAUSAL:C_CAUSAL + P] = i[:, None] <= i[None]
    t[:, C_HEADS:C_HEADS + P] = i[:, None] // DH1 == i[None] // DH1
    t[:, C_HEADS + P:C_HEADS + P + 8] = i[:, None] // DH1 == np.arange(8)[None]
    t[:, C_PAIR:C_PAIR + P] = i[:, None] // DK == i[None] // DK
    t[:, C_TOK:C_TOK + L] = np.arange(L)[None]
    t[:, C_TOKID:C_TOKID + NT] = i[:, None] + P * np.arange(NT)[None]
    t[:, C_ONE:C_ONE + P] = 1.0
    t[:, C_MHALF:C_MHALF + 32] = -0.5
    return t


def spread(ap, axis, n):
    shape = list(ap.shape)
    shape.insert(axis, n)
    return ap.unsqueeze(axis).broadcast_to(shape)


class Maker:

    def __init__(self, nc, ctx, prefix=""):
        self.nc, self.ctx, self.prefix = nc, ctx, prefix

    def sb(self, name, shape, dt=F32):
        return self.ctx.enter_context(self.nc.sbuf_tensor(self.prefix + name, shape, dt))

    def sem(self, name):
        return self.ctx.enter_context(self.nc.semaphore(self.prefix + name))


MERGE = 7


def merge_stats(nc, dve, stats, mean, var, done, i):
    ev, od = stats[:, :, 1], stats[:, :, 4]
    nc.vector.tensor_tensor(mean[:], ev, od, ALU.add).then_inc(done, 1)
    nc.vector.tensor_tensor(var[:, 1, :], ev, od, ALU.subtract).then_inc(done, 1)
    nc.vector.tensor_tensor(var[:, 2, :], stats[:, :, 2], stats[:, :, 5], ALU.add).then_inc(done, 1)
    dve.wait_ge(done, i * MERGE + 3)
    nc.vector.tensor_scalar(mean[:], mean[:], 0.5, None, ALU.mult).then_inc(done, 1)
    nc.vector.tensor_scalar(var[:, 2, :], var[:, 2, :], 1.0 / D, 1e-5, ALU.mult, ALU.add).then_inc(done, 1)
    nc.vector.tensor_tensor(var[:, 1, :], var[:, 1, :], var[:, 1, :], ALU.mult).then_inc(done, 1)
    dve.wait_ge(done, i * MERGE + 6)
    nc.vector.scalar_tensor_tensor(var[:, 0, :], var[:, 1, :], 0.25, var[:, 2, :], ALU.mult, ALU.add).then_inc(done, 1)


def attention0(nc, A, const, resid, x_in, ps, prob, mean_all, rstd_all):
    with ExitStack() as ctx:
        mk = Maker(nc, ctx, "a0_")
        sb, sem = mk.sb, mk.sem
        eye = const[:, C_EYE:C_EYE + P]
        eye4 = spread(eye, 1, H)
        level = [spread(const[:, C_LEVEL + n * P:C_LEVEL + (n + 1) * P], 1, H) for n in range(LEVELS)]
        up1 = spread(const[:, C_UP1:C_UP1 + P], 1, H)
        causal = spread(const[:, C_CAUSAL:C_CAUSAL + P], 1, 2)
        same_head = spread(const[:, C_PAIR:C_PAIR + P], 1, DB)
        mhalf = const[:, C_MHALF:C_MHALF + 32]

        w_qkv = sb("w_qkv", [P, DB, 3 * D])
        w_beta = sb("w_beta", [P, DB, P])
        w_route = sb("w_route", [P, DB, P])
        w_f2 = sb("w_f2", [P, 4, P])
        conv_w = sb("conv_w", [P, 6, 4])
        fir_sw = sb("fir_sw", [P, DB, TAPS_S])
        fir_lw = sb("fir_lw", [P, DB, TAPS_L])
        w_f1 = sb("w_f1", [P, 8, 2 * D])
        b_f1 = sb("b_f1", [P, 4])
        b_f2 = sb("b_f2", [P, 16])
        rtau = sb("rtau", [P, H])
        normw = sb("normw", [P, 1])
        w_o = sb("w_o", [P, DB, D])
        small_w = sb("small_w", [P, DB, H])
        small_f = sb("small_f", [P, 4, 16])

        stats = sb("stats", [P, NT, 6])
        mean = sb("mean", [P, NT])
        var = sb("var", [P, 3, NT])
        rstd = sb("rstd", [P, NT])
        g_stats = sb("g_stats", [P, NT, 6])
        g_mean = sb("g_mean", [P, NT])
        g_var = sb("g_var", [P, 3, NT])
        g_rstd = sb("g_rstd", [P, NT])
        xn = sb("xn", [P, NT, D])
        xT = sb("xT", [P, DB, L])
        qkv = sb("qkv", [P, 6, L])
        ez = sb("ez", [P, NT * H])
        beta = sb("beta", [P, NT * H])
        sq = [sb(f"sq{j}", [P, 512]) for j in range(2)]
        ss = sb("ss", [P, NT * 8])
        rs = sb("rs", [P, NT * 8])
        kz = sb("kz", [P, NT, H * P])
        qn = sb("qn", [P, NT, D])
        dv = sb("dv", [P, NT, 2, D])
        vk = sb("vk", [P, NT, 2, D])
        kT = [[sb(f"kT{t}{hb}", [P, 4, P]) for hb in range(DB)] for t in range(NT)]
        hidT = sb("hidT", [P, 4, L])
        tap = hidT[:, 0:3, :]
        AT = [hidT[:, t, :].rearrange("p (h c) -> p h c", h=H) for t in range(NT)]
        loc = [sb(f"loc{t}", [P, H, P]) for t in range(NT)]
        TT = [sb(f"TT{t}", [P, H, P]) for t in range(NT)]
        T = [sb(f"T{g}", [P, H, P]) for g in range(2)]
        X = [sb(f"X{g}", [P, H, P]) for g in range(2)]
        mixa = [T[g][:].rearrange("p h c -> p (h c)").rearrange("p (k d) -> p k d", k=2) for g in range(2)]
        mixb = [X[g][:].rearrange("p h c -> p (h c)").rearrange("p (k d) -> p k d", k=2) for g in range(2)]
        rT = [T[g][:].rearrange("p h c -> p (h c)") for g in range(2)]
        w_tok = [sb(f"w_tok{g}", [P, D]) for g in range(2)]
        nwT = [sb(f"nwT{t}", [P, DB, P]) for t in range(NT)]
        uadj = sb("uadj", [P, NT, D])
        S = sb("S", [P, DB, P])
        dT = sb("dT", [P, DB, L])
        firT = sb("firT", [P, 2, DB, L])
        lg = sb("lg", [P, NT * H, 4])
        mx = sb("mx", [P, NT * H])
        ex = sb("ex", [P, NT * H, 4])
        sm = sb("sm", [P, NT * H])
        pv = sb("pv", [P, NT * H])
        wt = sb("wt", [P, NT * H, 4])
        o = sb("o", [P, NT, D])
        osq = sb("osq", [P, NT, D])
        so = sb("so", [P, NT * H])
        ro = sb("ro", [P, NT * H])
        oT = [sb(f"oT{t}", [P, DB, P]) for t in range(2)]
        sc = sb("sc", [P, NT, E])
        g_top, g_den = sb("g_top", [P, NT]), sb("g_den", [P, NT])
        g_ex = sb("g_ex", [P, NT, E])
        w_rows = sb("w_rows", [E, D])

        loaded, gate_w_in, rows_in, prepared, prep = sem("loaded"), sem("gate_w_in"), sem("rows_in"), sem("prepared"), sem("prep")
        tau_exp, route_ps = sem("tau_exp"), sem("route_ps")
        stat_done, mean_ready, rstd_ready, xn_ready = (sem(n) for n in ("stat_done", "mean_ready", "rstd_ready", "xn_ready"))
        xT_ps, xT_ready = sem("xT_ps"), sem("xT_ready")
        proj_ps, tap3_done, conv_done, silu_done = sem("proj_ps"), sem("tap3_done"), sem("conv_done"), sem("silu_done")
        tap_ready, pool_conv = sem("tap_ready"), sem("pool_conv")
        z_ps, ez_ready, beta_ready = sem("z_ps"), sem("ez_ready"), sem("beta_ready")
        kq_ps, sq_ready, ss_ready, rs_ready, kqn_ready = (sem(n) for n in ("kq_ps", "sq_ready", "ss_ready", "rs_ready", "kqn_ready"))
        v_ps, v_ready, vk_ready = sem("v_ps"), sem("v_ready"), sem("vk_ready")
        kT_ps, kT_ready, al_ps, AT_ready, loc_ready = (sem(n) for n in ("kT_ps", "kT_ready", "al_ps", "AT_ready", "loc_ready"))
        tt1_ready, t1_ps, t1_ready = sem("tt1_ready"), sem("t1_ps"), sem("t1_ready")
        x_ps, x_ready, t_ps, t_ready, tt_ps, tt_ready = (
            sem(n) for n in ("x_ps", "x_ready", "t_ps", "t_ready", "tt_ps", "tt_ready"))
        uw_ps, uw_ready, wT_ps, wT_ready = sem("uw_ps"), sem("uw_ready"), sem("wT_ps"), sem("wT_ready")
        ws_ps, u_ready, o_ps, o_ready, s_ps, s_ready, d_ps, d_ready = (
            sem(n) for n in ("ws_ps", "u_ready", "o_ps", "o_ready", "s_ps", "s_ready", "d_ps", "d_ready"))
        fir_step = sem("fir_step")
        hid_ps, hid_ready, lg_ps = sem("hid_ps"), sem("hid_ready"), sem("lg_ps")
        ml_ready, ex_ready, wt_ready = sem("ml_ready"), sem("ex_ready"), sem("wt_ready")
        f_ps, mixa_ready, mixb_ready, mix_ready, osq_ready = (
            sem(n) for n in ("f_ps", "mixa_ready", "mixb_ready", "mix_ready", "osq_ready"))
        so_ready, ro_ready, on_ready = sem("so_ready"), sem("ro_ready"), sem("on_ready")
        oT_ps, oT_ready, y_ps, resid_done = sem("oT_ps"), sem("oT_ready"), sem("y_ps"), sem("resid_done")
        g_stat, g_mean_ready, g_rstd_ready, g_xn_ready, rT_ps, rT_ready, sc_ps, sc_ready, g_ex_ready, g_den_ready, prob_done = (
            sem(n) for n in ("g_stat", "g_mean_ready", "g_rstd_ready", "g_xn_ready", "rT_ps", "rT_ready", "sc_ps", "sc_ready",
                             "g_ex_ready", "g_den_ready", "prob_done"))

        def bank(n, lo=0, hi=512):
            return ps[:, n, lo:hi]

        def by_head(ap):
            return ap.rearrange("p (h c) -> p h c", h=H)

        def rows(i, t):
            return resid[:, bass.ds(i * NT + t, 1), :].rearrange("p a d -> p (a d)")

        def k_of(t):
            v = kz[:, t, :].rearrange("p (k a c) -> p k a c", k=2, a=4)
            return v[:, :, 0:4:3, 0:DK]

        proj_bank = (0, 1, 2, 0, 6, 7)
        on_dve = {0: 0, 2: 1, 3: 2, 5: 3}
        on_pool = {1: 0, 4: 1}

        def conv_wait(eng, b, m):
            if m in on_dve:
                eng.wait_ge(conv_done, b * 12 + 3 * on_dve[m] + 3)
            else:
                eng.wait_ge(pool_conv, b * 6 + 3 * on_pool[m] + 3)

        NLOAD = 17
        NFIR = 2 * (TAPS_S + TAPS_L)
        block = ctx.enter_context(nc.Block())

        @block.sync
        def _(sp):
            with nc.allow_non_contiguous_dma(reason="small parameters"):
                for j, n in enumerate(("W_q", "W_k", "W_v")):
                    sp.dma_start(w_qkv[:, :, j * D:(j + 1) * D],
                                 A["L0_attn_" + n].rearrange("(c p) n -> p c n", p=P)).then_inc(loaded, 16)
                sp.dma_start(small_w[:], A["L0_attn_W_b"].rearrange("(c p) n -> p c n", p=P)).then_inc(loaded, 16)
                for j, n in enumerate("qkv"):
                    sp.dma_start(conv_w[:, 2 * j:2 * j + 2, :],
                                 A[f"L0_attn_conv_w_{n}"].rearrange("(c p) k -> p c k", p=P)).then_inc(loaded, 16)
                sp.dma_start(fir_sw[:], A["L0_attn_fir_short_w"].rearrange("h d k -> (h d) k")
                             .rearrange("(c p) k -> p c k", p=P)).then_inc(loaded, 16)
                sp.dma_start(fir_lw[:], A["L0_attn_fir_long_w"].rearrange("h d k -> (h d) k")
                             .rearrange("(c p) k -> p c k", p=P)).then_inc(loaded, 16)
                sp.dma_start(b_f1[:], A["L0_attn_b_fuse1"].rearrange("(c p) -> p c", p=P)).then_inc(loaded, 16)
                sp.dma_start(small_f[:], A["L0_attn_W_fuse2"].rearrange("(c p) n -> p c n", p=P)).then_inc(loaded, 16)
                sp.dma_start(b_f2[:], A["L0_attn_b_fuse2"].unsqueeze(0).broadcast_to([P, 16])).then_inc(loaded, 16)
                sp.dma_start(rtau[:], A["L0_attn_others_log_tau"].unsqueeze(0).broadcast_to([P, H])).then_inc(loaded, 16)
                for half in range(2):
                    sp.dma_start(normw[64 * half:64 * half + 64, :],
                                 A["L0_attn_norm_w"].unsqueeze(1)).then_inc(loaded, 16)
                sp.dma_start(w_o[:], A["L0_attn_W_o"].rearrange("(c p) n -> p c n", p=P)).then_inc(loaded, 16)
                sp.dma_start(w_rows[:], A["L0_ffn_gate_w"]).then_inc(loaded, 16)
                sp.dma_start(w_f1[:], A["L0_attn_W_fuse1"].rearrange("(c p) n -> p c n", p=P)).then_inc(gate_w_in, 16)
                sp.dma_start(resid[:, NT:, :], x_in[:, NT:, :]).then_inc(rows_in, 16)

        def fir_order(k):
            if k < 4 * TAPS_S:
                return k // 2 % 2, k % 2, k // 4, 4
            k -= 4 * TAPS_S
            return 1, k % 2, TAPS_S + k // 2, 2

        @block.vector
        def _(dve):
            nc.vector.memset(kz[:].rearrange("p t c -> p (t c)"), 0.0).then_inc(prep, 1)
            nc.vector.memset(w_beta[:].rearrange("p c n -> p (c n)"), 0.0).then_inc(prep, 1)
            nc.vector.memset(w_route[:].rearrange("p c n -> p (c n)"), 0.0).then_inc(prep, 1)
            nc.vector.memset(w_f2[:].rearrange("p c n -> p (c n)"), 0.0).then_inc(prep, 1)
            dve.wait_ge(loaded, 16 * NLOAD)
            dve.wait_ge(prep, 4)
            nc.vector.tensor_copy(w_beta[:, :, 0:H], small_w[:]).then_inc(prepared, 1)
            nc.vector.tensor_copy(w_f2[:, :, 0:16], small_f[:]).then_inc(prepared, 1)
            nc.vector.tensor_scalar(w_o[:].rearrange("p c n -> p (c n)"), w_o[:].rearrange("p c n -> p (c n)"),
                                    normw[:, 0:1], None, ALU.mult).then_inc(prepared, 1)
            dve.wait_ge(route_ps, 1)
            nc.vector.tensor_copy(w_route[:, :, 0:E], bank(3, 0, DB * E).rearrange("p (c e) -> p c e", c=DB)).then_inc(prepared, 1)
            dve.wait_ge(tau_exp, 1)
            nc.vector.reciprocal(rtau[:], rtau[:]).then_inc(prep, 1)
            dve.wait_ge(prep, 5)

            def norm_in(b, route=None):
                for t in range(NT):
                    nc.vector.bn_stats(stats[:, t, :], rows(b, t)).then_inc(stat_done, 1)
                dve.wait_ge(stat_done, b * NT + NT)
                merge_stats(nc, dve, stats, mean, var, mean_ready, b)
                dve.wait_ge(mean_ready, b * MERGE + MERGE)
                dve.wait_ge(rstd_ready, b + 1)
                if route is not None:
                    dve.wait_ge(rT_ps, route * 2 + 2)
                for t in range(NT):
                    nc.vector.tensor_scalar(xn[:, t, :], rows(b, t), mean[:, t:t + 1], rstd[:, t:t + 1],
                                            ALU.subtract, ALU.mult).then_inc(xn_ready, 1)

            def conv(b, m):
                dve.wait_ge(tap3_done, b * 6 + m + 1)
                for s in range(1, 4):
                    if s > 1:
                        dve.wait_ge(conv_done, b * 12 + 3 * on_dve[m] + s - 1)
                    nc.vector.scalar_tensor_tensor(
                        qkv[:, m, s:], bank(proj_bank[m], 0, L - s), conv_w[:, m, 3 - s:4 - s],
                        qkv[:, m, s:], ALU.mult, ALU.add).then_inc(conv_done, 1)

            def fir(b, lo, hi):
                for k in range(lo, hi):
                    kind, c, s, back = fir_order(k)
                    w = (fir_sw, fir_lw)[kind]
                    n = (TAPS_S, TAPS_L)[kind]
                    v = qkv[:, 4 + c, 0:L - s]
                    if k == 0:
                        dve.wait_ge(silu_done, b * 6 + 6)
                    if s == 0:
                        nc.vector.tensor_scalar(firT[:, kind, c, :], v, w[:, c, n - 1:n], None, ALU.mult).then_inc(fir_step, 1)
                    else:
                        dve.wait_ge(fir_step, b * NFIR + k - back + 1)
                        nc.vector.scalar_tensor_tensor(firT[:, kind, c, s:], v, w[:, c, n - 1 - s:n - s],
                                                       firT[:, kind, c, s:], ALU.mult, ALU.add).then_inc(fir_step, 1)

            def route_stats(b):
                for t in range(NT):
                    nc.vector.bn_stats(g_stats[:, t, :], rows(b, t)).then_inc(g_stat, 1)
                dve.wait_ge(g_stat, b * NT + NT)
                merge_stats(nc, dve, g_stats, g_mean, g_var, g_mean_ready, b)

            def route_norm(b):
                dve.wait_ge(g_mean_ready, b * MERGE + MERGE)
                dve.wait_ge(g_rstd_ready, b + 1)
                for t in range(NT):
                    nc.vector.tensor_scalar(xn[:, t, :], rows(b, t), g_mean[:, t:t + 1], g_rstd[:, t:t + 1],
                                            ALU.subtract, ALU.mult).then_inc(g_xn_ready, 1)
                nc.vector.tensor_copy(mean_all[:, bass.ds(b * NT, NT)], g_mean[:]).then_inc(prob_done, 1)
                nc.vector.tensor_copy(rstd_all[:, bass.ds(b * NT, NT)], g_rstd[:]).then_inc(prob_done, 1)

            def route_scores(b):
                dve.wait_ge(sc_ps, b + 1)
                nc.vector.tensor_copy(sc[:], bank(7).rearrange("p (t e) -> p t e", t=NT)[:, :, 0:E]).then_inc(sc_ready, 1)
                dve.wait_ge(sc_ready, b * 3 + 1)
                nc.vector.reduce_max(g_top[:], sc[:], axis=AX.X).then_inc(sc_ready, 1)
                dve.wait_ge(sc_ready, b * 3 + 2)
                nc.vector.tensor_tensor(sc[:], sc[:], spread(g_top[:], 2, E), ALU.subtract).then_inc(sc_ready, 1)

            def route_prob(b):
                dve.wait_ge(g_ex_ready, b + 1)
                nc.vector.reduce_sum(g_den[:], g_ex[:], axis=AX.X).then_inc(g_den_ready, 1)
                dve.wait_ge(g_den_ready, b * 2 + 1)
                nc.vector.reciprocal(g_den[:], g_den[:]).then_inc(g_den_ready, 1)
                dve.wait_ge(g_den_ready, b * 2 + 2)
                nc.vector.tensor_tensor(prob[:, :, bass.ds(b * E, E)], g_ex[:], spread(g_den[:], 2, E), ALU.mult).then_inc(prob_done, 1)

            def main(b, route, norm_next):
                slot = 0
                for p2 in range(2):
                    for lv in range(1, LEVELS):
                        for g in range(2):
                            n = p2 * 12 + (lv - 1) * 2 + g + 1
                            dve.wait_ge(x_ps, b * 24 + n)
                            nc.vector.tensor_tensor(X[g][:], by_head(bank(g)), level[lv], ALU.mult).then_inc(x_ready, 1)
                        fir(b, slot * NFIR // 12, (slot + 1) * NFIR // 12)
                        slot += 1
                if route is not None:
                    route_stats(route)
                    route_norm(route)
                for t in range(NT):
                    if t:
                        dve.wait_ge(ws_ps, b * 3 + t)
                        dve.wait_ge(uw_ready, b * 8 + 8)
                        nc.vector.tensor_tensor(uadj[:, t, :], bank(4, 0, D), uadj[:, t, :], ALU.add).then_inc(u_ready, 1)
                    if t < NT - 1:
                        dve.wait_ge(s_ps, b * 3 + t + 1)
                        nc.vector.tensor_tensor(S[:], bank(6, 0, D).rearrange("p (a c) -> p a c", a=DB), same_head, ALU.mult).then_inc(s_ready, 1)
                if norm_next is not None:
                    if route is None:
                        dve.wait_ge(rows_in, 16)
                    norm_in(norm_next, route)
                if route is not None:
                    route_scores(route)

            def softmax_in(b, base):
                def step(ins):
                    base[0] += 1
                    ins.then_inc(ml_ready, 1)
                    dve.wait_ge(ml_ready, b * 11 + base[0])

                dve.wait_ge(lg_ps, b + 1)
                step(nc.vector.tensor_tensor(lg[:].rearrange("p (t h) c -> p t (h c)", t=NT),
                                             bank(6).rearrange("p (t c) -> p t c", t=NT)[:, :, 0:16], spread(b_f2[:], 1, NT), ALU.add))
                rt = spread(spread(rtau[:], 1, NT), 3, 3)
                l3 = lg[:, :, 0:3]
                step(nc.vector.tensor_tensor(l3.rearrange("p (t h) c -> p t h c", t=NT), l3.rearrange("p (t h) c -> p t h c", t=NT), rt, ALU.mult))
                step(nc.vector.reduce_max(mx[:], l3, axis=AX.X))
                step(nc.vector.tensor_tensor(l3, l3, spread(mx[:], 2, 3), ALU.subtract))

                def rest():
                    dve.wait_ge(ex_ready, 2 * b + 2)
                    step(nc.vector.reduce_sum(sm[:], ex[:, :, 0:3], axis=AX.X))
                    step(nc.vector.reciprocal(sm[:], sm[:]))
                    step(nc.vector.tensor_scalar(pv[:], ex[:, :, 3], 1.0, None, ALU.add))
                    step(nc.vector.reciprocal(pv[:], pv[:]))
                    step(nc.vector.tensor_scalar(mx[:], pv[:], 0.1 - 0.01, 1.0 - 0.1, ALU.mult, ALU.add))
                    step(nc.vector.tensor_tensor(pv[:], pv[:], mx[:], ALU.mult))
                    nc.vector.tensor_copy(wt[:, :, 3], pv[:]).then_inc(wt_ready, 1)
                    step(nc.vector.tensor_scalar(mx[:], pv[:], -1.0, 1.0, ALU.mult, ALU.add))
                    assert base[0] == 11
                    nc.vector.tensor_tensor(sm[:], sm[:], mx[:], ALU.mult).then_inc(wt_ready, 1)
                    dve.wait_ge(wt_ready, b * 3 + 2)
                    nc.vector.tensor_tensor(wt[:, :, 0:3], ex[:, :, 0:3], spread(sm[:], 2, 3), ALU.mult).then_inc(wt_ready, 1)
                    dve.wait_ge(wt_ready, b * 3 + 3)
                return rest

            def mix(b, t):
                dve.wait_ge(f_ps, b * 4 + t + 1)
                if t >= 2:
                    dve.wait_ge(mix_ready, b * 8 + 2 * (t - 2) + 2)
                w2 = wt[:, H * t:H * t + H, 0:2].rearrange("p h k -> p k h")
                nc.vector.tensor_tensor(mixa[t % 2].rearrange("p k (h c) -> p k h c", h=H),
                                        bank(4 + t % 2).rearrange("p (k h c) -> p k h c", k=2, h=H),
                                        spread(w2, 3, DK), ALU.mult).then_inc(mixa_ready, 1)

            def mix_sum(b, t):
                dve.wait_ge(mixa_ready, b * 4 + t + 1)
                nc.vector.tensor_tensor(o[:, t, :], mixa[t % 2][:, 0, :], mixa[t % 2][:, 1, :], ALU.add).then_inc(mix_ready, 1)
                dve.wait_ge(mix_ready, b * 8 + 2 * t + 1)
                dve.wait_ge(mixb_ready, b * 8 + 2 * t + 2)
                nc.vector.tensor_tensor(o[:, t, :], o[:, t, :], mixb[t % 2][:, 0, :], ALU.add).then_inc(mix_ready, 1)

            def kq_sums(b, p):
                for t in (2 * p, 2 * p + 1):
                    dve.wait_ge(sq_ready, b * 4 + t + 1)
                    nc.vector.reduce_sum(ss[:, 8 * t:8 * t + 8], sq[t % 2][:].rearrange("p (h c) -> p h c", c=DK),
                                         axis=AX.X).then_inc(ss_ready, 1)
                dve.wait_ge(ss_ready, b * 6 + 3 * p + 2)
                nc.vector.tensor_scalar(ss[:, 16 * p:16 * p + 16], ss[:, 16 * p:16 * p + 16], 1e-6, None, ALU.add).then_inc(ss_ready, 1)

            def kq_norm(b, p):
                dve.wait_ge(rs_ready, b * 2 + p + 1)
                for t in (2 * p, 2 * p + 1):
                    ks = spread(rs[:, 8 * t:8 * t + 4].rearrange("p (k a) -> p k a", k=2), 3, DK)
                    nc.vector.tensor_tensor(k_of(t), bank(t, 0, D).rearrange("p (k a c) -> p k a c", k=2, a=2), ks, ALU.mult).then_inc(kqn_ready, 1)
                    nc.vector.tensor_tensor(by_head(qn[:, t, :]), by_head(bank(t, D, 2 * D)),
                                            spread(rs[:, 8 * t + 4:8 * t + 8], 2, DK), ALU.mult).then_inc(kqn_ready, 1)

            def o_sums(b, p):
                for t in (2 * p, 2 * p + 1):
                    dve.wait_ge(osq_ready, b * 4 + t + 1)
                    nc.vector.reduce_sum(so[:, H * t:H * t + H], by_head(osq[:, t, :]), axis=AX.X).then_inc(so_ready, 1)
                dve.wait_ge(so_ready, b * 6 + 3 * p + 2)
                nc.vector.tensor_scalar(so[:, 8 * p:8 * p + 8], so[:, 8 * p:8 * p + 8], 1.0 / DK, 1e-5, ALU.mult, ALU.add).then_inc(so_ready, 1)

            def o_norm(b, p):
                dve.wait_ge(ro_ready, b * 2 + p + 1)
                for t in (2 * p, 2 * p + 1):
                    nc.vector.tensor_tensor(by_head(o[:, t, :]), by_head(o[:, t, :]),
                                            spread(ro[:, H * t:H * t + H], 2, DK), ALU.mult).then_inc(on_ready, 1)

            def add_out(b, p):
                for t in (2 * p, 2 * p + 1):
                    dve.wait_ge(y_ps, b * 4 + t + 1)
                    nc.vector.tensor_tensor(rows(b, t), bank(6 + t % 2, D, 2 * D), rows(b, t), ALU.add).then_inc(resid_done, 1)

            def join(tail, route, front):
                if tail is not None:
                    rest = softmax_in(tail, [0])
                if route is not None:
                    route_prob(route)
                if front is not None:
                    conv(front, 0)
                if tail is not None:
                    rest()
                    mix(tail, 0)
                    mix(tail, 1)
                if front is not None:
                    conv(front, 2)
                    conv(front, 3)
                    dve.wait_ge(ez_ready, front + 1)
                    nc.vector.tensor_scalar(beta[:], ez[:], 1.0, None, ALU.add).then_inc(beta_ready, 1)
                    dve.wait_ge(beta_ready, 2 * front + 1)
                    nc.vector.reciprocal(beta[:], beta[:]).then_inc(beta_ready, 1)
                if tail is not None:
                    mix_sum(tail, 0)
                    mix_sum(tail, 1)
                    mix(tail, 2)
                    mix(tail, 3)
                if front is not None:
                    conv(front, 5)
                if tail is not None:
                    o_sums(tail, 0)
                if front is not None:
                    kq_sums(front, 0)
                if tail is not None:
                    mix_sum(tail, 2)
                    mix_sum(tail, 3)
                    o_norm(tail, 0)
                    o_sums(tail, 1)
                if front is not None:
                    kq_sums(front, 1)
                if tail is not None:
                    o_norm(tail, 1)
                if front is not None:
                    kq_norm(front, 0)
                if tail is not None:
                    add_out(tail, 0)
                if front is not None:
                    kq_norm(front, 1)
                if tail is not None:
                    add_out(tail, 1)
                if front is not None:
                    for t in range(NT):
                        if tail is not None and t == 0:
                            dve.wait_ge(resid_done, tail * NT + NT)
                        dve.wait_ge(AT_ready, front * 4 + t + 1)
                        for k in range(2):
                            ins = nc.vector.tensor_tensor(loc[t][:, 2 * k:2 * k + 2, :],
                                                          bank(2 * (t % 2) + k).rearrange("p (a c) -> p a c", a=2)[:, :, P:2 * P], causal, ALU.mult)
                        ins.then_inc(loc_ready, 1)

            def flush(r):
                dve.wait_ge(resid_done, r * NT + NT)
                route_stats(r)
                route_norm(r)
                route_scores(r)
                route_prob(r)

            norm_in(0)
            join(None, None, 0)
            main(0, None, 1)
            join(0, None, 1)
            main(1, 0, 2)
            with dve.Fori(0, B - 3) as i:
                join(i + 1, i, i + 2)
                main(i + 2, i + 1, i + 3)
            join(B - 2, B - 3, B - 1)
            main(B - 1, B - 2, None)
            join(B - 1, B - 2, None)
            flush(B - 1)

        @block.gpsimd
        def _(pool):
            def norm_in(b):
                pool.wait_ge(mean_ready, b * MERGE + MERGE)
                pool.tensor_tensor(rstd[:], var[:, 0, :], mhalf[:, 0:NT], ALU.pow).then_inc(rstd_ready, 1)

            def main(b, route, norm_next):
                for p2 in range(2):
                    for g in range(2):
                        t = 2 * p2 + g
                        if p2:
                            tt1(b, t)
                if route is not None:
                    pool.wait_ge(g_mean_ready, route * MERGE + MERGE)
                    pool.tensor_tensor(g_rstd[:], g_var[:, 0, :], mhalf[:, 0:NT], ALU.pow).then_inc(g_rstd_ready, 1)
                if norm_next is not None:
                    norm_in(norm_next)

            def tt1(b, t):
                pool.wait_ge(AT_ready, b * 4 + t + 1)
                pool.tensor_tensor(TT[t][:], AT[t], up1, ALU.mult).then_inc(tt1_ready, 1)
                pool.wait_ge(tt1_ready, b * 8 + 2 * t + 1)
                pool.tensor_tensor(TT[t][:], TT[t][:], eye4, ALU.add).then_inc(tt1_ready, 1)

            def conv(b, m):
                for k in range(1, 4):
                    n = b * 6 + 3 * on_pool[m] + k
                    pool.wait_ge(tap_ready, n)
                    pool.wait_ge(pool_conv, n - 1)
                    pool.tensor_tensor(qkv[:, m, k:], tap[:, k - 1, 0:L - k], qkv[:, m, k:], ALU.add).then_inc(pool_conv, 1)

            def mixb_of(b, t):
                pool.wait_ge(o_ready, b * 8 + 8)
                if t >= 2:
                    pool.wait_ge(mix_ready, b * 8 + 2 * (t - 2) + 2)
                pool.tensor_tensor(mixb[t % 2].rearrange("p k (h c) -> p k h c", h=H),
                                   dv[:, t, :, :].rearrange("p k (h c) -> p k h c", h=H),
                                   spread(wt[:, H * t:H * t + H, 2:4].rearrange("p h k -> p k h"), 3, DK),
                                   ALU.mult).then_inc(mixb_ready, 1)
                pool.wait_ge(mixb_ready, b * 8 + 2 * t + 1)
                pool.tensor_tensor(mixb[t % 2][:, 0, :], mixb[t % 2][:, 0, :], mixb[t % 2][:, 1, :], ALU.add).then_inc(mixb_ready, 1)

            def join(tail, route, front):
                if front is not None:
                    conv(front, 1)
                if tail is not None:
                    pool.wait_ge(wt_ready, tail * 3 + 3)
                    mixb_of(tail, 0)
                    mixb_of(tail, 1)
                if front is not None:
                    conv(front, 4)
                if tail is not None:
                    mixb_of(tail, 2)
                    mixb_of(tail, 3)
                for p in range(2):
                    if tail is not None:
                        pool.wait_ge(so_ready, tail * 6 + 3 * p + 3)
                        pool.tensor_tensor(ro[:, 8 * p:8 * p + 8], so[:, 8 * p:8 * p + 8], mhalf[:, 0:8], ALU.pow).then_inc(ro_ready, 1)
                    if front is not None:
                        pool.wait_ge(ss_ready, front * 6 + 3 * p + 3)
                        pool.tensor_tensor(rs[:, 16 * p:16 * p + 16], ss[:, 16 * p:16 * p + 16], mhalf[:, 0:16], ALU.pow).then_inc(rs_ready, 1)
                if front is not None:
                    for t in range(NT):
                        bt = spread(beta[:, H * t:H * t + H], 2, DK)
                        pool.wait_ge(kqn_ready, front * 8 + 2 * t + 1)
                        pool.tensor_tensor(vk[:, t, 1, :].rearrange("p (k a c) -> p k a c", k=2, a=2), k_of(t),
                                           bt.rearrange("p (k a) c -> p k a c", k=2), ALU.mult).then_inc(vk_ready, 1)
                    pool.wait_ge(v_ready, front * 2 + 2)
                    for t in range(NT):
                        bt = spread(beta[:, H * t:H * t + H], 2, DK)
                        pool.tensor_tensor(by_head(vk[:, t, 0, :]), by_head(dv[:, t, 1, :]), bt, ALU.mult).then_inc(vk_ready, 1)
                if front is not None:
                    for t in range(2):
                        tt1(front, t)

            def flush(r):
                pool.wait_ge(g_mean_ready, r * MERGE + MERGE)
                pool.tensor_tensor(g_rstd[:], g_var[:, 0, :], mhalf[:, 0:NT], ALU.pow).then_inc(g_rstd_ready, 1)

            norm_in(0)
            join(None, None, 0)
            main(0, None, 1)
            join(0, None, 1)
            main(1, 0, 2)
            with pool.Fori(0, B - 3) as i:
                join(i + 1, i, i + 2)
                main(i + 2, i + 1, i + 3)
            join(B - 2, B - 3, B - 1)
            main(B - 1, B - 2, None)
            join(B - 1, B - 2, None)
            flush(B - 1)

        @block.scalar
        def _(act):
            act.wait_ge(loaded, 16 * NLOAD)
            nc.scalar.activation(rtau[:], rtau[:], ACT.Exp).then_inc(tau_exp, 1)

            def main(b, route, norm_next):
                for p2 in range(2):
                    for g in range(2):
                        act.wait_ge(t1_ps, b * 4 + 2 * p2 + g + 1)
                        nc.scalar.activation(T[g][:], by_head(bank(4 + g)), ACT.Copy).then_inc(t1_ready, 1)
                    for lv in range(1, LEVELS):
                        if lv < LEVELS - 1:
                            for g in range(2):
                                act.wait_ge(t_ps, b * 20 + p2 * 10 + (lv - 1) * 2 + g + 1)
                                nc.scalar.activation(T[g][:], by_head(bank(2 + g)), ACT.Copy).then_inc(t_ready, 1)
                        for g in range(2):
                            act.wait_ge(tt_ps, b * 24 + p2 * 12 + (lv - 1) * 2 + g + 1)
                            nc.scalar.activation(TT[2 * p2 + g][:], by_head(bank(4 + g)), ACT.Copy).then_inc(tt_ready, 1)
                for t in range(NT):
                    uw = by_head(bank(6 + t % 2))
                    act.wait_ge(uw_ps, b * 4 + t + 1)
                    if t >= 2:
                        act.wait_ge(wT_ps, b * 4 + t - 1)
                    nc.scalar.activation(by_head(w_tok[t % 2][:]), uw[:, :, DK:2 * DK], ACT.Copy, scale=-1.0).then_inc(uw_ready, 1)
                    nc.scalar.activation(by_head(uadj[:, t, :]), uw[:, :, 0:DK], ACT.Copy).then_inc(uw_ready, 1)
                    if t % 2:
                        for s in (t - 1, t):
                            act.wait_ge(wT_ps, b * 4 + s + 1)
                            nc.scalar.activation(nwT[s][:].rearrange("p a c -> p (a c)"), bank(4 + s % 2, 0, D), ACT.Copy).then_inc(wT_ready, 1)
                for t in range(NT):
                    act.wait_ge(o_ps, b * 4 + t + 1)
                    nc.scalar.activation(dT[:, :, t * P:(t + 1) * P], bank(5, 0, D).rearrange("p (a c) -> p a c", a=DB), ACT.Copy).then_inc(o_ready, 1)
                    if route is not None and t >= 2:
                        c = t - 2
                        act.wait_ge(rT_ps, route * 2 + c + 1)
                        nc.scalar.activation(rT[c], bank(7), ACT.Copy).then_inc(rT_ready, 1)
                for j in range(2):
                    act.wait_ge(d_ps, b * 2 + j + 1)
                    for k in range(2):
                        nc.scalar.activation(dv[:, 2 * j + k, 0, :], bank(4 + j, k * D, (k + 1) * D), ACT.Copy).then_inc(o_ready, 1)
                for m in range(4):
                    act.wait_ge(hid_ps, b * 4 + m + 1)
                    nc.scalar.activation(hidT[:, m, :], bank(m), ACT.Gelu, bias=b_f1[:, m:m + 1]).then_inc(hid_ready, 1)

            def tap3(b, m):
                act.wait_ge(proj_ps, b * 6 + m + 1)
                nc.scalar.activation(qkv[:, m, :], bank(proj_bank[m]), ACT.Copy, scale=conv_w[:, m, 3:4]).then_inc(tap3_done, 1)
                if m in on_pool:
                    act.wait_ge(tap3_done, b * 6 + m + 1)
                    act.wait_ge(pool_conv, b * 6 + 3 * on_pool[m])
                    for k in range(1, 4):
                        nc.scalar.activation(tap[:, k - 1, 0:L - k], bank(proj_bank[m], 0, L - k), ACT.Copy,
                                             scale=conv_w[:, m, 3 - k:4 - k]).then_inc(tap_ready, 1)

            def silu(b, m):
                conv_wait(act, b, m)
                nc.scalar.activation(qkv[:, m, :], qkv[:, m, :], ACT.Silu).then_inc(silu_done, 1)

            def kq_squares(b, p):
                for t in (2 * p, 2 * p + 1):
                    act.wait_ge(kq_ps, b * 4 + t + 1)
                    act.wait_ge(ss_ready, b * 6 + (t - 1 if p else 0))
                    nc.scalar.activation(sq[t % 2][:], bank(t), ACT.Square).then_inc(sq_ready, 1)

            def out_squares(b, p):
                for t in (2 * p, 2 * p + 1):
                    act.wait_ge(mix_ready, b * 8 + 2 * t + 2)
                    nc.scalar.activation(osq[:, t, :], o[:, t, :], ACT.Square).then_inc(osq_ready, 1)

            def out_T(b, p):
                for t in (2 * p, 2 * p + 1):
                    act.wait_ge(oT_ps, b * 4 + t + 1)
                    nc.scalar.activation(oT[t % 2][:].rearrange("p a c -> p (a c)"), bank(6 + t % 2, 0, D), ACT.Copy).then_inc(oT_ready, 1)

            def join(tail, route, front):
                if front is not None:
                    for c in range(DB):
                        act.wait_ge(xT_ps, front * 2 + c + 1)
                        nc.scalar.activation(xT[:, c, :], bank(c), ACT.Copy).then_inc(xT_ready, 1)
                if route is not None:
                    act.wait_ge(sc_ready, route * 3 + 3)
                    nc.scalar.activation(g_ex[:], sc[:], ACT.Exp).then_inc(g_ex_ready, 1)
                if tail is not None:
                    act.wait_ge(ml_ready, tail * 11 + 4)
                    nc.scalar.activation(ex[:, :, 0:3], lg[:, :, 0:3], ACT.Exp).then_inc(ex_ready, 1)
                    nc.scalar.activation(ex[:, :, 3], lg[:, :, 3], ACT.Exp, scale=-1.0).then_inc(ex_ready, 1)
                if front is not None:
                    act.wait_ge(z_ps, front + 1)
                    nc.scalar.activation(ez[:].rearrange("p (t h) -> p t h", t=NT), bank(3).rearrange("p (t h) -> p t h", t=NT)[:, :, 0:H],
                                         ACT.Exp, scale=-1.0).then_inc(ez_ready, 1)
                    tap3(front, 0)
                    tap3(front, 1)
                    silu(front, 0)
                    tap3(front, 2)
                    silu(front, 1)
                    tap3(front, 3)
                    tap3(front, 4)
                    tap3(front, 5)
                    silu(front, 2)
                    silu(front, 3)
                if tail is not None:
                    out_squares(tail, 0)
                if front is not None:
                    kq_squares(front, 0)
                    silu(front, 4)
                    silu(front, 5)
                    if tail is not None:
                        act.wait_ge(mixb_ready, tail * 8 + 8)
                    for j in range(2):
                        act.wait_ge(v_ps, front * 2 + j + 1)
                        nc.scalar.activation(dv[:, 2 * j:2 * j + 2, 1, :], bank(4 + j).rearrange("p (t c) -> p t c", t=2), ACT.Copy).then_inc(v_ready, 1)
                if tail is not None:
                    out_squares(tail, 1)
                if front is not None:
                    kq_squares(front, 1)
                if tail is not None:
                    out_T(tail, 0)
                if tail is not None:
                    out_T(tail, 1)
                if front is not None:
                    for t in range(NT + 1):
                        if t < NT:
                            for hb in range(DB):
                                act.wait_ge(kT_ps, front * 8 + 2 * t + hb + 1)
                                nc.scalar.activation(kT[t][hb][:].rearrange("p a c -> p (a c)"), bank(6 + hb), ACT.Copy).then_inc(kT_ready, 1)
                        if t:
                            act.wait_ge(al_ps, front * 4 + t)
                            for k in range(2):
                                ins = nc.scalar.activation(AT[t - 1][:, 2 * k:2 * k + 2, :],
                                                           bank(2 * ((t - 1) % 2) + k).rearrange("p (a c) -> p a c", a=2)[:, :, 0:P], ACT.Copy)
                            ins.then_inc(AT_ready, 1)

            def flush(r):
                for c in range(DB):
                    act.wait_ge(rT_ps, r * 2 + c + 1)
                    nc.scalar.activation(rT[c], bank(7), ACT.Copy).then_inc(rT_ready, 1)
                act.wait_ge(sc_ready, r * 3 + 3)
                nc.scalar.activation(g_ex[:], sc[:], ACT.Exp).then_inc(g_ex_ready, 1)

            join(None, None, 0)
            main(0, None, 1)
            join(0, None, 1)
            main(1, 0, 2)
            with act.Fori(0, B - 3) as i:
                join(i + 1, i, i + 2)
                main(i + 2, i + 1, i + 3)
            join(B - 2, B - 3, B - 1)
            main(B - 1, B - 2, None)
            join(B - 1, B - 2, None)
            flush(B - 1)

        @block.tensor
        def _(pe):
            mm = nc.tensor.matmul
            pe.wait_ge(loaded, 16 * NLOAD)
            for c in range(DB):
                ins = nc.tensor.transpose(bank(3, c * E, (c + 1) * E), w_rows[:, c * P:(c + 1) * P], const[0:E, C_EYE:C_EYE + E])
            ins.then_inc(route_ps, 1)
            pe.wait_ge(prepared, 4)

            def x_of(b, p2, lv, g):
                t = 2 * p2 + g
                if lv == 1:
                    pe.wait_ge(t1_ready, b * 4 + t + 1)
                else:
                    pe.wait_ge(t_ready, b * 20 + p2 * 10 + (lv - 2) * 2 + g + 1)
                for h in range(H):
                    ins = mm(bank(g, h * P, (h + 1) * P), AT[t][:, h, :], T[g][:, h, :], start=True, stop=True)
                ins.then_inc(x_ps, 1)

            def inverse(b, p2):
                for g in range(2):
                    t = 2 * p2 + g
                    pe.wait_ge(tt1_ready, b * 8 + 2 * t + 2)
                    if p2:
                        pe.wait_ge(tt_ready, b * 24 + 10 + g + 1)
                    for h in range(H):
                        ins = nc.tensor.transpose(bank(4 + g, h * P, (h + 1) * P), TT[t][:, h, :], eye)
                    ins.then_inc(t1_ps, 1)
                if p2 == 0:
                    pe.wait_ge(loc_ready, b * 4 + 4)
                for g in range(2):
                    x_of(b, p2, 1, g)
                for lv in range(1, LEVELS):
                    last = lv == LEVELS - 1
                    for g in range(2):
                        t = 2 * p2 + g
                        if lv == 1:
                            mm(bank(2 + g), eye, T[g][:].rearrange("p h c -> p (h c)"), start=True, stop=False, skip_group_check=True)
                        if lv > 1:
                            pe.wait_ge(tt_ready, b * 24 + p2 * 12 + (lv - 2) * 2 + g + 1)
                        if last:
                            mm(bank(4 + g), eye, TT[t][:].rearrange("p h c -> p (h c)"), start=True, stop=False, skip_group_check=True)
                        pe.wait_ge(x_ready, b * 24 + p2 * 12 + (lv - 1) * 2 + g + 1)
                        for h in range(H):
                            if last:
                                ins = mm(bank(4 + g, h * P, (h + 1) * P), X[g][:, h, :], TT[t][:, h, :],
                                         start=False, stop=h == H - 1, skip_group_check=True)
                            else:
                                ins = mm(bank(2 + g, h * P, (h + 1) * P), TT[t][:, h, :], X[g][:, h, :],
                                         start=False, stop=lv == LEVELS - 2 and h == H - 1, skip_group_check=True)
                        ins.then_inc(tt_ps if last else t_ps, 1)
                    if not last:
                        for g in range(2):
                            pe.wait_ge(t_ready, b * 20 + p2 * 10 + (lv - 1) * 2 + g + 1)
                            for h in range(H):
                                ins = nc.tensor.transpose(bank(4 + g, h * P, (h + 1) * P), T[g][:, h, :], eye)
                            ins.then_inc(tt_ps, 1)
                            x_of(b, p2, lv + 1, g)

            def u_w(b, t):
                pe.wait_ge(tt_ready, b * 24 + (t // 2) * 12 + 10 + t % 2 + 1)
                pe.wait_ge(uw_ready, b * 8 + (2 * (t - 1) if t >= 2 else 0))
                for h in range(H):
                    ins = mm(bank(6 + t % 2, h * P, (h + 1) * P), TT[t][:, h, :], vk[:, t, :, h * DK:(h + 1) * DK], start=True, stop=True)
                ins.then_inc(uw_ps, 1)

            def w_T(b, t):
                pe.wait_ge(uw_ready, b * 8 + 2 * t + 1)
                if t >= 2:
                    pe.wait_ge(wT_ready, b * 4 + t - 1)
                for hb in range(DB):
                    ins = nc.tensor.transpose(bank(4 + t % 2, hb * P, (hb + 1) * P), w_tok[t % 2][:, hb * P:(hb + 1) * P], eye)
                ins.then_inc(wT_ps, 1)

            gate_in = [xT[:, 0, :], xT[:, 1, :], firT[:, 0, 0, :], firT[:, 0, 1, :], firT[:, 1, 0, :], firT[:, 1, 1, :],
                       dT[:, 0, :], dT[:, 1, :]]

            def hidden(m, lo, hi):
                for c in range(lo, hi):
                    ins = mm(bank(m), w_f1[:, c, m * P:(m + 1) * P], gate_in[c], start=c == 0, stop=c == 7)
                return ins

            def route_T(r, c):
                pe.wait_ge(g_xn_ready, r * 4 + 4)
                if c:
                    pe.wait_ge(rT_ready, r * 2 + c)
                for t in range(NT):
                    ins = nc.tensor.transpose(bank(7, t * P, (t + 1) * P), xn[:, t, c * P:(c + 1) * P], eye)
                ins.then_inc(rT_ps, 1)

            def route_scores(r):
                pe.wait_ge(rT_ready, r * 2 + 2)
                for t in range(NT):
                    for c in range(DB):
                        ins = mm(bank(7, t * P, (t + 1) * P), rT[c][:, t * P:(t + 1) * P], w_route[:, c, :], start=c == 0, stop=c == DB - 1)
                ins.then_inc(sc_ps, 1)

            def scan_ws(b, t):
                pe.wait_ge(s_ready, b * 3 + t)
                pe.wait_ge(wT_ready, b * 4 + 4)
                if t >= 2:
                    pe.wait_ge(u_ready, b * 3 + t - 1)
                for hb in range(DB):
                    ins = mm(bank(4, hb * P, (hb + 1) * P), nwT[t][:, hb, :], S[:, hb, :], start=True, stop=True)
                ins.then_inc(ws_ps, 1)

            def scan_out(b, t):
                if t:
                    pe.wait_ge(o_ready, b * 8 + t)
                    pe.wait_ge(u_ready, b * 3 + t)
                else:
                    pe.wait_ge(wT_ready, b * 4 + 4)
                    pe.wait_ge(uw_ready, b * 8 + 8)
                for hb in range(DB):
                    if t:
                        mm(bank(5, hb * P, (hb + 1) * P), S[:, hb, :], kT[t][hb][:, 3, :], start=True, stop=False, skip_group_check=True)
                    for a in range(2):
                        h = 2 * hb + a
                        ins = mm(ps[64 * a:64 * a + 64, 5, hb * P:(hb + 1) * P], uadj[:, t, h * DK:(h + 1) * DK], loc[t][:, h, :],
                                 start=t == 0, stop=True, skip_group_check=True)
                ins.then_inc(o_ps, 1)
                if t < NT - 1:
                    for hb in range(DB):
                        for a in range(2):
                            ins = mm(bank(6, hb * P, (hb + 1) * P), kz[:, t, (2 * hb + a) * P:(2 * hb + a + 1) * P], uadj[:, t, hb * P:(hb + 1) * P],
                                     start=t == 0 and hb == 0 and a == 0, stop=t == NT - 2 and hb == DB - 1 and a == 1, skip_group_check=True)
                    ins.then_inc(s_ps, 1)

            def main(b, route, norm_next):
                inverse(b, 0)
                inverse(b, 1)
                u_w(b, 0)
                u_w(b, 1)
                pe.wait_ge(fir_step, b * NFIR + NFIR)
                hidden(0, 0, 6)
                w_T(b, 0)
                w_T(b, 1)
                u_w(b, 2)
                u_w(b, 3)
                hidden(1, 0, 6)
                w_T(b, 2)
                w_T(b, 3)
                pe.wait_ge(t_ready, b * 20 + 20)
                hidden(2, 0, 2)
                scan_out(b, 0)
                hidden(2, 2, 4)
                scan_ws(b, 1)
                hidden(2, 4, 6)
                scan_out(b, 1)
                hidden(3, 0, 2)
                scan_ws(b, 2)
                hidden(3, 2, 4)
                scan_out(b, 2)
                if route is not None:
                    route_T(route, 0)
                hidden(3, 4, 5)
                scan_ws(b, 3)
                hidden(3, 5, 6)
                if route is not None:
                    route_T(route, 1)
                scan_out(b, 3)
                pe.wait_ge(o_ready, b * 8 + 4)
                for m in range(4):
                    hidden(m, 6, 8).then_inc(hid_ps, 1)
                for j in range(2):
                    for k in range(2):
                        t = 2 * j + k
                        for hb in range(DB):
                            ins = nc.tensor.transpose(bank(4 + j, k * D + hb * P, k * D + (hb + 1) * P), dT[:, hb, t * P:(t + 1) * P], eye)
                    ins.then_inc(d_ps, 1)
                if route is not None:
                    route_scores(route)
                pe.wait_ge(s_ready, b * 3 + 3)
                for t in range(NT):
                    for c in range(4):
                        if t == 0:
                            pe.wait_ge(hid_ready, b * 4 + c + 1)
                        ins = mm(bank(6, t * P, (t + 1) * P), hidT[:, c, t * P:(t + 1) * P], w_f2[:, c, :], start=c == 0, stop=c == 3)
                ins.then_inc(lg_ps, 1)

            def f_of(b, t):
                if t < 2:
                    pe.wait_ge(o_ready, b * 8 + 8)
                else:
                    pe.wait_ge(mixa_ready, b * 4 + t - 1)
                for kind in range(2):
                    for c in range(DB):
                        ins = nc.tensor.transpose(bank(4 + t % 2, (2 * kind + c) * P, (2 * kind + c + 1) * P), firT[:, kind, c, t * P:(t + 1) * P], eye)
                ins.then_inc(f_ps, 1)

            def project(b, m):
                if m == 3:
                    conv_wait(pe, b, 0)
                elif m < 3:
                    pe.wait_ge(xT_ready, b * 2 + 2)
                for c in range(DB):
                    ins = mm(bank(proj_bank[m]), w_qkv[:, c, m * P:(m + 1) * P], xT[:, c, :], start=c == 0, stop=c == DB - 1)
                ins.then_inc(proj_ps, 1)

            def out_pair(b, p):
                for t in (2 * p, 2 * p + 1):
                    pe.wait_ge(on_ready, b * 4 + t + 1)
                    if p:
                        pe.wait_ge(resid_done, b * 4 + t - 1)
                    for c in range(DB):
                        ins = nc.tensor.transpose(bank(6 + t % 2, c * P, (c + 1) * P), o[:, t, c * P:(c + 1) * P], eye)
                    ins.then_inc(oT_ps, 1)
                for t in (2 * p, 2 * p + 1):
                    pe.wait_ge(oT_ready, b * 4 + t + 1)
                    for c in range(DB):
                        ins = mm(bank(6 + t % 2, D, 2 * D), oT[t % 2][:, c, :], w_o[:, c, :], start=c == 0, stop=c == 1)
                    ins.then_inc(y_ps, 1)

            def join(tail, route, front):
                if front is not None:
                    pe.wait_ge(xn_ready, front * 4 + 4)
                    for c in range(DB):
                        for t in range(NT):
                            ins = nc.tensor.transpose(bank(c, t * P, (t + 1) * P), xn[:, t, c * P:(c + 1) * P], eye)
                        ins.then_inc(xT_ps, 1)
                if tail is not None:
                    f_of(tail, 0)
                    f_of(tail, 1)
                if front is not None:
                    pe.wait_ge(xT_ready, front * 2 + 2)
                    for t in range(NT):
                        for c in range(DB):
                            ins = mm(bank(3, t * P, (t + 1) * P), xT[:, c, t * P:(t + 1) * P], w_beta[:, c, :], start=c == 0, stop=c == DB - 1)
                    ins.then_inc(z_ps, 1)
                    for m in range(4):
                        project(front, m)
                    if tail is not None:
                        pe.wait_ge(ml_ready, tail * 11 + 1)
                    if route is not None:
                        pe.wait_ge(sc_ready, route * 3 + 1)
                    for m in range(4, 6):
                        project(front, m)
                if tail is not None:
                    f_of(tail, 2)
                    f_of(tail, 3)
                if front is not None:
                    pe.wait_ge(silu_done, front * 6 + 4)
                    pe.wait_ge(ez_ready, front + 1)
                    conv_wait(pe, front, 3)
                    for t in range(NT):
                        for c in range(4):
                            ins = nc.tensor.transpose(bank(t, c * P, (c + 1) * P), qkv[:, (c + 2) % 4, t * P:(t + 1) * P], eye)
                        ins.then_inc(kq_ps, 1)
                    if tail is not None:
                        pe.wait_ge(mixa_ready, tail * 4 + 4)
                    pe.wait_ge(silu_done, front * 6 + 6)
                    for t in range(NT):
                        for c in range(2):
                            ins = nc.tensor.transpose(bank(4 + t // 2, (t % 2) * D + c * P, (t % 2) * D + (c + 1) * P),
                                                      qkv[:, 4 + c, t * P:(t + 1) * P], eye)
                        if t % 2:
                            ins.then_inc(v_ps, 1)
                    conv_wait(pe, front, 4)
                    conv_wait(pe, front, 5)
                if tail is not None:
                    out_pair(tail, 0)
                    out_pair(tail, 1)
                if front is not None:
                    if tail is not None:
                        pe.wait_ge(resid_done, tail * 4 + 4)
                    for t in range(NT + 1):
                        if t:
                            pe.wait_ge(kT_ready, front * 8 + 2 * t)
                        if t < NT:
                            pe.wait_ge(vk_ready, front * 8 + t + 1)
                            pe.wait_ge(kqn_ready, front * 8 + 8)
                            for hb in range(DB):
                                for n, src in enumerate((kz[:, t, hb * 2 * P:hb * 2 * P + P], kz[:, t, hb * 2 * P + P:(hb + 1) * 2 * P],
                                                         vk[:, t, 1, hb * P:(hb + 1) * P], qn[:, t, hb * P:(hb + 1) * P])):
                                    ins = nc.tensor.transpose(bank(6 + hb, n * P, (n + 1) * P), src, eye)
                                ins.then_inc(kT_ps, 1)
                        if t:
                            s = t - 1
                            if s >= 2:
                                pe.wait_ge(loc_ready, front * 4 + s - 1)
                            for h in range(H):
                                k4 = kT[s][h // 2]
                                ins = mm(bank(2 * (s % 2) + h // 2, (h % 2) * 2 * P, (h % 2 + 1) * 2 * P),
                                         k4[:, h % 2, :], k4[:, 2:4, :], start=True, stop=True)
                            ins.then_inc(al_ps, 1)

            def flush(r):
                route_T(r, 0)
                route_T(r, 1)
                route_scores(r)

            join(None, None, 0)
            pe.wait_ge(gate_w_in, 16)
            main(0, None, 1)
            join(0, None, 1)
            main(1, 0, 2)
            with pe.Fori(0, B - 3) as i:
                join(i + 1, i, i + 2)
                main(i + 2, i + 1, i + 3)
            join(B - 2, B - 3, B - 1)
            main(B - 1, B - 2, None)
            join(B - 1, B - 2, None)
            flush(B - 1)


def choose_tokens(nc, A, const, ps, weights, first, prob, idxT, gT, idx_dram):
    R = B * E
    with ExitStack() as ctx:
        mk = Maker(nc, ctx, "ch_")
        sb, sem = mk.sb, mk.sem
        work = sb("work", [R, L])
        vals = sb("vals", [R, CAP])
        idx = sb("idx", [R, CAP], U32)
        idxf = sb("idxf", [R, CAP])
        rows_ps, found, moved, back_ps = (sem(n) for n in ("rows_ps", "found", "moved", "back_ps"))
        HB = F1 // P
        wqkv, qnw, knw, wout, bout, wg, wu, wd = weights
        raw = [sb(f"raw{n}", [P, HB * D], I32) for n in range(3)]
        rawf = [sb(f"rawf{n}", [P, HB * D]) for n in range(3)]
        loaded, raw_in, raw_ready, raw_ps, raw_done = (sem(n) for n in ("loaded", "raw_in", "raw_ready", "raw_ps", "raw_done"))
        ints = [("L1_ffn_w_gate", HB), ("L1_ffn_w_up", HB), ("L1_ffn_w_down", DB)]
        block = ctx.enter_context(nc.Block())

        @block.scalar
        def _(act):
            act.wait_ge(raw_in, 48)
            for n in range(3):
                nc.scalar.activation(rawf[n][:], raw[n][:], ACT.Copy, scale=1.0 / 127.0).then_inc(raw_ready, 1)
            for n in range(3):
                for q in range(4):
                    act.wait_ge(raw_ps, 4 * n + q + 1)
                    if n < 2:
                        dst = (wg, wu)[n][:, q // 2, (q % 2) * 384:(q % 2) * 384 + 384]
                    else:
                        dst = wd[:, 3 * (q // 2):3 * (q // 2) + 3, (q % 2) * P:(q % 2 + 1) * P]
                    src = ps[:, 4 + q, 0:384]
                    nc.scalar.activation(dst, src if n < 2 else src.rearrange("p (a c) -> p a c", a=3), ACT.Copy).then_inc(raw_done, 1)

        @block.vector
        def _(dve):
            n = [0]

            def chain(ins):
                n[0] += 1
                ins.then_inc(found, 1)
                dve.wait_ge(found, n[0])

            dve.wait_ge(rows_ps, 1)
            chain(nc.vector.tensor_copy(work[:], ps[0:R, 0, :]))
            for r in range(CAP // 8):
                v = vals[:, 8 * r:8 * r + 8]
                chain(nc.vector.max(v, work[:]))
                chain(nc.vector.max_index(idx[:, 8 * r:8 * r + 8], v, work[:]))
                chain(nc.vector.match_replace(work[:], v, work[:], -1.0))
            nc.vector.tensor_copy(idxf[:], idx[:]).then_inc(moved, 1)
            dve.wait_ge(back_ps, 1)
            nc.vector.tensor_copy(idxT[:], ps[:, 1, 0:R]).then_inc(moved, 1)
            nc.vector.tensor_copy(gT[:], ps[:, 1, P:P + R]).then_inc(moved, 1)

        @block.sync
        def _(sp):
            for n, (name, rb) in enumerate(ints):
                sp.dma_start(raw[n][:].rearrange("p (r c) -> p r c", r=rb), A[name].rearrange("(r p) c -> p r c", p=P)).then_inc(raw_in, 16)
            with nc.allow_non_contiguous_dma(reason="small parameters"):
                sp.dma_start(wqkv[:], A["L1_attn_W_qkv"].rearrange("(c p) n -> p c n", p=P)).then_inc(loaded, 16)
                sp.dma_start(qnw[:], A["L1_attn_qn_w"].rearrange("(c p) -> p c", p=P)).then_inc(loaded, 16)
                sp.dma_start(knw[:], A["L1_attn_kn_w"].unsqueeze(0).broadcast_to([P, D])).then_inc(loaded, 16)
                sp.dma_start(wout[:], A["L1_attn_W_out"].rearrange("(c p) n -> p c n", p=P)).then_inc(loaded, 16)
                sp.dma_start(bout[:], A["L1_attn_b_out"].unsqueeze(0).broadcast_to([P, D])).then_inc(loaded, 16)
            sp.dma_start(first[0][:], A["L0_ffn_w1"][0].rearrange("(c p) f -> p c f", p=P)).then_inc(loaded, 16)
            sp.dma_start(first[1][:], A["L0_ffn_w2"][0].rearrange("(c p) d -> p c d", p=P)).then_inc(loaded, 16)
            sp.wait_ge(moved, 1)
            sp.dma_start(idx_dram, idxf[:]).then_inc(loaded, 16)
            sp.wait_ge(loaded, 16 * 8)

        @block.tensor
        def _(pe):
            for t in range(NT):
                ins = nc.tensor.transpose(ps[0:R, 0, t * P:(t + 1) * P], prob[:, t, :], const[:, C_EYE:C_EYE + P])
            ins.then_inc(rows_ps, 1)
            for n in range(3):
                pe.wait_ge(raw_ready, n + 1)
                for q in range(4):
                    if n:
                        pe.wait_ge(raw_done, 4 * (n - 1) + q + 1)
                    for r in range(3):
                        if n < 2:
                            at = (3 * (q % 2) + r) * D + (q // 2) * P
                        else:
                            at = (q % 2) * F1 + (3 * (q // 2) + r) * P
                        ins = nc.tensor.transpose(ps[:, 4 + q, r * P:(r + 1) * P], rawf[n][:, at:at + P], const[:, C_EYE:C_EYE + P])
                    ins.then_inc(raw_ps, 1)
            pe.wait_ge(moved, 1)
            nc.tensor.transpose(ps[:, 1, 0:R], idxf[:], const[0:R, C_EYE:C_EYE + R])
            nc.tensor.transpose(ps[:, 1, P:P + R], vals[:], const[0:R, C_EYE:C_EYE + R]).then_inc(back_ps, 1)


def gather_tokens(nc, const, resid, ps, mean_all, rstd_all, idx_dram, slots):
    with ExitStack() as ctx:
        mk = Maker(nc, ctx, "ga_")
        sb, sem = mk.sb, mk.sem
        idxb = [sb(f"idxb{j}", [P, E * CAP]) for j in range(2)]
        xn = [[sb(f"xn{j}{t}", [P, D]) for t in range(NT)] for j in range(2)]
        pick = [sb(f"pick{j}", [P, NT, E * CAP]) for j in range(2)]
        st = [[sb(f"m{j}", [P, NT]), sb(f"r{j}", [P, NT])] for j in range(2)]
        idx_in, in_ready, out_ps, out_ready = ([sem(f"{n}{j}") for j in range(2)] for n in ("idx_in", "in_ready", "out_ps", "out_ready"))
        IN = 2 + 2 * NT
        rows = idx_dram.rearrange("(n e) s -> n (e s)", e=E)
        block = ctx.enter_context(nc.Block())

        @block.sync
        def _(sp):
            with sp.Fori(0, B // 2) as i:
                for j in range(2):
                    sp.wait_ge(in_ready[j], i * IN)
                    sp.dma_start(idxb[j][:], rows[bass.ds(2 * i + j, 1), :].broadcast_to([P, E * CAP])).then_inc(idx_in[j], 16)

        @block.vector
        def _(dve):
            with dve.Fori(0, B // 2) as i:
                for j in range(2):
                    nc.vector.tensor_copy(st[j][0][:], mean_all[:, bass.ds((2 * i + j) * NT, NT)]).then_inc(in_ready[j], 1)
                    nc.vector.tensor_copy(st[j][1][:], rstd_all[:, bass.ds((2 * i + j) * NT, NT)]).then_inc(in_ready[j], 1)
                    dve.wait_ge(in_ready[j], i * IN + 2)
                    dve.wait_ge(out_ps[j], i * 4)
                    dve.wait_ge(idx_in[j], i * 16 + 16)
                    for t in range(NT):
                        nc.vector.tensor_scalar(xn[j][t][:], resid[:, bass.ds((2 * i + j) * NT + t, 1), :].rearrange("p a d -> p (a d)"),
                                                st[j][0][:, t:t + 1], st[j][1][:, t:t + 1], ALU.subtract, ALU.mult).then_inc(in_ready[j], 1)
                        nc.vector.tensor_scalar(pick[j][:, t, :], idxb[j][:], const[:, C_TOKID + t:C_TOKID + t + 1], None,
                                                ALU.is_equal).then_inc(in_ready[j], 1)

        @block.scalar
        def _(act):
            with act.Fori(0, B // 2) as i:
                for j in range(2):
                    for half in range(2):
                        for c in range(DB):
                            act.wait_ge(out_ps[j], i * 4 + 2 * half + c + 1)
                            dst = slots[:, 4 * half:4 * half + 4, bass.ds(c * B * CAP + (2 * i + j) * CAP, CAP)]
                            nc.scalar.activation(dst, ps[:, 4 * j + 2 * half + c, :].rearrange("p (e s) -> p e s", e=4),
                                                 ACT.Copy).then_inc(out_ready[j], 1)

        @block.tensor
        def _(pe):
            with pe.Fori(0, B // 2) as i:
                for j in range(2):
                    pe.wait_ge(out_ready[j], i * 4)
                    pe.wait_ge(in_ready[j], i * IN + IN)
                    for half in range(2):
                        for c in range(DB):
                            for t in range(NT):
                                ins = nc.tensor.matmul(ps[:, 4 * j + 2 * half + c, :], xn[j][t][:, c * P:(c + 1) * P],
                                                       pick[j][:, t, half * 512:(half + 1) * 512], start=t == 0, stop=t == NT - 1)
                            ins.then_inc(out_ps[j], 1)


def experts(nc, A, ps, first, slots):
    FB = F0 // P
    with ExitStack() as ctx:
        mk = Maker(nc, ctx, "ex_")
        sb, sem = mk.sb, mk.sem
        w1 = [first[0], sb("w1_1", [P, DB, F0])]
        w2 = [first[1], sb("w2_1", [P, FB, D])]
        hT = [sb(f"hT{half}", [P, FB, 512]) for half in range(2)]
        w_in, dn_ps = ([sem(f"{n}{j}") for j in range(2)] for n in ("w_in", "dn_ps"))
        up_ps, up_ready, dn_ready = sem("up_ps"), sem("up_ready"), sem("dn_ready")
        w1_dram = A["L0_ffn_w1"].rearrange("e (c p) f -> p e c f", p=P)
        w2_dram = A["L0_ffn_w2"].rearrange("e (c p) d -> p e c d", p=P)
        block = ctx.enter_context(nc.Block())

        @block.sync
        def _(sp):
            def load(e, j):
                sp.dma_start(w1[j][:], w1_dram[:, bass.ds(e, 1), :, :].rearrange("p a c f -> p (a c) f")).then_inc(w_in[j], 16)
                sp.dma_start(w2[j][:], w2_dram[:, bass.ds(e, 1), :, :].rearrange("p a c f -> p (a c) f")).then_inc(w_in[j], 16)

            load(1, 1)
            with sp.Fori(1, E // 2) as i:
                for j in range(2):
                    sp.wait_ge(dn_ps[j], i * B)
                    load(2 * i + j, j)

        @block.tensor
        def _(pe):
            with pe.Fori(0, E // 2) as i:
                for j in range(2):
                    up, dn = i * 4 * FB + j * 2 * FB, i * 2 * B + j * B
                    pe.wait_ge(w_in[j], i * 32 + 32 * j)
                    for half in range(2):
                        for f in range(FB):
                            n = half * FB + f
                            if n >= 4:
                                pe.wait_ge(up_ready, up + n - 3)
                            for c in range(DB):
                                ins = nc.tensor.matmul(ps[:, n % 4, :], w1[j][:, c, f * P:(f + 1) * P],
                                                       slots[:, bass.ds(2 * i + j, 1), c * B * CAP + half * 512:c * B * CAP + half * 512 + 512].rearrange("p a s -> p (a s)"),
                                                       start=c == 0, stop=c == DB - 1)
                            ins.then_inc(up_ps, 1)
                    for n in range(B):
                        half = n // 4
                        if n % 4 == 0:
                            pe.wait_ge(up_ready, up + (half + 1) * FB)
                        if n >= 4:
                            pe.wait_ge(dn_ready, dn + n - 3)
                        else:
                            pe.wait_ge(dn_ready, dn)
                        for f in range(FB):
                            ins = nc.tensor.matmul(ps[:, 4 + n % 4, 0:D], hT[half][:, f, (n % 4) * CAP:(n % 4 + 1) * CAP], w2[j][:, f, :],
                                                   start=f == 0, stop=f == FB - 1)
                        ins.then_inc(dn_ps[j], 1)

        @block.scalar
        def _(act):
            with act.Fori(0, E // 2) as i:
                for j in range(2):
                    up, dn = i * 4 * FB + j * 2 * FB, i * 2 * B + j * B
                    for half in range(2):
                        act.wait_ge(dn_ps[1 - j], (i + j) * B)
                        for f in range(FB):
                            n = half * FB + f
                            act.wait_ge(up_ps, up + n + 1)
                            nc.scalar.activation(hT[half][:, f, :], ps[:, n % 4, :], ACT.Gelu).then_inc(up_ready, 1)

        @block.vector
        def _(dve):
            with dve.Fori(0, E // 2) as i:
                for j in range(2):
                    up, dn = i * 4 * FB + j * 2 * FB, i * 2 * B + j * B
                    for n in range(B):
                        dve.wait_ge(dn_ps[j], i * B + n + 1)
                        nc.vector.tensor_copy(slots[:, bass.ds(2 * i + j, 1), n * D:(n + 1) * D].rearrange("p a d -> p (a d)"),
                                              ps[:, 4 + n % 4, 0:D]).then_inc(dn_ready, 1)


def layer1(nc, const, resid, ps, weights, slots, idxT, gT, out):
    HB = F1 // P
    NB = P + 8
    with ExitStack() as ctx:
        mk = Maker(nc, ctx, "l1_")
        sb, sem = mk.sb, mk.sem
        eye = const[:, C_EYE:C_EYE + P]
        mhalf = const[:, C_MHALF:C_MHALF + NT]
        ones = const[:, C_ONE:C_ONE + P]
        heads = const[:, C_HEADS:C_HEADS + NB]
        wqkv, qnw, knw, wout, bout, wg, wu, wd = weights
        idxn, gn = sb("idxn", [P, E]), sb("gn", [P, E])
        put = sb("put", [P, E, L])
        xw = [sb(f"xw{j}", [P, NT, D]) for j in range(2)]
        stats = sb("stats", [P, NT, 6])
        mean, var, rstd = sb("mean", [P, NT]), sb("var", [P, 3, NT]), sb("rstd", [P, NT])
        xn = sb("xn", [P, NT, D])
        xT = sb("xT", [P, DB, L])
        fT = sb("fT", [P, DB, L])
        qT = sb("qT", [P, DB, L])
        sqq = xn[:].rearrange("p t d -> p (t d)").rearrange("p (c l) -> p c l", c=DB)
        sqk = sb("sqk", [P, D])
        ssk, ssq = sb("ssk", [P, NT]), sb("ssq", [P, NT])
        rk, rq = sb("rk", [P, NT]), sb("rq", [P, NT])
        k2 = sb("k2", [P, NT, D])
        vx = sb("vx", [P, NT, DB, NB])
        kvm = sb("kvm", [P, DB, NB])
        nrm = sb("nrm", [P, 2, DB, 8])
        o = sb("o", [P, 2, D])
        oT = [sb(f"oT{t}", [P, DB, P]) for t in range(2)]
        gs = sb("gs", [P, 2, 512])
        hT = sb("hT", [P, HB, L])

        ones_set = sem("ones_set")
        small, put_ready, add_ps, xw_ready, bias_ready = (sem(n) for n in ("small", "put_ready", "add_ps", "xw_ready", "bias_ready"))
        stat_done, mean_ready, rstd_ready, xn_ready, xT_ps, xT_ready = (
            sem(n) for n in ("stat_done", "mean_ready", "rstd_ready", "xn_ready", "xT_ps", "xT_ready"))
        f_stat, f_mean, f_rstd, f_xn, fT_ps, fT_ready = (sem(n) for n in ("f_stat", "f_mean", "f_rstd", "f_xn", "fT_ps", "fT_ready"))
        kv_ps, v_ready, ssk_ready, rk_ready, kk_ready, k2_ready = (
            sem(n) for n in ("kv_ps", "v_ready", "ssk_ready", "rk_ready", "kk_ready", "k2_ready"))
        q_ps, q_ready, ssq_ps, ssq_ready, rq_ready, kvm_ps, kvm_ready = (
            sem(n) for n in ("q_ps", "q_ready", "ssq_ps", "ssq_ready", "rq_ready", "kvm_ps", "kvm_ready"))
        att_ps, nrm_step, o_ready, oT_ps, oT_ready, wo_ps, att_out = (
            sem(n) for n in ("att_ps", "nrm_step", "o_ready", "oT_ps", "oT_ready", "wo_ps", "att_out"))
        g_ps, g_ready, u_ps, h_ready, y_ps, y_ready = (
            sem(n) for n in ("g_ps", "g_ready", "u_ps", "h_ready", "y_ps", "y_ready"))
        stored = [sem(f"stored{j}") for j in range(2)]
        mm = nc.tensor.matmul
        block = ctx.enter_context(nc.Block())

        def bank(n, lo=0, hi=512):
            return ps[:, n, lo:hi]

        out_v = out.rearrange("b (t p) d -> p b t d", p=P)

        @block.sync
        def _(sp):
            with sp.Fori(0, B // 2) as i:
                for j in range(2):
                    sp.wait_ge(y_ready, i * 2 * NT + (j + 1) * NT)
                    sp.dma_start(out_v[:, bass.ds(2 * i + j, 1), :, :].rearrange("p a t d -> p (a t) d"), xw[j][:]).then_inc(stored[j], 16)
            for j in range(2):
                sp.wait_ge(stored[j], 16 * (B // 2))

        def steps(eng, step):
            step(0, 0, None)
            with eng.Fori(0, B // 2 - 1) as i:
                step(2 * i + 1, 1, 2 * i)
                step(2 * i + 2, 0, 2 * i + 1)
            step(B - 1, 1, B - 2)
            step(None, 0, B - 1)

        @block.vector
        def _(dve):
            nc.vector.memset(vx[:, :, :, P:NB].rearrange("p a b c -> p (a b) c"), 1.0).then_inc(ones_set, 1)

            def one_hot(n, lo, hi):
                if lo == 0:
                    nc.vector.tensor_copy(idxn[:], idxT[:, bass.ds(n * E, E)]).then_inc(small, 1)
                    nc.vector.tensor_copy(gn[:], gT[:, bass.ds(n * E, E)]).then_inc(small, 1)
                    dve.wait_ge(small, n * 2 + 2)
                    dve.wait_ge(add_ps, n * NT)
                for e in range(lo, hi):
                    nc.vector.tensor_scalar(put[:, e, :], const[:, C_TOK:C_TOK + L], idxn[:, e:e + 1], gn[:, e:e + 1],
                                            ALU.is_equal, ALU.mult).then_inc(put_ready, 1)

            def hidden(f, m):
                dve.wait_ge(u_ps, f * HB + m + 1)
                dve.wait_ge(g_ready, f * HB + m + 1)
                if m == 0:
                    dve.wait_ge(y_ps, f * NT)
                nc.vector.tensor_tensor(hT[:, m, :], bank(6 + m % 2), gs[:, m % 2, :], ALU.mult).then_inc(h_ready, 1)

            def add_y(f, par, lo, hi):
                for t in range(lo, hi):
                    dve.wait_ge(y_ps, f * NT + t + 1)
                    nc.vector.tensor_tensor(xw[par][:, t, :], bank(4 + t, 0, D), xw[par][:, t, :], ALU.add).then_inc(y_ready, 1)

            def keys(n, lo, hi):
                for t in range(lo, hi):
                    dve.wait_ge(v_ready, n * NT + t + 1)
                    nc.vector.tensor_tensor(k2[:, t, :], bank(2 + t % 2, 0, D), knw[:], ALU.mult).then_inc(kk_ready, 1)

            def divide(n, t):
                r = nrm[:, t % 2, :, :]
                dve.wait_ge(att_ps, n * NT + t + 1)
                att = bank(2 + t % 2, 0, DB * NB).rearrange("p (k c) -> p k c", k=DB)
                nc.vector.tensor_scalar(r, att[:, :, P:NB], rq[:, t:t + 1], 1e-6, ALU.mult, ALU.add).then_inc(nrm_step, 1)
                dve.wait_ge(nrm_step, n * 3 * NT + 3 * t + 1)
                nc.vector.reciprocal(r, r).then_inc(nrm_step, 1)
                dve.wait_ge(nrm_step, n * 3 * NT + 3 * t + 2)
                nc.vector.tensor_scalar(r, r, rq[:, t:t + 1], None, ALU.mult).then_inc(nrm_step, 1)
                dve.wait_ge(nrm_step, n * 3 * NT + 3 * t + 3)
                if t >= 2:
                    dve.wait_ge(oT_ps, n * NT + t - 1)
                for hb in range(DB):
                    ins = nc.vector.tensor_tensor(o[:, t % 2, hb * P:(hb + 1) * P].rearrange("p (h c) -> p h c", h=8),
                                                  att[:, hb, 0:P].rearrange("p (h c) -> p h c", h=8),
                                                  spread(r[:, hb, :], 2, DH1), ALU.mult)
                ins.then_inc(o_ready, 1)

            def add_wo(n, par, t):
                dve.wait_ge(wo_ps, n * NT + t + 1)
                if t == 0:
                    dve.wait_ge(bias_ready, n + 1)
                nc.vector.tensor_tensor(xw[par][:, t, :], bank(t % 2, D, 2 * D), xw[par][:, t, :], ALU.add).then_inc(att_out, 1)

            def step(n, par, f):
                if f is not None:
                    for t in range(NT):
                        dve.wait_ge(att_out, f * NT + t + 1)
                        nc.vector.bn_stats(stats[:, t, :], xw[1 - par][:, t, :]).then_inc(f_stat, 1)
                    dve.wait_ge(f_stat, f * NT + NT)
                    merge_stats(nc, dve, stats, mean, var, f_mean, f)
                    dve.wait_ge(f_rstd, f + 1)
                    for t in range(NT):
                        nc.vector.tensor_scalar(xn[:, t, :], xw[1 - par][:, t, :], mean[:, t:t + 1], rstd[:, t:t + 1],
                                                ALU.subtract, ALU.mult).then_inc(f_xn, 1)
                if n is not None:
                    if f is not None:
                        dve.wait_ge(stored[par], (n - par) * 8)
                    for t in range(NT):
                        dve.wait_ge(add_ps, n * NT + t + 1)
                        nc.vector.tensor_tensor(xw[par][:, t, :], bank(t % 2, 0, D),
                                                resid[:, bass.ds(n * NT + t, 1), :].rearrange("p a d -> p (a d)"), ALU.add).then_inc(xw_ready, 1)
                        dve.wait_ge(xw_ready, n * NT + t + 1)
                        if t == 0 and f is not None:
                            dve.wait_ge(f_xn, f * NT + NT)
                        nc.vector.bn_stats(stats[:, t, :], xw[par][:, t, :]).then_inc(stat_done, 1)
                    dve.wait_ge(stat_done, n * NT + NT)
                    merge_stats(nc, dve, stats, mean, var, mean_ready, n)
                    dve.wait_ge(rstd_ready, n + 1)
                    if f is not None:
                        dve.wait_ge(fT_ps, f * 2 + 2)
                    for t in range(NT):
                        nc.vector.tensor_scalar(xn[:, t, :], xw[par][:, t, :], mean[:, t:t + 1], rstd[:, t:t + 1],
                                                ALU.subtract, ALU.mult).then_inc(xn_ready, 1)
                if f is not None:
                    for m in range(3):
                        hidden(f, m)
                if n is not None:
                    keys(n, 0, 2)
                if f is not None:
                    hidden(f, 3)
                if n is not None:
                    keys(n, 2, 4)
                    dve.wait_ge(ssk_ready, n * (NT + 1) + NT)
                    nc.vector.tensor_scalar(ssk[:], ssk[:], 1.0 / D, 1e-6, ALU.mult, ALU.add).then_inc(ssk_ready, 1)
                    if n is not last:
                        one_hot(n + 1, 0, 4)
                if f is not None:
                    hidden(f, 4)
                if n is not None:
                    dve.wait_ge(ssq_ps, n + 1)
                    nc.vector.tensor_scalar(ssq[:], bank(0).rearrange("p (t c) -> p t c", t=NT)[:, :, 0], 1.0 / D, 1e-6,
                                            ALU.mult, ALU.add).then_inc(ssq_ready, 1)
                if f is not None:
                    hidden(f, 5)
                if n is not None:
                    dve.wait_ge(kvm_ps, n + 1)
                    for hb in range(DB):
                        nc.vector.tensor_tensor(kvm[:, hb, :], bank(1, hb * NB, (hb + 1) * NB), heads, ALU.mult).then_inc(kvm_ready, 1)
                    if n is not last:
                        one_hot(n + 1, 4, E)
                    dve.wait_ge(rq_ready, n + 1)
                    divide(n, 0)
                    divide(n, 1)
                    if f is not None:
                        add_y(f, 1 - par, 0, 1)
                    divide(n, 2)
                    add_wo(n, par, 0)
                    divide(n, 3)
                    add_wo(n, par, 1)
                    if f is not None:
                        add_y(f, 1 - par, 1, 4)
                    add_wo(n, par, 2)
                    add_wo(n, par, 3)
                else:
                    add_y(f, 1 - par, 0, 4)

            last = B - 1
            one_hot(0, 0, E)
            steps(dve, step)

        @block.gpsimd
        def _(pool):
            def step(n, par, f):
                if f is not None:
                    pool.wait_ge(f_mean, (f + 1) * MERGE)
                    pool.tensor_tensor(rstd[:], var[:, 0, :], mhalf, ALU.pow).then_inc(f_rstd, 1)
                if n is not None:
                    pool.wait_ge(mean_ready, (n + 1) * MERGE)
                    pool.tensor_tensor(rstd[:], var[:, 0, :], mhalf, ALU.pow).then_inc(rstd_ready, 1)
                    pool.wait_ge(xn_ready, n * NT + NT)
                    pool.tensor_tensor(xw[par][:], xw[par][:], spread(bout[:], 1, NT), ALU.add).then_inc(bias_ready, 1)
                    pool.wait_ge(ssk_ready, (n + 1) * (NT + 1))
                    pool.tensor_tensor(rk[:], ssk[:], mhalf, ALU.pow).then_inc(rk_ready, 1)
                    pool.wait_ge(ssq_ready, n + 1)
                    pool.tensor_tensor(rq[:], ssq[:], mhalf, ALU.pow).then_inc(rq_ready, 1)

            steps(pool, step)

        @block.scalar
        def _(act):
            def gate(f, m):
                act.wait_ge(g_ps, f * HB + m + 1)
                if m >= 2:
                    act.wait_ge(h_ready, f * HB + m - 1)
                nc.scalar.activation(gs[:, m % 2, :], bank(4 + m % 2), ACT.Silu).then_inc(g_ready, 1)

            def from_kv(n, t):
                act.wait_ge(kv_ps, n * NT + t + 1)
                act.wait_ge(ssk_ready, n * (NT + 1) + t)
                nc.scalar.activation(sqk[:], bank(2 + t % 2, 0, D), ACT.Square, accum_out=ssk[:, t:t + 1]).then_inc(ssk_ready, 1)
                nc.scalar.activation(vx[:, t, :, 0:P], bank(2 + t % 2, D, 2 * D).rearrange("p (k c) -> p k c", k=DB), ACT.Copy).then_inc(v_ready, 1)

            def step(n, par, f):
                if f is not None:
                    for c in range(DB):
                        act.wait_ge(fT_ps, f * 2 + c + 1)
                        nc.scalar.activation(fT[:, c, :], bank(2 + c), ACT.Copy).then_inc(fT_ready, 1)
                    gate(f, 0)
                    gate(f, 1)
                if n is not None:
                    for c in range(DB):
                        act.wait_ge(xT_ps, n * 2 + c + 1)
                        nc.scalar.activation(xT[:, c, :], bank(2 + c), ACT.Copy).then_inc(xT_ready, 1)
                if f is not None:
                    gate(f, 2)
                if n is not None:
                    for c in range(DB):
                        act.wait_ge(q_ps, n * 2 + c + 1)
                        nc.scalar.activation(sqq[:, c, :], bank(c), ACT.Square).then_inc(q_ready, 1)
                        nc.scalar.activation(qT[:, c, :], bank(c), ACT.Relu, scale=qnw[:, c:c + 1]).then_inc(q_ready, 1)
                    from_kv(n, 0)
                    from_kv(n, 1)
                if f is not None:
                    gate(f, 3)
                if n is not None:
                    from_kv(n, 2)
                    from_kv(n, 3)
                if f is not None:
                    gate(f, 4)
                if n is not None:
                    act.wait_ge(rk_ready, n + 1)
                    act.wait_ge(kk_ready, n * NT + NT)
                    for t in range(NT):
                        nc.scalar.activation(k2[:, t, :], k2[:, t, :], ACT.Relu, scale=rk[:, t:t + 1]).then_inc(k2_ready, 1)
                if f is not None:
                    gate(f, 5)
                if n is not None:
                    for t in range(NT):
                        act.wait_ge(oT_ps, n * NT + t + 1)
                        nc.scalar.activation(oT[t % 2][:].rearrange("p a c -> p (a c)"), bank(t % 2, 0, D), ACT.Copy).then_inc(oT_ready, 1)

            act.wait_ge(ones_set, 1)
            steps(act, step)

        @block.tensor
        def _(pe):
            def scatter(n, t):
                if t == 0:
                    pe.wait_ge(put_ready, n * E + E)
                if t >= 2:
                    pe.wait_ge(xw_ready, n * NT + t - 1)
                for e in range(E):
                    ins = mm(bank(t % 2, 0, D), put[:, e, t * P:(t + 1) * P], slots[:, e, bass.ds(n * D, D)], start=e == 0, stop=e == E - 1)
                ins.then_inc(add_ps, 1)

            def transposed(done):
                for c in range(DB):
                    for t in range(NT):
                        ins = nc.tensor.transpose(bank(2 + c, t * P, (t + 1) * P), xn[:, t, c * P:(c + 1) * P], eye)
                    ins.then_inc(done, 1)

            def gate_up(f, m):
                if m == 0:
                    pe.wait_ge(fT_ready, f * 2 + 2)
                    pe.wait_ge(y_ready, f * NT)
                if m >= 2:
                    pe.wait_ge(g_ready, f * HB + m - 1)
                for c in range(DB):
                    ins = mm(bank(4 + m % 2), wg[:, c, m * P:(m + 1) * P], fT[:, c, :], start=c == 0, stop=c == DB - 1)
                ins.then_inc(g_ps, 1)
                if m >= 2:
                    pe.wait_ge(h_ready, f * HB + m - 1)
                for c in range(DB):
                    ins = mm(bank(6 + m % 2), wu[:, c, m * P:(m + 1) * P], fT[:, c, :], start=c == 0, stop=c == DB - 1)
                ins.then_inc(u_ps, 1)

            def down(f, t):
                if t == 0:
                    pe.wait_ge(h_ready, f * HB + HB)
                for m in range(HB):
                    ins = mm(bank(4 + t, 0, D), hT[:, m, t * P:(t + 1) * P], wd[:, m, :], start=m == 0, stop=m == HB - 1)
                ins.then_inc(y_ps, 1)

            def keys_values(n, t):
                if t >= 2:
                    pe.wait_ge(kk_ready, n * NT + t - 1)
                for c in range(DB):
                    ins = mm(bank(2 + t % 2), xT[:, c, t * P:(t + 1) * P], wqkv[:, c, D:3 * D], start=c == 0, stop=c == DB - 1)
                ins.then_inc(kv_ps, 1)

            def attend(n, t):
                if t < 2:
                    pe.wait_ge(kk_ready, n * NT + 2 + t + 1)
                else:
                    pe.wait_ge(o_ready, n * NT + t - 1)
                for hb in range(DB):
                    ins = mm(bank(2 + t % 2, hb * NB, (hb + 1) * NB), qT[:, hb, t * P:(t + 1) * P], kvm[:, hb, :], start=True, stop=True)
                ins.then_inc(att_ps, 1)

            def out_T(n, t):
                pe.wait_ge(o_ready, n * NT + t + 1)
                if t >= 2:
                    pe.wait_ge(att_out, n * NT + t - 1)
                else:
                    pe.wait_ge(ssq_ready, n + 1)
                    pe.wait_ge(kvm_ready, n * 2 + 2)
                for c in range(DB):
                    ins = nc.tensor.transpose(bank(t % 2, c * P, (c + 1) * P), o[:, t % 2, c * P:(c + 1) * P], eye)
                ins.then_inc(oT_ps, 1)

            def out_mm(n, t):
                pe.wait_ge(oT_ready, n * NT + t + 1)
                for c in range(DB):
                    ins = mm(bank(t % 2, D, 2 * D), oT[t % 2][:, c, :], wout[:, c, :], start=c == 0, stop=c == DB - 1)
                ins.then_inc(wo_ps, 1)

            def step(n, par, f):
                if n is not None:
                    if f is not None:
                        pe.wait_ge(att_out, f * NT + NT)
                    for t in range(NT):
                        scatter(n, t)
                if f is not None:
                    pe.wait_ge(f_xn, f * NT + NT)
                    transposed(fT_ps)
                    gate_up(f, 0)
                    gate_up(f, 1)
                if n is not None:
                    pe.wait_ge(xn_ready, n * NT + NT)
                    transposed(xT_ps)
                if f is not None:
                    gate_up(f, 2)
                if n is not None:
                    pe.wait_ge(xw_ready, n * NT + NT)
                    pe.wait_ge(xT_ready, n * 2 + 2)
                    for m in range(DB):
                        for c in range(DB):
                            ins = mm(bank(m), wqkv[:, c, m * P:(m + 1) * P], xT[:, c, :], start=c == 0, stop=c == DB - 1)
                        ins.then_inc(q_ps, 1)
                    keys_values(n, 0)
                    keys_values(n, 1)
                if f is not None:
                    gate_up(f, 3)
                if n is not None:
                    keys_values(n, 2)
                    keys_values(n, 3)
                if f is not None:
                    gate_up(f, 4)
                if n is not None:
                    pe.wait_ge(q_ready, n * 4 + 4)
                    for t in range(NT):
                        for c in range(DB):
                            ins = mm(bank(0, t * P, (t + 1) * P), sqq[:, c, t * P:(t + 1) * P], ones, start=c == 0, stop=c == DB - 1)
                    ins.then_inc(ssq_ps, 1)
                if f is not None:
                    gate_up(f, 5)
                if n is not None:
                    for hb in range(DB):
                        for t in range(NT):
                            pe.wait_ge(k2_ready, n * NT + t + 1)
                            ins = mm(bank(1, hb * NB, (hb + 1) * NB), k2[:, t, hb * P:(hb + 1) * P], vx[:, t, hb, :], start=t == 0, stop=t == NT - 1)
                    ins.then_inc(kvm_ps, 1)
                if f is not None:
                    down(f, 0)
                if n is not None:
                    pe.wait_ge(kvm_ready, n * 2 + 2)
                    attend(n, 0)
                    attend(n, 1)
                if f is not None:
                    down(f, 1)
                if n is not None:
                    out_T(n, 0)
                    out_T(n, 1)
                    attend(n, 2)
                    attend(n, 3)
                if f is not None:
                    down(f, 2)
                if n is not None:
                    out_mm(n, 0)
                    out_mm(n, 1)
                if f is not None:
                    down(f, 3)
                if n is not None:
                    out_T(n, 2)
                    out_T(n, 3)
                    out_mm(n, 2)
                    out_mm(n, 3)

            steps(pe, step)


def program(nc, A, out):
    with ExitStack() as ctx:
        mk = Maker(nc, ctx)
        const = mk.sb("const", [P, C_END])
        resid = mk.sb("resid", [P, B * NT, D])
        ps = ctx.enter_context(nc.psum_tensor("ps", [P, 8, 512], F32))
        idx_dram = nc.dram_tensor("idx_dram", [B * E, CAP], F32).ap()
        x_in = A["L0_attn_hidden_states"].rearrange("b (t p) d -> p (b t) d", p=P)
        got = mk.sem("got")
        with nc.Block() as block:
            @block.sync
            def _(sp):
                sp.dma_start(resid[:, 0:NT, :], x_in[:, 0:NT, :]).then_inc(got, 16)
                sp.dma_start(const[:], A["const"]).then_inc(got, 16)
                sp.wait_ge(got, 32)
        prob = mk.sb("prob", [P, NT, B * E])
        mean_all, rstd_all = mk.sb("mean_all", [P, B * NT]), mk.sb("rstd_all", [P, B * NT])
        attention0(nc, A, const, resid, x_in, ps, prob, mean_all, rstd_all)
        weights = (mk.sb("wqkv", [P, DB, 3 * D]), mk.sb("qnw", [P, DB]), mk.sb("knw", [P, D]), mk.sb("wout", [P, DB, D]),
                   mk.sb("bout", [P, D]), mk.sb("wg", [P, DB, F1]), mk.sb("wu", [P, DB, F1]), mk.sb("wd", [P, F1 // P, D]))
        slots = mk.sb("slots", [P, E, DB * B * CAP])
        idxT, gT = mk.sb("idxT", [P, B * E]), mk.sb("gT", [P, B * E])
        with ExitStack() as until_layer1:
            early = Maker(nc, until_layer1, "ex_")
            first = (early.sb("w1_0", [P, DB, F0]), early.sb("w2_0", [P, F0 // P, D]))
            choose_tokens(nc, A, const, ps, weights, first, prob, idxT, gT, idx_dram)
            gather_tokens(nc, const, resid, ps, mean_all, rstd_all, idx_dram, slots)
            experts(nc, A, ps, first, slots)
        layer1(nc, const, resid, ps, weights, slots, idxT, gT, out)


def kernel(**inputs):
    import numpy as _np
    import concourse.bacc as _bacc
    from concourse import mybir as _mybir
    from concourse.bass_utils import run_bass_kernel_spmd as _run

    nc = _bacc.Bacc("TRN2", target_bir_lowering=False, num_devices=1)
    arrays, aps = {}, {}
    for name, a in {**inputs, "const": constant_table()}.items():
        a = _np.ascontiguousarray(a)
        arrays[f"in_{name}"] = a
        aps[name] = nc.dram_tensor(f"in_{name}", a.shape, _mybir.dt.from_np(a.dtype), kind="ExternalInput").ap()
    out = nc.dram_tensor("out_0", (B, L, D), F32, kind="ExternalOutput").ap()
    program(nc, aps, out)
    return _run(nc, [arrays], core_ids=[0]).results[0]["out_0"]
```
